# Optimizing a Trainium2 kernel written in Bass

```python
import numpy as np
import jax
import jax.numpy as jnp

def _softmax(x, axis=-1):
    return jax.nn.softmax(x, axis=axis)

def _gelu(x):
    return jax.nn.gelu(x, approximate=True)

def _silu(x):
    return jax.nn.silu(x)

def _sigmoid(x):
    return jax.nn.sigmoid(x)

def _layernorm(x, axis=-1, eps=1e-05):
    m = jnp.mean(x, axis=axis, keepdims=True)
    v = jnp.var(x, axis=axis, keepdims=True)
    return (x - m) / jnp.sqrt(v + eps)

def _scatter_add(tgt, idx, src, axis=0):
    return tgt.at[idx].add(src)

def _segment_sum(src, seg, n):
    return jax.ops.segment_sum(src, seg, n)
kernel_name = 'mk_cond_seq_d4_seqx_r4_95d1a3'

def setup_inputs(seed: int=0):
    np.random.seed(seed)
    _w = jnp.asarray

    def _rec_inputs():
        import jax
        import jax.numpy as jnp
        _rk = jax.random.key(seed)
        x = -0.0003929 + 0.9999 * jax.random.normal(jax.random.fold_in(_rk, 1), (16, 256, 256), jnp.float32)
        _lenS = 256 - jax.random.randint(jax.random.fold_in(_rk, 7), (16,), 0, max(1, 256 // 4) + 1, jnp.int32)
        _lenS2 = 256 - jax.random.randint(jax.random.fold_in(_rk, 8), (16,), 0, max(1, 256 // 4) + 1, jnp.int32)
        cond_1024 = 0.00386106 + 1.00199 * jax.random.normal(jax.random.fold_in(_rk, 11), (16, 256), jnp.float32)
        _validS = jnp.arange(256)[None, :] < _lenS[:, None]
        _validS2 = jnp.arange(256)[None, :] < _lenS2[:, None]
        _causal = jnp.tril(jnp.ones((256, 256), dtype=bool))
        mask_BxSxSx11_ik0 = jnp.where(jnp.ones((16, 256, 256, 11), dtype=bool), 0, 1).astype(jnp.int32)
        return (x, cond_1024, mask_BxSxSx11_ik0)
    x, cond_1024, mask_BxSxSx11_ik0 = _rec_inputs()

    def _L0_cond_setup():
        import jax, jax.numpy as jnp
        import numpy as np
        FEAT = 256
        ADA = 256
        INTER = 256
        RANK = 8
        EPS = 1e-05

        def _layernorm(a, g, b):
            mu = jnp.mean(a, axis=-1, keepdims=True)
            var = jnp.mean(jnp.square(a - mu), axis=-1, keepdims=True)
            return (a - mu) * jax.lax.rsqrt(var + EPS) * g + b
        key = jax.random.key(seed)
        ks = jax.random.split(key, 6)
        B, T = (16, 256)
        x = jax.random.normal(ks[0], (B, T, FEAT), dtype=jnp.float32)
        ada_emb = jax.random.normal(ks[1], (B, ADA), dtype=jnp.float32)
        W1 = jax.random.normal(ks[2], (ADA, INTER), dtype=jnp.float32) / np.sqrt(ADA)
        b1 = jnp.zeros((INTER,), dtype=jnp.float32)
        W2 = jax.random.normal(ks[3], (INTER, FEAT * RANK * 4), dtype=jnp.float32) * (0.1 / np.sqrt(INTER))
        b2 = jnp.zeros((FEAT * RANK * 4,), dtype=jnp.float32)
        ln_g = jnp.ones((ADA,), dtype=jnp.float32)
        ln_b = jnp.zeros((ADA,), dtype=jnp.float32)
        return {'x': x, 'ada_emb': ada_emb, 'ln_g': ln_g, 'ln_b': ln_b, 'W1': W1, 'b1': b1, 'W2': W2, 'b2': b2}
    _L0_cond_all = _L0_cond_setup()
    _L0_cond_in = {k: v for k, v in _L0_cond_all.items() if k in ('ln_g', 'ln_b', 'W1', 'b1', 'W2', 'b2')}
    del _L0_cond_all

    def _L1_cond_setup():
        import jax, jax.numpy as jnp
        import numpy as np
        NONGT = 20
        H = 16
        NEG = -9000000000000000.0

        def _gat_attention(self_feat, cond_adj, label_bias, Wq, bq, Wk, bk, Wout, bout):
            B, N, F = self_feat.shape
            ng = min(NONGT, N)
            dh = F // H
            kv = self_feat[:, :ng]
            qh = (self_feat @ Wq.T + bq).reshape(B, N, H, dh)
            kh = (kv @ Wk.T + bk).reshape(B, ng, H, dh)
            aff = jnp.einsum('bnhd,bmhd->bnhm', qh, kh) * (1.0 / np.sqrt(dh))
            mask = cond_adj[:, :, None, :] > 0
            aff = jnp.where(mask, aff, NEG) + label_bias[:, :, None, :]
            w = jax.nn.softmax(aff, axis=-1)
            out_t = jnp.einsum('bnhm,bmf->bnhf', w, kv)
            out = jnp.einsum('bnhf,hgf->bnhg', out_t, Wout) + bout.reshape(H, F // H)
            return out.reshape(B, N, F)

        def _forward(v, q, adj, W_self, b_self, w_bias, b_bias, Wq, bq, Wk, bk, Wout, bout):
            adj_f = adj.astype(jnp.float32)
            exp_v = v
            row_zero = exp_v.sum(-1) == 0
            q_exp = jnp.where(row_zero[..., None], 0.0, q[:, None, :])
            vcq = jnp.concatenate([exp_v, q_exp], axis=-1)
            self_feat = vcq @ W_self.T + b_self
            output = self_feat
            for d in range(2):
                A = adj_f if d == 0 else jnp.swapaxes(adj_f, 1, 2)
                A = A[:, :, :NONGT, :]
                cond = A.sum(-1)
                vb = A @ w_bias + b_bias
                output = output + _gat_attention(self_feat, cond, vb, Wq[d], bq[d], Wk[d], bk[d], Wout[d], bout[d])
            rel = jax.nn.relu(output)
            return exp_v + rel
        key = jax.random.key(seed)
        ks = jax.random.split(key, 8)
        B, N, L, F, Q = (64, 36, 11, 256, 256)
        IN = F + Q
        s = 0.02
        return {'v': jax.random.normal(ks[0], (B, N, F), jnp.float32), 'q': jax.random.normal(ks[1], (B, Q), jnp.float32), 'adj': jax.random.randint(ks[2], (B, N, N, L), 0, 2, jnp.int32), 'W_self': jax.random.normal(ks[3], (F, IN), jnp.float32) * s, 'b_self': jnp.zeros((F,), jnp.float32), 'w_bias': jax.random.normal(ks[4], (L,), jnp.float32) * s, 'b_bias': jnp.zeros((), jnp.float32), 'Wq': jax.random.normal(ks[5], (2, F, F), jnp.float32) * s, 'bq': jnp.zeros((2, F), jnp.float32), 'Wk': jax.random.normal(ks[6], (2, F, F), jnp.float32) * s, 'bk': jnp.zeros((2, F), jnp.float32), 'Wout': jax.random.normal(ks[7], (2, H, F // H, F), jnp.float32) * s, 'bout': jnp.zeros((2, F), jnp.float32)}
    _L1_cond_all = _L1_cond_setup()
    _L1_cond_in = {k: v for k, v in _L1_cond_all.items() if k in ('W_self', 'b_self', 'w_bias', 'b_bias', 'Wq', 'bq', 'Wk', 'bk', 'Wout', 'bout')}
    del _L1_cond_all

    def _L2_cond_setup():
        import jax, jax.numpy as jnp
        import numpy as np
        H = 256
        NH = 16
        DH = H // NH
        MLP = 4 * H
        EPS = 1e-05

        def _ln(x):
            m = jnp.mean(x, axis=-1, keepdims=True)
            v = jnp.mean((x - m) ** 2, axis=-1, keepdims=True)
            return (x - m) * jax.lax.rsqrt(v + EPS)

        def _modulate(x, shift, scale):
            return x * (1.0 + scale[:, None, :]) + shift[:, None, :]
        key = jax.random.key(seed)
        ks = jax.random.split(key, 12)
        s = 1.0 / np.sqrt(H)
        inp = {'x': jax.random.normal(ks[0], (8, 256, H), jnp.float32), 'c': jax.random.normal(ks[1], (8, H), jnp.float32), 'Wc': jax.random.normal(ks[2], (H, 6 * H), jnp.float32) * s, 'bc': jnp.zeros((6 * H,), jnp.float32), 'Wq': jax.random.normal(ks[3], (H, H), jnp.float32) * s, 'bq': jnp.zeros((H,), jnp.float32), 'Wk': jax.random.normal(ks[4], (H, H), jnp.float32) * s, 'bk': jnp.zeros((H,), jnp.float32), 'Wv': jax.random.normal(ks[5], (H, H), jnp.float32) * s, 'bv': jnp.zeros((H,), jnp.float32), 'Wo': jax.random.normal(ks[6], (H, H), jnp.float32) * s, 'bo': jnp.zeros((H,), jnp.float32), 'W1': jax.random.normal(ks[7], (H, MLP), jnp.float32) * s, 'b1': jnp.zeros((MLP,), jnp.float32), 'W2': jax.random.normal(ks[8], (MLP, H), jnp.float32) * (1.0 / np.sqrt(MLP)), 'b2': jnp.zeros((H,), jnp.float32)}
        return inp
    _L2_cond_all = _L2_cond_setup()
    _L2_cond_in = {k: v for k, v in _L2_cond_all.items() if k in ('Wc', 'bc', 'Wq', 'bq', 'Wk', 'bk', 'Wv', 'bv', 'Wo', 'bo', 'W1', 'b1', 'W2', 'b2')}
    del _L2_cond_all

    def _L3_cond_setup():
        import jax, jax.numpy as jnp
        import numpy as np
        H = 16
        EPS = 1e-05

        def layer_norm(x, g, b):
            mu = jnp.mean(x, axis=-1, keepdims=True)
            var = jnp.var(x, axis=-1, keepdims=True)
            return (x - mu) * jax.lax.rsqrt(var + EPS) * g + b
        key = jax.random.key(seed)
        ks = jax.random.split(key, 8)
        B, T, D, TE = (4, 1024, 256, 256)
        s = 0.02
        return {'x': jax.random.normal(ks[0], (B, T, D), jnp.float32), 'emb': jax.random.normal(ks[1], (B, 1, TE), jnp.float32), 'gate_msa': jax.random.normal(ks[2], (B, 1, D), jnp.float32), 'norm_g': jnp.ones((D,), jnp.float32), 'norm_b': jnp.zeros((D,), jnp.float32), 'Wq': jax.random.normal(ks[3], (D, D), jnp.float32) * s, 'bq': jnp.zeros((D,), jnp.float32), 'Wk': jax.random.normal(ks[4], (D, D), jnp.float32) * s, 'bk': jnp.zeros((D,), jnp.float32), 'Wv': jax.random.normal(ks[5], (D, D), jnp.float32) * s, 'bv': jnp.zeros((D,), jnp.float32), 'emb_W': jax.random.normal(ks[6], (TE, 2 * D), jnp.float32) * s, 'emb_b': jnp.zeros((2 * D,), jnp.float32), 'sn_g': jnp.ones((D,), jnp.float32), 'sn_b': jnp.zeros((D,), jnp.float32), 'out_W': jax.random.normal(ks[7], (D, D), jnp.float32) * s, 'out_b': jnp.zeros((D,), jnp.float32)}
    _L3_cond_all = _L3_cond_setup()
    _L3_cond_in = {k: v for k, v in _L3_cond_all.items() if k in ('norm_g', 'norm_b', 'Wq', 'bq', 'Wk', 'bk', 'Wv', 'bv', 'emb_W', 'emb_b', 'sn_g', 'sn_b', 'out_W', 'out_b')}
    del _L3_cond_all
    return {'x': x, 'cond_1024': cond_1024, 'mask_BxSxSx11_ik0': mask_BxSxSx11_ik0, 'L0_cond_ln_g': _L0_cond_in['ln_g'], 'L0_cond_ln_b': _L0_cond_in['ln_b'], 'L0_cond_W1': _L0_cond_in['W1'], 'L0_cond_b1': _L0_cond_in['b1'], 'L0_cond_W2': _L0_cond_in['W2'], 'L0_cond_b2': _L0_cond_in['b2'], 'L1_cond_W_self': _L1_cond_in['W_self'], 'L1_cond_b_self': _L1_cond_in['b_self'], 'L1_cond_w_bias': _L1_cond_in['w_bias'], 'L1_cond_b_bias': _L1_cond_in['b_bias'], 'L1_cond_Wq': _L1_cond_in['Wq'], 'L1_cond_bq': _L1_cond_in['bq'], 'L1_cond_Wk': _L1_cond_in['Wk'], 'L1_cond_bk': _L1_cond_in['bk'], 'L1_cond_Wout': _L1_cond_in['Wout'], 'L1_cond_bout': _L1_cond_in['bout'], 'L2_cond_Wc': _L2_cond_in['Wc'], 'L2_cond_bc': _L2_cond_in['bc'], 'L2_cond_Wq': _L2_cond_in['Wq'], 'L2_cond_bq': _L2_cond_in['bq'], 'L2_cond_Wk': _L2_cond_in['Wk'], 'L2_cond_bk': _L2_cond_in['bk'], 'L2_cond_Wv': _L2_cond_in['Wv'], 'L2_cond_bv': _L2_cond_in['bv'], 'L2_cond_Wo': _L2_cond_in['Wo'], 'L2_cond_bo': _L2_cond_in['bo'], 'L2_cond_W1': _L2_cond_in['W1'], 'L2_cond_b1': _L2_cond_in['b1'], 'L2_cond_W2': _L2_cond_in['W2'], 'L2_cond_b2': _L2_cond_in['b2'], 'L3_cond_norm_g': _L3_cond_in['norm_g'], 'L3_cond_norm_b': _L3_cond_in['norm_b'], 'L3_cond_Wq': _L3_cond_in['Wq'], 'L3_cond_bq': _L3_cond_in['bq'], 'L3_cond_Wk': _L3_cond_in['Wk'], 'L3_cond_bk': _L3_cond_in['bk'], 'L3_cond_Wv': _L3_cond_in['Wv'], 'L3_cond_bv': _L3_cond_in['bv'], 'L3_cond_emb_W': _L3_cond_in['emb_W'], 'L3_cond_emb_b': _L3_cond_in['emb_b'], 'L3_cond_sn_g': _L3_cond_in['sn_g'], 'L3_cond_sn_b': _L3_cond_in['sn_b'], 'L3_cond_out_W': _L3_cond_in['out_W'], 'L3_cond_out_b': _L3_cond_in['out_b']}

def reference(x, cond_1024, mask_BxSxSx11_ik0, L0_cond_ln_g, L0_cond_ln_b, L0_cond_W1, L0_cond_b1, L0_cond_W2, L0_cond_b2, L1_cond_W_self, L1_cond_b_self, L1_cond_w_bias, L1_cond_b_bias, L1_cond_Wq, L1_cond_bq, L1_cond_Wk, L1_cond_bk, L1_cond_Wout, L1_cond_bout, L2_cond_Wc, L2_cond_bc, L2_cond_Wq, L2_cond_bq, L2_cond_Wk, L2_cond_bk, L2_cond_Wv, L2_cond_bv, L2_cond_Wo, L2_cond_bo, L2_cond_W1, L2_cond_b1, L2_cond_W2, L2_cond_b2, L3_cond_norm_g, L3_cond_norm_b, L3_cond_Wq, L3_cond_bq, L3_cond_Wk, L3_cond_bk, L3_cond_Wv, L3_cond_bv, L3_cond_emb_W, L3_cond_emb_b, L3_cond_sn_g, L3_cond_sn_b, L3_cond_out_W, L3_cond_out_b):
    import jax
    import jax.numpy as jnp

    def _L0_cond_ref(x, ada_emb, ln_g, ln_b, W1, b1, W2, b2):
        import jax, jax.numpy as jnp
        import numpy as np
        FEAT = 256
        ADA = 256
        INTER = 256
        RANK = 8
        EPS = 1e-05

        def _layernorm(a, g, b):
            mu = jnp.mean(a, axis=-1, keepdims=True)
            var = jnp.mean(jnp.square(a - mu), axis=-1, keepdims=True)
            return (a - mu) * jax.lax.rsqrt(var + EPS) * g + b
        B, T, D = x.shape
        h = jax.nn.gelu(_layernorm(ada_emb, ln_g, ln_b) @ W1 + b1, approximate=False)
        w = h @ W2 + b2
        a1, bb1, a2, bb2 = jnp.split(w, 4, axis=-1)
        a1 = a1.reshape(B, D, RANK)
        bb1 = bb1.reshape(B, D, RANK)
        a2 = a2.reshape(B, D, RANK)
        bb2 = bb2.reshape(B, D, RANK)
        y = jnp.einsum('btd,bdr->btr', x, a1)
        y = jnp.einsum('btr,bdr->btd', y, bb1)
        y = jax.nn.gelu(y, approximate=False)
        y = jnp.einsum('btd,bdr->btr', y, a2)
        y = jnp.einsum('btr,bdr->btd', y, bb2)
        return y + x

    def _L1_cond_ref(v, q, adj, W_self, b_self, w_bias, b_bias, Wq, bq, Wk, bk, Wout, bout):
        import jax, jax.numpy as jnp
        import numpy as np
        NONGT = 20
        H = 16
        NEG = -9000000000000000.0

        def _gat_attention(self_feat, cond_adj, label_bias, Wq, bq, Wk, bk, Wout, bout):
            B, N, F = self_feat.shape
            ng = min(NONGT, N)
            dh = F // H
            kv = self_feat[:, :ng]
            qh = (self_feat @ Wq.T + bq).reshape(B, N, H, dh)
            kh = (kv @ Wk.T + bk).reshape(B, ng, H, dh)
            aff = jnp.einsum('bnhd,bmhd->bnhm', qh, kh) * (1.0 / np.sqrt(dh))
            mask = cond_adj[:, :, None, :] > 0
            aff = jnp.where(mask, aff, NEG) + label_bias[:, :, None, :]
            w = jax.nn.softmax(aff, axis=-1)
            out_t = jnp.einsum('bnhm,bmf->bnhf', w, kv)
            out = jnp.einsum('bnhf,hgf->bnhg', out_t, Wout) + bout.reshape(H, F // H)
            return out.reshape(B, N, F)

        def _forward(v, q, adj, W_self, b_self, w_bias, b_bias, Wq, bq, Wk, bk, Wout, bout):
            adj_f = adj.astype(jnp.float32)
            exp_v = v
            row_zero = exp_v.sum(-1) == 0
            q_exp = jnp.where(row_zero[..., None], 0.0, q[:, None, :])
            vcq = jnp.concatenate([exp_v, q_exp], axis=-1)
            self_feat = vcq @ W_self.T + b_self
            output = self_feat
            for d in range(2):
                A = adj_f if d == 0 else jnp.swapaxes(adj_f, 1, 2)
                A = A[:, :, :NONGT, :]
                cond = A.sum(-1)
                vb = A @ w_bias + b_bias
                output = output + _gat_attention(self_feat, cond, vb, Wq[d], bq[d], Wk[d], bk[d], Wout[d], bout[d])
            rel = jax.nn.relu(output)
            return exp_v + rel
        return _forward(v, q, adj, W_self, b_self, w_bias, b_bias, Wq, bq, Wk, bk, Wout, bout)

    def _L2_cond_ref(x, c, Wc, bc, Wq, bq, Wk, bk, Wv, bv, Wo, bo, W1, b1, W2, b2):
        import jax, jax.numpy as jnp
        import numpy as np
        H = 256
        NH = 16
        DH = H // NH
        MLP = 4 * H
        EPS = 1e-05

        def _ln(x):
            m = jnp.mean(x, axis=-1, keepdims=True)
            v = jnp.mean((x - m) ** 2, axis=-1, keepdims=True)
            return (x - m) * jax.lax.rsqrt(v + EPS)

        def _modulate(x, shift, scale):
            return x * (1.0 + scale[:, None, :]) + shift[:, None, :]
        B, S, _ = x.shape
        c6 = jax.nn.silu(c) @ Wc + bc
        sh_msa, sc_msa, g_msa, sh_mlp, sc_mlp, g_mlp = jnp.split(c6, 6, axis=-1)
        xm = _modulate(_ln(x), sh_msa, sc_msa)
        q = (xm @ Wq + bq).reshape(B, S, NH, DH)
        k = (xm @ Wk + bk).reshape(B, S, NH, DH)
        v = (xm @ Wv + bv).reshape(B, S, NH, DH)
        q = q / DH
        w = jnp.einsum('bqhc,bkhc->bhqk', q, k)
        w = jax.nn.softmax(w, axis=-1)
        y = jnp.einsum('bhqk,bkhc->bqhc', w, v).reshape(B, S, H)
        x = x + g_msa[:, None, :] * (y @ Wo + bo)
        xm2 = _modulate(_ln(x), sh_mlp, sc_mlp)
        h = jax.nn.gelu(xm2 @ W1 + b1, approximate=False)
        x = x + g_mlp[:, None, :] * (h @ W2 + b2)
        return x

    def _L3_cond_ref(x, emb, gate_msa, norm_g, norm_b, Wq, bq, Wk, bk, Wv, bv, emb_W, emb_b, sn_g, sn_b, out_W, out_b):
        import jax, jax.numpy as jnp
        import numpy as np
        H = 16
        EPS = 1e-05

        def layer_norm(x, g, b):
            mu = jnp.mean(x, axis=-1, keepdims=True)
            var = jnp.var(x, axis=-1, keepdims=True)
            return (x - mu) * jax.lax.rsqrt(var + EPS) * g + b
        B, T, D = x.shape
        dh = D // H
        xn = layer_norm(x, norm_g, norm_b)
        q = (xn @ Wq + bq).reshape(B, T, H, dh)
        k = (xn @ Wk + bk).reshape(B, T, H, dh)
        v = (xn @ Wv + bv).reshape(B, T, H, dh)
        q = jax.nn.softmax(q, axis=-1)
        k = jax.nn.softmax(k, axis=1)
        ctx = jnp.einsum('bnhd,bnhl->bhdl', k, v)
        y = jnp.einsum('bnhd,bhdl->bnhl', q, ctx).reshape(B, T, D)
        emb_out = jax.nn.silu(emb) @ emb_W + emb_b
        scale, shift = jnp.split(emb_out, 2, axis=-1)
        h = layer_norm(y, sn_g, sn_b) * (1.0 + scale) + shift
        h = jax.nn.silu(h) @ out_W + out_b
        return x + gate_msa * h
    x = _L0_cond_ref(x, cond_1024, L0_cond_ln_g, L0_cond_ln_b, L0_cond_W1, L0_cond_b1, L0_cond_W2, L0_cond_b2)
    x = _L1_cond_ref(x, cond_1024, mask_BxSxSx11_ik0, L1_cond_W_self, L1_cond_b_self, L1_cond_w_bias, L1_cond_b_bias, L1_cond_Wq, L1_cond_bq, L1_cond_Wk, L1_cond_bk, L1_cond_Wout, L1_cond_bout)
    x = _L2_cond_ref(x, cond_1024, L2_cond_Wc, L2_cond_bc, L2_cond_Wq, L2_cond_bq, L2_cond_Wk, L2_cond_bk, L2_cond_Wv, L2_cond_bv, L2_cond_Wo, L2_cond_bo, L2_cond_W1, L2_cond_b1, L2_cond_W2, L2_cond_b2)
    x = _L3_cond_ref(x, cond_1024[:, None, :], cond_1024[:, None, :], L3_cond_norm_g, L3_cond_norm_b, L3_cond_Wq, L3_cond_bq, L3_cond_Wk, L3_cond_bk, L3_cond_Wv, L3_cond_bv, L3_cond_emb_W, L3_cond_emb_b, L3_cond_sn_g, L3_cond_sn_b, L3_cond_out_W, L3_cond_out_b)
    return x

_drawn_inputs = setup_inputs


def setup_inputs(seed=0):
    import zlib

    import numpy as np

    out = dict(_drawn_inputs(seed))
    spreads = {'L0_cond_ln_g': (1.0, 0.2),
     'L0_cond_ln_b': (0.0, 0.31),
     'L0_cond_b1': (0.0, 0.296),
     'L0_cond_b2': (0.0, 0.1),
     'L1_cond_b_self': (0.0, 0.1),
     'L1_cond_bq': (0.0, 0.1),
     'L1_cond_bk': (0.0, 0.1),
     'L1_cond_bout': (0.0, 0.1),
     'L2_cond_bc': (0.0, 0.1),
     'L2_cond_bq': (0.0, 2.0),
     'L2_cond_bk': (0.0, 2.0),
     'L2_cond_bv': (0.0, 0.1),
     'L2_cond_bo': (0.0, 0.1),
     'L2_cond_b1': (0.0, 0.1),
     'L2_cond_b2': (0.0, 0.1),
     'L3_cond_norm_g': (1.0, 0.6),
     'L3_cond_norm_b': (0.0, 0.276),
     'L3_cond_bq': (0.0, 2.0),
     'L3_cond_bk': (0.0, 2.0),
     'L3_cond_bv': (0.0, 0.1),
     'L3_cond_emb_b': (0.0, 0.348),
     'L3_cond_sn_g': (1.0, 0.2),
     'L3_cond_sn_b': (0.0, 0.563),
     'L3_cond_out_b': (0.0, 0.1)}
    factors = {'L3_cond_Wq': 8.0, 'L3_cond_Wk': 8.0}
    for name, (base, spread) in spreads.items():
        noise = np.random.default_rng([zlib.crc32(name.encode()), seed]).standard_normal(out[name].shape)
        drawn = base * np.exp(spread * noise) if base else spread * noise
        out[name] = jnp.asarray(drawn.astype(out[name].dtype))
    for name, factor in factors.items():
        out[name] = (out[name] * factor).astype(out[name].dtype)
    return out
```

```python
from contextlib import ExitStack

import concourse.bass as bass
from concourse import mybir

F32 = mybir.dt.float32
BF16 = mybir.dt.bfloat16
I32 = mybir.dt.int32
ALU = mybir.AluOpType
ACT = mybir.ActivationFunctionType
AX = mybir.AxisListType.X

B, T, D = 16, 256, 256
P = 128
C = D // P
TT = T // P
H = 16
DH = D // H
HC = P // DH
RANK = 8
M = 20
MP = 24
NL = 11
MLP = 4 * D
EPS = 1e-5
NEG = -9000000000000000.0
SLOTS = 2
SPLIT_Q = (0, 0, 1, 1, 0, 2)
SPLIT_K = (0, 1, 0, 1, 2, 0)
KS = DH * len(SPLIT_Q)

W_COLS = {}
_at = 0
for _name, _n in (("self", C * D), ("gq", 2 * C * D), ("gk", 2 * C * D), ("gv", C * 2 * D),
                  ("q2", C * D), ("k2", C * D), ("v2", C * D), ("o2", C * D),
                  ("w1", C * MLP), ("w2", MLP // P * D),
                  ("q3", C * D), ("k3", C * D), ("v3", C * D), ("o3", C * D)):
    W_COLS[_name] = (_at, _n)
    _at += _n
W_TOTAL = _at
V_COLS = {}
_at = 0
for _name, _n in (("ln_g", C), ("ln_b", C), ("b1", C), ("b2", 64), ("bself", C), ("gbq", 2 * C), ("gbk", 2 * C),
                  ("gbout", 2 * C), ("bc", 6 * C), ("bq2", C), ("bk2", C), ("bo2", C), ("mb1", MLP // P),
                  ("mb2", C), ("n3g", C), ("n3b", C), ("bk3", C), ("embb", 2 * C), ("sng", C), ("snb", C),
                  ("ob3", C), ("cond", C * B)):
    V_COLS[_name] = (_at, _n)
    _at += _n
V_TOTAL = _at
R_COLS = {"bv2": (0, D), "bq3": (D, D), "bv3": (2 * D, D), "wl": (3 * D, NL), "bb": (3 * D + NL, 1)}
R_TOTAL = 3 * D + NL + 1
S_COLS = {"selfq": (0, C * D), "w1": (C * D, C * D), "wc": (2 * C * D, C * 6 * D), "emb": (8 * C * D, C * 2 * D)}
S_TOTAL = 10 * C * D
NLOW = 4 * C * RANK
MOD = NLOW
AFF = MOD + 6 * C
GATE = AFF + 2 * C
NPAR = GATE + C


class Progress:

    def __init__(self, sems, names):
        self.sems, self.names = sems, names
        self.next = [0] * len(sems)

    def inc(self, s, name):
        assert self.names[self.next[s] % len(self.names)] == name, (name, self.names[self.next[s] % len(self.names)])
        self.next[s] += 1
        return self.sems[s], 1

    def at(self, s, it, name):
        return self.sems[s], it * len(self.names) + self.names.index(name) + 2

    def past(self, s, it):
        return self.sems[s], it * len(self.names) + 1

    def begin(self, engine):
        for sem in self.sems:
            engine.sem_inc(sem, 1)


def build(nc, x_in, cond_in, adj_in, w_in, v_in, r_in, s_in, low_in, out):
    ctx = ExitStack()
    with ctx:
        def sb(name, shape, dt=F32):
            return ctx.enter_context(nc.sbuf_tensor(name, shape, dt))

        def sem(name):
            return ctx.enter_context(nc.semaphore(name))

        def progress(name, names):
            return Progress([sem(f"{name}_{s}") for s in range(SLOTS)], names.split())

        W = sb("W", [P, W_TOTAL])
        V = sb("V", [P, V_TOTAL])
        R = sb("R", [P, R_TOTAL])
        par_all = sb("par_all", [P, B, NPAR])
        ident = sb("ident", [P, P])
        mean_w = sb("mean_w", [P, P])
        ones_c = sb("ones_c", [P, 1])
        eps_c = sb("eps_c", [P, 1])
        sel = sb("sel", [96, H, P], BF16)
        blk16 = sb("blk16", [P, HC, DH])
        blk24 = sb("blk24", [4 * MP, 4, DH])
        probs = sb("probs", [P, 4, 4, T])

        def w(name, a):
            lo, n = W_COLS[name]
            return W[:, lo:lo + n].rearrange("p (a n) -> p a n", a=a)

        def vec(name):
            lo, n = V_COLS[name]
            return V[:, lo:lo + n]

        def row(name):
            lo, n = R_COLS[name]
            return R[:, lo:lo + n]

        class Slot:
            pass

        SL = []
        for s in range(SLOTS):
            o = Slot()

            def own(name, shape, dt=F32, s=s):
                return sb(f"{name}{s}", shape, dt)

            o.par_low = own("par_low", [P, NLOW])
            o.par = own("par", [P, NPAR - NLOW])
            o.x = own("x", [P, C, T])
            o.x1 = own("x1_", [P, C, T])
            o.x2 = own("x2_", [P, C, T])
            o.xc = own("xc", [P, C, T])
            o.sq = own("sq", [P, C, T])
            o.rstd = own("rstd", [P, T])
            o.xm = own("xm", [P, C, T])
            o.big = own("big", [P, 8, T])
            o.bbT = own("bbT", [P, 2, C, P])
            o.y1 = own("y1_", [P, T])
            o.zrow = own("zrow", [P, T])
            o.qrow = own("qrow", [P, D])
            o.sfrep = own("sfrep", [P, C, 4, MP])
            o.kb = own("kb", [P, 2 * C, M])
            o.cond = own("cond_", [P, TT, 2 * M])
            o.mask = own("mask", [P, TT, 2 * M])
            o.bias = own("bias", [P, TT, 2 * M])
            o.mx = own("mx", [P, 2 * H])
            o.sm = own("sm", [P, 2 * H])
            o.ri = own("ri", [P, 2 * H])
            o.stack = own("stack", [P, 2 * H * T], BF16)
            o.parts = own("parts", [P, 3 * 2 * C * T], BF16)
            o.vp = own("vp", [P, TT, H, 2 * DH])
            o.yF = own("yF", [P, C, T])
            o.mx2 = own("mx2_", [P, TT, H])
            o.nmx = own("nmx", [96, T], BF16)
            o.ks = own("ks", [P, C])
            o.nk = own("nk", [P, C])
            o.ctx = own("ctx_", [P, C, P])
            st = o.stack[:, :].bitcast(F32)
            o.adj = st[:, 0:880].bitcast(I32).rearrange("p (t n) -> p t n", t=TT)
            o.adjw = st[:, 880:1760].rearrange("p (t n) -> p t n", t=TT)
            o.S = st[:, 1760:1760 + 2 * H * M].rearrange("p (g m) -> p g m", m=M)
            o.gq = st[:, 2400:2400 + C * T].rearrange("p (c t) -> p c t", c=C)
            o.kbd = st[:, 2912:2912 + 2 * C * HC * M].rearrange("p (g h m) -> p g h m", h=HC, m=M)
            o.sf = st[:, 3552:3552 + C * T].rearrange("p (c t) -> p c t", c=C)
            o.gq1 = o.xm
            o.st = o.stack[:, :].rearrange("p (k h t) -> p k h t", k=2, h=H)
            o.qk = o.big[:, 0:4, :].rearrange("p (k c) t -> p k c t", k=2)
            o.rest = o.big[:, 4:8, :].rearrange("p (k c) t -> p k c t", k=2)
            o.part = o.parts[:, :].rearrange("p (j k c t) -> p j k c t", j=3, k=2, c=C)
            pf = o.parts[:, :].bitcast(F32)
            o.P = pf[:, :].rearrange("p (t h m) -> p t h m", t=TT, m=MP)
            o.oraw = pf[:, 0:1024].rearrange("p (g t) -> p g t", g=4)
            o.yq = pf[:, 1024:1536].rearrange("p (g l) -> p g l", l=DH)
            o.kT = pf[:, 0:512].rearrange("p (t c) -> p t c", t=TT)
            o.vt = pf[:, 512:1024].rearrange("p (t c) -> p t c", t=TT)
            o.ke = pf[:, 1024:1536].rearrange("p (c t) -> p c t", c=C)
            o.PT = o.big
            o.vbd = o.yF[0:4 * MP, :, :].rearrange("p a n -> p (a n)").rearrange("p (g n) -> p g n", g=8)
            o.h = o.big
            o.q3 = o.big[:, 0:2, :]
            o.q3s = o.big[:, 2:4, :]
            o.kf = o.big[:, 4:6, :]
            SL.append(o)

        G = ctx.enter_context(nc.psum_tensor("G", [P, SLOTS, 2, 512], F32))
        SS = ctx.enter_context(nc.psum_tensor("SS", [P, 2, 1024], F32))
        scr = [nc.dram_tensor(f"scr{s}", [3, 2, C * P, T], BF16, kind="Internal").ap() for s in range(SLOTS)]
        qscr = nc.dram_tensor("qscr", [B, D], F32, kind="Internal").ap()

        start_w = probs[:, :, :, :].rearrange("p a b t -> p (a b t)")
        sw_f = SL[1].big[:, 0:4, :].rearrange("p a t -> p (a t)")

        def sw(name, a):
            lo, n = S_COLS[name]
            src = start_w[:, lo:lo + n] if lo + n <= 4096 else sw_f[:, lo - 4096:lo + n - 4096]
            return src.rearrange("p (a n) -> p a n", a=a)

        low_w = [SL[s].stack[:, :].bitcast(F32).rearrange("p (c n) -> p c n", c=C) for s in range(SLOTS)]
        ct = sb("ct", [B, D])
        cstat = sb("cstat", [B, 16])
        cT = sb("cT", [P, C, B])
        hT = sb("hT", [P, C, 32])
        wsb = SL[0].big[:, 0:2, :].rearrange("p a t -> p (a t)")
        sil = sb("sil", [P, C * B])
        sil2 = sb("sil2", [P, C * B])
        e1 = sb("e1", [P, 2 * C, B])

        ld_small = sem("ld_small")
        ld_start = sem("ld_start")
        ld_low = [sem(f"ld_low{i}") for i in range(2)]
        ld_w = sem("ld_w")
        ld_x = [sem(f"ld_x{s}") for s in range(SLOTS)]
        ld_adj = [sem(f"ld_adj{s}") for s in range(SLOTS)]
        split_out = [sem(f"split_out{s}") for s in range(SLOTS)]
        stacked = [sem(f"stacked{s}") for s in range(SLOTS)]
        stored = [sem(f"stored{s}") for s in range(SLOTS)]
        q_out = sem("q_out")
        ld_q = [sem(f"ld_q{s}") for s in range(SLOTS)]
        const_done = sem("const_done")
        pool_mask = sem("pool_mask")
        pre_pe = sem("pre_pe")
        pre_dve = sem("pre_dve")
        pre_act = sem("pre_act")

        pool_p = progress("pool_par", "low par pads")
        pool_g = progress("pool_gat", "p0 p1")
        pe_low = progress("pe_low", "bb y1 y2 z x1")
        act_low = progress("act_low", "g")
        dve_low = progress("dve_low", "bb y1 z x1")
        pe_gat = progress("pe_gat", "sum self q0 k q1 v s0 s1 t0 t1 pv")
        act_gat = progress("act_gat", "sf e0 e1 t0 t1")
        dve_gat = progress("dve_gat", "cond adjw vb mask neg bias zrow sfrep q0 kb kbd q1 vbd "
                           "m0 a0 x0 d0 s0 r0 m1 a1 x1 d1 s1 r1 o0 o1 x2")
        LN = "mean var"
        pe_ln = [progress(f"pe_ln{i}", LN) for i in range(4)]
        act_ln = [progress(f"act_ln{i}", "sq ln rstd") for i in range(4)]
        dve_ln = [progress(f"dve_ln{i}", "xc xn xm") for i in range(4)]
        pe_att = progress("pe_att", "q k v " + " ".join(f"m{u}" for u in range(8)) + " mx "
                          + " ".join(f"e{u}" + (f" p{u // 2 - 1}" if u % 2 and u > 1 else "") for u in range(8))
                          + " p3 ot yt o")
        act_att = progress("act_att", "c1 c2 " + " ".join(f"e{u}" for u in range(8)) + " o y")
        dve_att = progress("dve_att", "q k r1 vp c3 " + " ".join(f"m{u}" for u in range(8))
                           + " hi lo ri yq t x3")
        pe_mlp = progress("pe_mlp", "h0 h1 h2 h3 w2")
        act_mlp = progress("act_mlp", "h0 h1 h2 h3")
        dve_mlp = progress("dve_mlp", "t x4")
        pe_lin = progress("pe_lin", "q k v qT kT ctx y o")
        act_lin = progress("act_lin", "eq ek qT kT y tanh")
        dve_lin = progress("dve_lin", "q mx d k nk v sm ri p rk ctx s t out")

        N_CONST = 7 + SLOTS * 7
        block = ctx.enter_context(nc.Block())

        @block.sync
        def _(sp):
            sp.dma_start(V[:, :], v_in).then_inc(ld_small, 16)
            sp.dma_start(ct[:, :], cond_in).then_inc(ld_small, 16)
            sp.dma_start(R[:, :], r_in.to_broadcast([P, R_TOTAL])).then_inc(ld_small, 16)
            sp.dma_start(start_w[:, 0:4096], s_in[:, 0:4096]).then_inc(ld_start, 16)
            sp.dma_start(sw_f, s_in[:, 4096:]).then_inc(ld_start, 16)
            for p in range(4):
                if p >= 2:
                    sp.wait_ge(pre_pe, 5 + 2 * (p - 2))
                sp.dma_start(low_w[p % 2], low_in[p]).then_inc(ld_low[p % 2], 16)
            sp.wait_ge(pre_dve, 6)
            sp.dma_start(qscr, ct[:, :]).then_inc(q_out, 16)
            sp.wait_ge(q_out, 16)
            with sp.Fori(0, B // SLOTS) as it:
                counts = [[(sm, sp.snap(n)) for sm, n in (
                    dve_att.at(s, it, "c3"), act_att.at(s, it, "c2"), pe_gat.at(s, it, "pv"), (split_out[s], it * 16 + 16))]
                    for s in range(SLOTS)]
                for s, o in enumerate(SL):
                    third, second, graph_read, parts_out = counts[s]
                    sp.wait_ge(*third)
                    sp.wait_ge(*second)
                    sp.dma_start(scr[s].rearrange("j k (c p) t -> p (j k c) t", p=P),
                                 o.part.rearrange("p j k c t -> p (j k c) t")).then_inc(split_out[s], 16)
                    sp.wait_ge(*parts_out)
                    sp.wait_ge(*graph_read)
                    for k, split in enumerate((SPLIT_Q, SPLIT_K)):
                        for j, part in enumerate(split):
                            sp.dma_start(o.st[j * DH:(j + 1) * DH, k, :, :],
                                         scr[s][part, k].rearrange("(h c) t -> c h t", c=DH)).then_inc(stacked[s], 16)
            for s in range(SLOTS):
                sp.wait_ge(stored[s], 16 * (B // SLOTS + 1))

        @block.gpsimd
        def _(pool):
            for p in (pool_p, pool_g):
                p.begin(pool)
            def mark(ins):
                ins.then_inc(const_done, 1)

            n = 0
            for t in (ident[:, :], sel[:, :, :]):
                pool.memset(t, 0.0).then_inc(pool_mask, 1)
                n += 1
            for t in (blk16[:, :, :], blk24[:, :, :]):
                pool.memset(t, 1.0).then_inc(pool_mask, 1)
                n += 1
            pool.wait_ge(pool_mask, n)
            mark(pool.affine_select(out=ident[:, :], in_=ident[:, :], compare_op=ALU.not_equal, fill=1.0, base=0,
                                    pattern=[[-1, P]], channel_multiplier=1))
            for base in (0, -32):
                pool.affine_select(out=sel[:, :, :], in_=sel[:, :, :], compare_op=ALU.not_equal, fill=1.0, base=base,
                                   pattern=[[-1, H], [0, P]], channel_multiplier=1).then_inc(pool_mask, 1)
                n += 1
                pool.wait_ge(pool_mask, n)
            for t, size, g in ((blk16, DH, HC), (blk24, MP, 4)):
                pool.affine_select(out=t[:, :, :], in_=t[:, :, :], compare_op=ALU.is_ge, fill=0.0, base=0,
                                   pattern=[[-size, g], [0, DH]], channel_multiplier=1).then_inc(pool_mask, 1)
                n += 1
                pool.wait_ge(pool_mask, n)
                mark(pool.affine_select(out=t[:, :, :], in_=t[:, :, :], compare_op=ALU.is_ge, fill=0.0, base=size - 1,
                                        pattern=[[size, g], [0, DH]], channel_multiplier=-1))
            mark(pool.memset(mean_w[:, :], 1.0 / D))
            mark(pool.memset(ones_c[:, :], 1.0))
            mark(pool.memset(eps_c[:, :], EPS))
            mark(pool.memset(hT[:, :, :], 0.0))
            for o in SL:
                for t in (o.bbT[:, :, :, :], o.y1[:, :], o.zrow[:, :], o.qrow[:, :], o.sfrep[:, :, :, :], o.nmx[:, :]):
                    mark(pool.memset(t, 0.0))
                mark(pool.memset(o.vp[:, :, :, :], 1.0))
            pool.wait_ge(pre_dve, 17)
            pool.wait_ge(q_out, 16)
            with pool.Fori(0, B // SLOTS) as it:
                def load(s, o):
                    b = it * SLOTS + s
                    pool.wait_ge(*dve_low.past(s, it))
                    pool.dma_start(o.x[:, :, :], x_in[bass.ds(b, 1)].rearrange("o p c t -> p (o c) t")).then_inc(ld_x[s], 16)
                    pool.wait_ge(*pe_gat.past(s, it))
                    pool.dma_start(o.qrow[0:1, :], qscr[bass.ds(b, 1)]).then_inc(ld_q[s], 16)
                    pool.wait_ge(*pe_att.past(s, it))
                    pool.dma_start(o.adj, adj_in[bass.ds(b, 1)].rearrange("o (t p) n -> p (o t) n", p=P)).then_inc(ld_adj[s], 16)

                def params(s, o):
                    b = it * SLOTS + s
                    pool.wait_ge(*pe_low.past(s, it))
                    pool.tensor_copy(o.par_low[:, :], par_all[:, bass.ds(b, 1), 0:NLOW].rearrange("p o n -> p (o n)"))\
                        .then_inc(*pool_p.inc(s, "low"))
                    pool.wait_ge(*dve_lin.past(s, it))
                    pool.tensor_copy(o.par[:, :], par_all[:, bass.ds(b, 1), NLOW:NPAR].rearrange("p o n -> p (o n)"))\
                        .then_inc(*pool_p.inc(s, "par"))
                    pool.memset(o.P[:, :, :, M:MP], 0.0).then_inc(*pool_p.inc(s, "pads"))

                def gat_norm(s, o, t):
                    pool.wait_ge(*dve_gat.at(s, it, f"r{t}"))
                    pool.tensor_tensor(o.P[:, t, :, 0:M], o.P[:, t, :, 0:M],
                                       o.ri[:, :].unsqueeze(2).to_broadcast([P, 2 * H, M]), ALU.mult)\
                        .then_inc(*pool_g.inc(s, f"p{t}"))

                for s, o in enumerate(SL):
                    load(s, o)
                for s, o in enumerate(SL):
                    params(s, o)
                for t in range(TT):
                    for s, o in enumerate(SL):
                        gat_norm(s, o, t)

        @block.tensor
        def _(pe):
            for p in (pe_low, pe_gat, *pe_ln, pe_att, pe_mlp, pe_lin):
                p.begin(pe)
            def mm(out_, lhsT, rhs, start=True, stop=True):
                return pe.matmul(out_, lhsT, rhs, start=start, stop=stop)

            def dense_f(bank, wt, src, cols=C, n=T):
                for m in range(cols):
                    for c in range(C):
                        last = mm(bank[:, m * n:(m + 1) * n], wt[:, c, m * P:(m + 1) * P], src[:, c, :],
                                  c == 0, c == C - 1)
                return last

            def dense_t(bank, wt, src):
                for t in range(TT):
                    for c in range(C):
                        last = mm(bank[:, t * D:(t + 1) * D], src[:, c, t * P:(t + 1) * P], wt[:, c, :],
                                  c == 0, c == C - 1)
                return last

            A0, A1, A2, A3 = SS[:, 0, 0:512], SS[:, 0, 512:1024], SS[:, 1, 0:512], SS[:, 1, 512:1024]
            pe.wait_ge(const_done, N_CONST)
            pe.wait_ge(ld_start, 32)
            pe.wait_ge(ld_small, 48)
            cF = vec("cond").rearrange("p (c b) -> p c b", c=C)
            for c in range(C):
                last = mm(A3[0:B, 0:D], cF[:, c, :], sw("selfq", C)[:, c, :], c == 0, c == C - 1)
            last.then_inc(pre_pe, 1)
            pe.wait_ge(pre_dve, 2)
            for c in range(C):
                last = pe.transpose(A0[:, c * B:(c + 1) * B], ct[:, c * P:(c + 1) * P], ident[0:B, 0:B])
            last.then_inc(pre_pe, 1)
            pe.wait_ge(pre_dve, 4)
            for m in range(C):
                for c in range(C):
                    last = mm(A1[:, m * B:(m + 1) * B], sw("w1", C)[:, c, m * P:(m + 1) * P], cT[:, c, :],
                              c == 0, c == C - 1)
            last.then_inc(pre_pe, 1)
            pe.wait_ge(pre_act, 3)
            for p in range(4):
                pe.wait_ge(ld_low[p % 2], 16 * (p // 2 + 1))
                if p:
                    pe.wait_ge(pre_act, 3 + p)
                for a in range(4):
                    for c in range(C):
                        last = mm(A2[32 * a:32 * a + 32, :], hT[:, c, :], low_w[p % 2][:, c, a * 512:(a + 1) * 512],
                                  c == 0, c == C - 1)
                last.then_inc(pre_pe, 1)
                pe.wait_ge(pre_act, 4 + p)
                if p:
                    pe.wait_ge(pre_dve, 6 + p)
                else:
                    pe.wait_ge(pre_dve, 4)
                for j in range(4):
                    last = pe.transpose(A0[:, j * P:(j + 1) * P], wsb[:, j * P:(j + 1) * P], ident[:, :])
                last.then_inc(pre_pe, 1)
            pe.wait_ge(pre_act, 8)
            pe.wait_ge(pre_dve, 13)
            silv = sil[:, :].rearrange("p (c b) -> p c b", c=C)
            for m in range(6 * C):
                for c in range(C):
                    mm(A1[:, m * B:(m + 1) * B], sw("wc", C)[:, c, m * P:(m + 1) * P], silv[:, c, :], c == 0, c == C - 1)
            for m in range(2 * C):
                for c in range(C):
                    last = mm(A1[:, (6 * C + m) * B:(6 * C + m + 1) * B], sw("emb", C)[:, c, m * P:(m + 1) * P],
                              silv[:, c, :], c == 0, c == C - 1)
            last.then_inc(pre_pe, 1)
            pe.wait_ge(pre_dve, 17)
            pe.wait_ge(ld_w, 32)

            with pe.Fori(0, B // SLOTS) as it:
                def low_1(s, o):
                    pe.wait_ge(*pool_p.at(s, it, "low"))
                    pe.wait_ge(*dve_lin.past(s, it))
                    for f in range(2):
                        for c in range(C):
                            k = (2 * f + 1) * C * RANK + c * RANK
                            last = pe.transpose(G[0:RANK, s, 1, (f * C + c) * P:(f * C + c + 1) * P],
                                                o.par_low[:, k:k + RANK], ident[:, :])
                    last.then_inc(*pe_low.inc(s, "bb"))
                    pe.wait_ge(ld_x[s], it * 16 + 16)
                    for c in range(C):
                        last = mm(G[0:RANK, s, 0, 0:T], o.par_low[:, c * RANK:(c + 1) * RANK], o.x[:, c, :], c == 0, c == C - 1)
                    last.then_inc(*pe_low.inc(s, "y1"))

                def low_2(s, o):
                    pe.wait_ge(*dve_low.at(s, it, "y1"))
                    for c in range(C):
                        last = mm(G[:, s, 0, c * T:(c + 1) * T], o.bbT[:, 0, c, :], o.y1[:, :])
                    last.then_inc(*pe_low.inc(s, "y2"))

                def low_3(s, o):
                    pe.wait_ge(*act_low.at(s, it, "g"))
                    for c in range(C):
                        k = 2 * C * RANK + c * RANK
                        last = mm(G[0:RANK, s, 1, 0:T], o.par_low[:, k:k + RANK], o.xm[:, c, :], c == 0, c == C - 1)
                    last.then_inc(*pe_low.inc(s, "z"))

                def low_4(s, o):
                    pe.wait_ge(*dve_low.at(s, it, "z"))
                    for c in range(C):
                        last = mm(G[:, s, 0, c * T:(c + 1) * T], o.bbT[:, 1, c, :], o.y1[:, :])
                    last.then_inc(*pe_low.inc(s, "x1"))

                def gat_sum(s, o):
                    pe.wait_ge(*dve_low.at(s, it, "x1"))
                    for c in range(C):
                        last = mm(G[0:1, s, 1, 0:T], ones_c[:, :], o.x1[:, c, :], c == 0, c == C - 1)
                    last.then_inc(*pe_gat.inc(s, "sum"))

                def gat_self(s, o):
                    pe.wait_ge(*dve_gat.at(s, it, "zrow"))
                    pe.wait_ge(ld_q[s], it * 16 + 16)
                    for m in range(C):
                        for c in range(C):
                            mm(G[:, s, 0, m * T:(m + 1) * T], w("self", C)[:, c, m * P:(m + 1) * P], o.x1[:, c, :],
                               c == 0, False)
                        last = mm(G[:, s, 0, m * T:(m + 1) * T], o.qrow[:, m * P:(m + 1) * P], o.zrow[:, :], False, True)
                    last.then_inc(*pe_gat.inc(s, "self"))

                def gat_qk(s, o):
                    pe.wait_ge(*act_gat.at(s, it, "sf"))
                    wq, wk = w("gq", 2 * C), w("gk", 2 * C)
                    dense_f(G[:, s, 1, :], wq[:, 0:C, :], o.sf).then_inc(*pe_gat.inc(s, "q0"))
                    for d in range(2):
                        for m in range(C):
                            for c in range(C):
                                last = mm(G[:, s, 0, (d * C + m) * M:(d * C + m + 1) * M],
                                          wk[:, d * C + c, m * P:(m + 1) * P], o.sf[:, c, 0:M], c == 0, c == C - 1)
                    last.then_inc(*pe_gat.inc(s, "k"))

                def gat_qv(s, o):
                    pe.wait_ge(*dve_gat.at(s, it, "q0"))
                    dense_f(G[:, s, 1, :], w("gq", 2 * C)[:, C:2 * C, :], o.sf).then_inc(*pe_gat.inc(s, "q1"))
                    pe.wait_ge(*dve_gat.at(s, it, "kb"))
                    pe.wait_ge(*dve_gat.at(s, it, "sfrep"))
                    for c in range(C):
                        last = mm(G[0:4 * MP, s, 0, :], o.sfrep[:, c, :, :].rearrange("p a m -> p (a m)"),
                                  w("gv", C)[:, c, :], c == 0, c == C - 1)
                    last.then_inc(*pe_gat.inc(s, "v"))

                def gat_scores(s, o, t):
                    pe.wait_ge(*dve_gat.at(s, it, "vbd" if t == 0 else "m0"))
                    for d, q in enumerate((o.gq, o.gq1)):
                        for c in range(C):
                            last = mm(G[:, s, d, c * HC * M:(c + 1) * HC * M], q[:, c, t * P:(t + 1) * P],
                                      o.kbd[:, d * C + c, :, :].rearrange("p h m -> p (h m)"))
                    last.then_inc(*pe_gat.inc(s, f"s{t}"))

                def gat_turn(s, o, t):
                    pe.wait_ge(*pool_g.at(s, it, f"p{t}"))
                    pe.wait_ge(*(dve_gat.at(s, it, "m1") if t == 0 else act_gat.at(s, it, "t0")))
                    for g in range(8):
                        last = pe.transpose(G[0:4 * MP, s, g // 4, g % 4 * P:(g % 4 + 1) * P],
                                            o.P[:, t, 4 * g:4 * g + 4, :].rearrange("p h m -> p (h m)"), ident[:, :])
                    last.then_inc(*pe_gat.inc(s, f"t{t}"))

                def gat_values(s, o):
                    pe.wait_ge(*act_gat.at(s, it, "t1"))
                    for g in range(4):
                        a = g % 2 * 64
                        for d in range(2):
                            last = mm(G[a:a + 64, s, 0, g // 2 * T:(g // 2 + 1) * T], o.vbd[:, d * 4 + g, :],
                                      o.PT[0:4 * MP, d * 4 + g, :], d == 0, d == 1)
                    last.then_inc(*pe_gat.inc(s, "pv"))

                def mean(i, s, o, src, *ready):
                    for r in ready:
                        pe.wait_ge(*r)
                    for c in range(C):
                        last = mm(G[:, s, 1, 0:T], mean_w[:, :], src[:, c, :], c == 0, c == C - 1)
                    last.then_inc(*pe_ln[i].inc(s, "mean"))

                def var(i, s, o):
                    pe.wait_ge(*act_ln[i].at(s, it, "sq"))
                    for c in range(C):
                        last = mm(G[:, s, 0, 0:T], mean_w[:, :], o.sq[:, c, :], c == 0, c == C - 1)
                    last.then_inc(*pe_ln[i].inc(s, "var"))

                def att_qkv(s, o):
                    pe.wait_ge(*dve_ln[0].at(s, it, "xm"))
                    dense_f(G[:, s, 0, :], w("q2", C), o.xm).then_inc(*pe_att.inc(s, "q"))
                    dense_f(G[:, s, 1, :], w("k2", C), o.xm).then_inc(*pe_att.inc(s, "k"))

                def att_v(s, o):
                    pe.wait_ge(*dve_att.at(s, it, "q"))
                    dense_t(G[:, s, 0, :], w("v2", C), o.xm).then_inc(*pe_att.inc(s, "v"))

                def att_max(s, o):
                    pe.wait_ge(stacked[s], (it + 1) * 16 * 2 * len(SPLIT_Q))
                    for u in range(8):
                        if u >= 2:
                            pe.wait_ge(*dve_att.at(s, it, f"m{u - 2}"))
                        elif s:
                            pe.wait_ge(*dve_att.at(0, it, f"m{u + 6}"))
                        else:
                            pe.wait_ge(*act_att.past(1, it))
                        for k in range(2):
                            for t in range(TT):
                                h = 2 * u + k
                                last = mm(SS[:, u % 2, (k * TT + t) * T:(k * TT + t + 1) * T],
                                          o.st[0:KS, 0, h, t * P:(t + 1) * P], o.st[0:KS, 1, h, :])
                        last.then_inc(*pe_att.inc(s, f"m{u}"))

                def att_turn_max(s, o):
                    pe.wait_ge(*dve_att.at(s, it, "m7"))
                    for t in range(TT):
                        last = pe.transpose(G[0:H, s, 1, t * P:(t + 1) * P], o.mx2[:, t, :], ident[:, :])
                    last.then_inc(*pe_att.inc(s, "mx"))

                def att_exp(s, o):
                    pe.wait_ge(*dve_att.at(s, it, "lo"))
                    for u in range(8):
                        if u >= 2:
                            pe.wait_ge(*act_att.at(s, it, f"e{u - 2}"))
                        elif s:
                            pe.wait_ge(*act_att.at(0, it, f"e{u + 6}"))
                        else:
                            pe.wait_ge(*dve_att.at(1, it, f"m{u + 6}"))
                        for k in range(2):
                            for t in range(TT):
                                h = 2 * u + k
                                q = SS[:, u % 2, (k * TT + t) * T:(k * TT + t + 1) * T]
                                mm(q, o.st[0:KS, 1, h, t * P:(t + 1) * P], o.st[0:KS, 0, h, :], True, False)
                                last = mm(q, sel[:, h, :], o.nmx[:, :], False, True)
                        last.then_inc(*pe_att.inc(s, f"e{u}"))
                        if u % 2 and u > 1:
                            values(s, o, u // 2 - 1)
                    values(s, o, 3)

                def values(s, o, g):
                    pe.wait_ge(*act_att.at(s, it, f"e{2 * g + 1}"))
                    for t in range(TT):
                        for a in range(4):
                            u, k = (4 * g + a) // 2, a % 2
                            last = mm(G[32 * a:32 * a + 32, s, g // 2, g % 2 * T:(g % 2 + 1) * T],
                                      o.vp[:, t, 4 * g + a, :], probs[:, u % 4, k * TT + t, :], t == 0, t == TT - 1)
                    last.then_inc(*pe_att.inc(s, f"p{g}"))

                def att_turn(s, o):
                    pe.wait_ge(*act_att.at(s, it, "o"))
                    for t in range(TT):
                        for g in range(4):
                            last = pe.transpose(G[:, s, t, g * P:(g + 1) * P], o.oraw[:, g, t * P:(t + 1) * P], ident[:, :])
                    last.then_inc(*pe_att.inc(s, "ot"))

                def att_back(s, o):
                    pe.wait_ge(*dve_att.at(s, it, "yq"))
                    yq = o.yq.rearrange("p (t g) l -> p t (g l)", t=TT)
                    for c in range(C):
                        for t in range(TT):
                            last = pe.transpose(G[:, s, 0, c * T + t * P:c * T + (t + 1) * P],
                                                yq[:, t, c * P:(c + 1) * P], ident[:, :])
                    last.then_inc(*pe_att.inc(s, "yt"))

                def att_out(s, o):
                    pe.wait_ge(*act_att.at(s, it, "y"))
                    dense_f(G[:, s, 1, :], w("o2", C), o.yF).then_inc(*pe_att.inc(s, "o"))

                def mlp_up(s, o, i):
                    if i == 0:
                        pe.wait_ge(*dve_ln[1].at(s, it, "xm"))
                    if i >= 2:
                        pe.wait_ge(*act_mlp.at(s, it, f"h{i - 2}"))
                    dense_f(G[:, s, i % 2, :], w("w1", C)[:, :, i * 2 * P:(i + 1) * 2 * P], o.xm)\
                        .then_inc(*pe_mlp.inc(s, f"h{i}"))

                def mlp_down(s, o):
                    pe.wait_ge(*act_mlp.at(s, it, "h3"))
                    K = MLP // P
                    for m in range(C):
                        for k in range(K):
                            last = mm(G[:, s, 0, m * T:(m + 1) * T], w("w2", K)[:, k, m * P:(m + 1) * P], o.h[:, k, :],
                                      k == 0, k == K - 1)
                    last.then_inc(*pe_mlp.inc(s, "w2"))

                def lin_q(s, o):
                    pe.wait_ge(*dve_ln[2].at(s, it, "xm"))
                    dense_t(G[:, s, 0, :], w("q3", C), o.xm).then_inc(*pe_lin.inc(s, "q"))
                    dense_f(G[:, s, 1, :], w("k3", C), o.xm).then_inc(*pe_lin.inc(s, "k"))

                def lin_v(s, o):
                    pe.wait_ge(*dve_lin.at(s, it, "q"))
                    dense_t(G[:, s, 0, :], w("v3", C), o.xm).then_inc(*pe_lin.inc(s, "v"))

                def lin_turn(s, o):
                    pe.wait_ge(*dve_lin.at(s, it, "p"))
                    for c in range(C):
                        for t in range(TT):
                            last = pe.transpose(G[:, s, 1, c * T + t * P:c * T + (t + 1) * P],
                                                o.q3[:, t, c * P:(c + 1) * P], ident[:, :])
                    last.then_inc(*pe_lin.inc(s, "qT"))
                    pe.wait_ge(*act_lin.at(s, it, "ek"))
                    for t in range(TT):
                        for c in range(C):
                            last = pe.transpose(G[:, s, 0, t * D + c * P:t * D + (c + 1) * P],
                                                o.ke[:, c, t * P:(t + 1) * P], ident[:, :])
                    last.then_inc(*pe_lin.inc(s, "kT"))

                def lin_ctx(s, o):
                    pe.wait_ge(*act_lin.at(s, it, "kT"))
                    for c in range(C):
                        for t in range(TT):
                            last = mm(G[:, s, 1, c * P:(c + 1) * P], o.kT[:, t, c * P:(c + 1) * P],
                                      o.vt[:, t, c * P:(c + 1) * P], t == 0, t == TT - 1)
                    last.then_inc(*pe_lin.inc(s, "ctx"))

                def lin_y(s, o):
                    pe.wait_ge(*dve_lin.at(s, it, "ctx"))
                    for c in range(C):
                        last = mm(G[:, s, 0, c * T:(c + 1) * T], o.ctx[:, c, :], o.q3s[:, c, :])
                    last.then_inc(*pe_lin.inc(s, "y"))

                def lin_out(s, o):
                    pe.wait_ge(*dve_lin.at(s, it, "s"))
                    dense_f(G[:, s, 1, :], w("o3", C), o.sq).then_inc(*pe_lin.inc(s, "o"))

                def each(f, *a):
                    for s, o in enumerate(SL):
                        f(s, o, *a)

                each(low_1)
                each(low_2)
                each(low_3)
                each(low_4)
                each(gat_sum)
                each(gat_self)
                each(gat_qk)
                each(gat_qv)
                each(gat_scores, 0)
                each(gat_scores, 1)
                each(gat_turn, 0)
                each(gat_turn, 1)
                each(gat_values)
                for s, o in enumerate(SL):
                    mean(0, s, o, o.x2, dve_gat.at(s, it, "x2"))
                for s, o in enumerate(SL):
                    var(0, s, o)
                each(att_qkv)
                each(att_v)
                each(att_max)
                each(att_turn_max)
                each(att_exp)
                each(att_turn)
                each(att_back)
                each(att_out)
                for s, o in enumerate(SL):
                    mean(1, s, o, o.x1, dve_att.at(s, it, "x3"))
                for s, o in enumerate(SL):
                    var(1, s, o)
                for i in range(4):
                    each(mlp_up, i)
                each(mlp_down)
                for s, o in enumerate(SL):
                    mean(2, s, o, o.x2, dve_mlp.at(s, it, "x4"))
                for s, o in enumerate(SL):
                    var(2, s, o)
                each(lin_q)
                each(lin_v)
                each(lin_turn)
                each(lin_ctx)
                each(lin_y)
                for s, o in enumerate(SL):
                    mean(3, s, o, o.yF, act_lin.at(s, it, "y"))
                for s, o in enumerate(SL):
                    var(3, s, o)
                each(lin_out)

        @block.scalar
        def _(act):
            for p in (act_low, act_gat, *act_ln, act_att, act_mlp, act_lin):
                p.begin(act)
            for s in range(SLOTS):
                act.sem_inc(stored[s], 16)
            half = W_COLS["q2"][0]
            act.dma_start(W[:, 0:half], w_in[:, 0:half]).then_inc(ld_w, 16)
            act.dma_start(W[:, half:], w_in[:, half:]).then_inc(ld_w, 16)
            act.wait_ge(const_done, N_CONST)
            act.wait_ge(pre_dve, 1)
            act.activation(cstat[:, 8:9], cstat[:, 7:8], ACT.Ln, bias=eps_c[0:B, :]).then_inc(pre_act, 1)
            act.wait_ge(pre_act, 1)
            act.activation(cstat[:, 9:10], cstat[:, 8:9], ACT.Exp, scale=-0.5).then_inc(pre_act, 1)
            A1, A2 = SS[:, 0, 512:1024], SS[:, 1, 0:512]
            act.wait_ge(pre_pe, 3)
            act.activation(hT[:, 0, 0:B], A1[:, 0:B], ACT.Gelu, bias=vec("b1")[:, 0:1])
            act.activation(hT[:, 1, 0:B], A1[:, B:2 * B], ACT.Gelu, bias=vec("b1")[:, 1:2]).then_inc(pre_act, 1)
            for p in range(4):
                act.wait_ge(pre_pe, 4 + 2 * p)
                if p:
                    act.wait_ge(pre_pe, 3 + 2 * p)
                act.activation(wsb[:, :], A2, ACT.Copy).then_inc(pre_act, 1)
            act.activation(sil2[:, :], vec("cond"), ACT.Exp, scale=-1.0).then_inc(pre_act, 1)
            with act.Fori(0, B // SLOTS) as it:
                def low_gelu(s, o):
                    act.wait_ge(*pe_low.at(s, it, "y2"))
                    act.activation(o.xm[:, :, :].rearrange("p c t -> p (c t)"), G[:, s, 0, :], ACT.Gelu)\
                        .then_inc(*act_low.inc(s, "g"))

                def gat_self(s, o):
                    act.wait_ge(*pe_gat.at(s, it, "self"))
                    for m in range(C):
                        last = act.activation(o.sf[:, m, :], G[:, s, 0, m * T:(m + 1) * T], ACT.Identity,
                                              bias=vec("bself")[:, m:m + 1])
                    last.then_inc(*act_gat.inc(s, "sf"))

                def gat_exp(s, o, t):
                    act.wait_ge(*dve_gat.at(s, it, f"d{t}"))
                    act.activation(o.P[:, t, :, 0:M], o.S, ACT.Exp).then_inc(*act_gat.inc(s, f"e{t}"))

                def gat_turned(s, o, t):
                    act.wait_ge(*pe_gat.at(s, it, f"t{t}"))
                    act.activation(o.PT[0:4 * MP, :, t * P:(t + 1) * P],
                                   G[0:4 * MP, s, :, :].rearrange("p a (g n) -> p (a g) n", n=P), ACT.Copy)\
                        .then_inc(*act_gat.inc(s, f"t{t}"))

                def square(i, s, o):
                    act.wait_ge(*dve_ln[i].at(s, it, "xc"))
                    act.activation(o.sq[:, :, :], o.xc[:, :, :], ACT.Square).then_inc(*act_ln[i].inc(s, "sq"))

                def rstd(i, s, o):
                    act.wait_ge(*pe_ln[i].at(s, it, "var"))
                    act.activation(o.rstd[:, :], G[:, s, 0, 0:T], ACT.Ln, bias=eps_c[:, :])\
                        .then_inc(*act_ln[i].inc(s, "ln"))
                    act.wait_ge(*act_ln[i].at(s, it, "ln"))
                    act.activation(o.rstd[:, :], o.rstd[:, :], ACT.Exp, scale=-0.5).then_inc(*act_ln[i].inc(s, "rstd"))

                def att_split(s, o):
                    act.wait_ge(*dve_att.at(s, it, "k"))
                    act.activation(o.part[:, 0], o.qk, ACT.Copy).then_inc(*act_att.inc(s, "c1"))
                    act.wait_ge(*dve_att.at(s, it, "r1"))
                    act.activation(o.part[:, 1], o.rest, ACT.Copy).then_inc(*act_att.inc(s, "c2"))

                def att_exp(s, o):
                    for u in range(8):
                        act.wait_ge(*pe_att.at(s, it, f"e{u}"))
                        if u >= 4:
                            act.wait_ge(*pe_att.at(s, it, f"p{(u - 4) // 2}"))
                        elif s:
                            act.wait_ge(*pe_att.at(0, it, f"p{u // 2 + 2}"))
                        else:
                            act.wait_ge(*pe_att.past(1, it))
                        act.activation(probs[:, u % 4, :, :].rearrange("p a t -> p (a t)"), SS[:, u % 2, :], ACT.Exp)\
                            .then_inc(*act_att.inc(s, f"e{u}"))

                def att_o(s, o):
                    act.wait_ge(*pe_att.at(s, it, "p3"))
                    act.activation(o.oraw.rearrange("p g t -> p (g t)"),
                                   G[:, s, :, :].rearrange("p a n -> p (a n)"), ACT.Copy)\
                        .then_inc(*act_att.inc(s, "o"))

                def att_y(s, o):
                    act.wait_ge(*pe_att.at(s, it, "yt"))
                    act.activation(o.yF[:, :, :].rearrange("p c t -> p (c t)"), G[:, s, 0, :], ACT.Copy)\
                        .then_inc(*act_att.inc(s, "y"))

                def mlp_gelu(s, o, i):
                    act.wait_ge(*pe_mlp.at(s, it, f"h{i}"))
                    for k in range(2):
                        m = 2 * i + k
                        last = act.activation(o.h[:, m, :], G[:, s, i % 2, k * T:(k + 1) * T], ACT.Gelu,
                                              bias=vec("mb1")[:, m:m + 1])
                    last.then_inc(*act_mlp.inc(s, f"h{i}"))

                def lin_exp(s, o):
                    act.wait_ge(*dve_lin.at(s, it, "d"))
                    act.activation(o.q3, o.q3, ACT.Exp).then_inc(*act_lin.inc(s, "eq"))
                    act.wait_ge(*dve_lin.at(s, it, "nk"))
                    for c in range(C):
                        last = act.activation(o.ke[:, c, :], o.kf[:, c, :], ACT.Exp, bias=o.nk[:, c:c + 1],
                                              accum_out=o.ks[:, c:c + 1])
                    last.then_inc(*act_lin.inc(s, "ek"))

                def lin_turned(s, o):
                    act.wait_ge(*pe_lin.at(s, it, "qT"))
                    act.activation(o.q3s.rearrange("p c t -> p (c t)"), G[:, s, 1, :], ACT.Copy)\
                        .then_inc(*act_lin.inc(s, "qT"))
                    act.wait_ge(*pe_lin.at(s, it, "kT"))
                    act.activation(o.kT.rearrange("p t c -> p (t c)"), G[:, s, 0, :], ACT.Copy)\
                        .then_inc(*act_lin.inc(s, "kT"))

                def lin_y(s, o):
                    act.wait_ge(*pe_lin.at(s, it, "y"))
                    act.activation(o.yF[:, :, :].rearrange("p c t -> p (c t)"), G[:, s, 0, :], ACT.Copy)\
                        .then_inc(*act_lin.inc(s, "y"))

                def lin_tanh(s, o):
                    act.wait_ge(*dve_ln[3].at(s, it, "xm"))
                    act.activation(o.sq[:, :, :], o.xm[:, :, :], ACT.Tanh).then_inc(*act_lin.inc(s, "tanh"))

                def store(s, o):
                    act.wait_ge(*dve_lin.at(s, it, "out"))
                    act.dma_start(out[bass.ds(it * SLOTS + s, 1)].rearrange("o p c t -> p (o c) t"), o.xc[:, :, :])\
                        .then_inc(stored[s], 16)

                def each(f, *a):
                    for s, o in enumerate(SL):
                        f(s, o, *a)

                def norm(i):
                    for s, o in enumerate(SL):
                        square(i, s, o)
                    for s, o in enumerate(SL):
                        rstd(i, s, o)

                each(low_gelu)
                each(gat_self)
                each(gat_exp, 0)
                each(gat_exp, 1)
                each(gat_turned, 0)
                each(gat_turned, 1)
                norm(0)
                each(att_split)
                each(att_exp)
                each(att_o)
                each(att_y)
                norm(1)
                for i in range(4):
                    each(mlp_gelu, i)
                norm(2)
                each(lin_exp)
                each(lin_turned)
                each(lin_y)
                norm(3)
                each(lin_tanh)
                each(store)

        @block.vector
        def _(dve):
            for p in (dve_low, dve_gat, *dve_ln, dve_att, dve_mlp, dve_lin):
                p.begin(dve)
            A0, A1, A3 = SS[:, 0, 0:512], SS[:, 0, 512:1024], SS[:, 1, 512:1024]
            n = 0

            def done(ins):
                nonlocal n
                n += 1
                ins.then_inc(pre_dve, 1)

            dve.wait_ge(ld_small, 48)
            stat = sem("stat")
            dve.bn_stats(cstat[:, 0:6], ct[:, :]).then_inc(stat, 1)
            dve.wait_ge(stat, 1)
            done(dve.bn_aggr(cstat[:, 6:8], cstat[:, 0:6]))
            dve.wait_ge(pre_act, 2)
            dve.wait_ge(pre_dve, 1)
            done(dve.tensor_scalar(ct[:, :], ct[:, :], cstat[:, 6:7], cstat[:, 9:10], ALU.subtract, ALU.mult))
            dve.wait_ge(pre_pe, 2)
            for c in range(C):
                done(dve.tensor_scalar(cT[:, c, :], A0[:, c * B:(c + 1) * B], vec("ln_g")[:, c:c + 1],
                                       vec("ln_b")[:, c:c + 1], ALU.mult, ALU.add))
            dve.wait_ge(pre_pe, 1)
            dve.tensor_tensor(vec("gbout")[:, 0:C], vec("gbout")[:, 0:C], vec("gbout")[:, C:2 * C], ALU.add)\
                .then_inc(stat, 1)
            done(dve.tensor_copy(ct[:, :], A3[0:B, 0:D]))
            done(dve.tensor_copy(par_all[:, :, GATE:GATE + C].rearrange("p b c -> p c b"),
                                 vec("cond").rearrange("p (c b) -> p c b", c=C)))
            for p in range(4):
                dve.wait_ge(pre_pe, 5 + 2 * p)
                lo = p * C * RANK
                done(dve.tensor_tensor(
                    par_all[:, :, lo:lo + 16].rearrange("p b (a j) -> p j a b", j=4),
                    A0.rearrange("p (j a b) -> p j a b", j=4, a=4)[:, :, :, 0:B],
                    vec("b2")[:, lo:lo + 16].rearrange("p (a j) -> p j a", j=4).unsqueeze(3).to_broadcast([P, 4, 4, B]),
                    ALU.add))
            dve.wait_ge(pre_act, 8)
            done(dve.tensor_scalar(sil2[:, :], sil2[:, :], 1.0, None, ALU.add))
            dve.wait_ge(pre_dve, 11)
            done(dve.reciprocal(sil2[:, :], sil2[:, :]))
            dve.wait_ge(pre_dve, 12)
            done(dve.tensor_tensor(sil[:, :], sil2[:, :], vec("cond"), ALU.mult))
            dve.wait_ge(pre_pe, 12)
            mods = A1[:, 0:6 * C * B].rearrange("p (k b) -> p k b", b=B)
            emb = A1[:, 6 * C * B:8 * C * B].rearrange("p (k b) -> p k b", b=B)
            dve.tensor_tensor(par_all[:, :, MOD:AFF].rearrange("p b k -> p k b"), mods,
                              vec("bc").unsqueeze(2).to_broadcast([P, 6 * C, B]), ALU.add).then_inc(stat, 1)
            dve.tensor_tensor(e1[:, :, :], emb, vec("embb").unsqueeze(2).to_broadcast([P, 2 * C, B]), ALU.add)\
                .then_inc(stat, 1)
            dve.wait_ge(stat, 4)
            for k in (1, 4):
                q = par_all[:, :, MOD + k * C:MOD + (k + 1) * C]
                dve.tensor_scalar(q, q, 1.0, None, ALU.add).then_inc(stat, 1)
            dve.tensor_scalar(e1[:, 0:C, :], e1[:, 0:C, :], 1.0, 0.5, ALU.add, ALU.mult).then_inc(stat, 1)
            dve.tensor_scalar(e1[:, C:2 * C, :], e1[:, C:2 * C, :], 0.5, None, ALU.mult).then_inc(stat, 1)
            dve.wait_ge(stat, 8)
            for c in range(C):
                done(dve.tensor_scalar(par_all[:, :, AFF + c], e1[:, c, :], vec("sng")[:, c:c + 1], None, ALU.mult))
                done(dve.scalar_tensor_tensor(out=par_all[:, :, AFF + C + c], in0=e1[:, c, :],
                                              scalar=vec("snb")[:, c:c + 1], in1=e1[:, C + c, :],
                                              op0=ALU.mult, op1=ALU.add))
            dve.wait_ge(const_done, N_CONST)
            assert n == 17
            with dve.Fori(0, B // SLOTS) as it:
                def low_1(s, o):
                    dve.wait_ge(*pe_low.at(s, it, "bb"))
                    dve.tensor_copy(o.bbT[0:RANK, :, :, :].rearrange("p f c n -> p (f c n)"), G[0:RANK, s, 1, :])\
                        .then_inc(*dve_low.inc(s, "bb"))
                    dve.wait_ge(*pe_low.at(s, it, "y1"))
                    dve.tensor_copy(o.y1[0:RANK, :], G[0:RANK, s, 0, 0:T]).then_inc(*dve_low.inc(s, "y1"))

                def low_3(s, o):
                    dve.wait_ge(*pe_low.at(s, it, "z"))
                    dve.tensor_copy(o.y1[0:RANK, :], G[0:RANK, s, 1, 0:T]).then_inc(*dve_low.inc(s, "z"))

                def low_4(s, o):
                    dve.wait_ge(*pe_low.at(s, it, "x1"))
                    dve.tensor_tensor(o.x1[:, :, :], G[:, s, 0, :].rearrange("p (c t) -> p c t", c=C), o.x[:, :, :],
                                      ALU.add).then_inc(*dve_low.inc(s, "x1"))

                def gat_adj(s, o):
                    dve.wait_ge(ld_adj[s], it * 16 + 16)
                    adj = o.adj.rearrange("p t (m l) -> p (t m) l", l=NL)
                    adjw = o.adjw.rearrange("p t (m l) -> p (t m) l", l=NL)
                    flat = [x[:, :, :].rearrange("p t m -> p (t m)") for x in (o.cond, o.mask, o.bias)]
                    dve.tensor_reduce(flat[0], adj, AX, ALU.add).then_inc(*dve_gat.inc(s, "cond"))
                    dve.tensor_tensor(adjw, adj, row("wl").unsqueeze(1).to_broadcast([P, TT * 2 * M, NL]), ALU.mult)\
                        .then_inc(*dve_gat.inc(s, "adjw"))
                    dve.wait_ge(*dve_gat.at(s, it, "adjw"))
                    dve.tensor_reduce(flat[2], adjw, AX, ALU.add).then_inc(*dve_gat.inc(s, "vb"))
                    dve.tensor_scalar(flat[1], flat[0], 0.0, None, ALU.is_gt).then_inc(*dve_gat.inc(s, "mask"))
                    dve.wait_ge(*dve_gat.at(s, it, "mask"))
                    dve.tensor_scalar(flat[0], flat[1], -NEG, NEG, ALU.mult, ALU.add).then_inc(*dve_gat.inc(s, "neg"))
                    dve.wait_ge(*dve_gat.at(s, it, "neg"))
                    dve.scalar_tensor_tensor(out=flat[2], in0=flat[2], scalar=row("bb"), in1=flat[0],
                                             op0=ALU.add, op1=ALU.add).then_inc(*dve_gat.inc(s, "bias"))

                def gat_zrow(s, o):
                    dve.wait_ge(*pe_gat.at(s, it, "sum"))
                    dve.tensor_scalar(o.zrow[0:1, :], G[0:1, s, 1, 0:T], 0.0, None, ALU.not_equal)\
                        .then_inc(*dve_gat.inc(s, "zrow"))

                def gat_query(s, o, d, q):
                    dve.wait_ge(*pe_gat.at(s, it, f"q{d}"))
                    for m in range(C):
                        k = d * C + m
                        last = dve.tensor_scalar(q[:, m, :], G[:, s, 1, m * T:(m + 1) * T], vec("gbq")[:, k:k + 1],
                                                 float(DH) ** -0.5, ALU.add, ALU.mult)
                    last.then_inc(*dve_gat.inc(s, f"q{d}"))

                def gat_self(s, o):
                    dve.wait_ge(*act_gat.at(s, it, "sf"))
                    dve.tensor_copy(o.sfrep[:, :, :, 0:M], o.sf[:, :, 0:M].unsqueeze(2).to_broadcast([P, C, 4, M]))\
                        .then_inc(*dve_gat.inc(s, "sfrep"))

                def gat_keys(s, o):
                    gat_query(s, o, 0, o.gq)
                    dve.wait_ge(*pe_gat.at(s, it, "k"))
                    dve.tensor_tensor(o.kb[:, :, :], G[:, s, 0, 0:2 * C * M].rearrange("p (g m) -> p g m", m=M),
                                      vec("gbk").unsqueeze(2).to_broadcast([P, 2 * C, M]), ALU.add)\
                        .then_inc(*dve_gat.inc(s, "kb"))
                    dve.wait_ge(*dve_gat.at(s, it, "kb"))
                    dve.tensor_tensor(o.kbd, o.kb[:, :, :].unsqueeze(2).to_broadcast([P, 2 * C, HC, M]),
                                      blk16[:, :, 0].unsqueeze(1).unsqueeze(3).to_broadcast([P, 2 * C, HC, M]),
                                      ALU.mult).then_inc(*dve_gat.inc(s, "kbd"))

                def gat_vals(s, o):
                    gat_query(s, o, 1, o.gq1)
                    dve.wait_ge(*pe_gat.at(s, it, "v"))
                    dve.tensor_tensor(o.vbd, G[0:4 * MP, s, 0, :].rearrange("p (g n) -> p g n", g=8),
                                      blk24[:, :, :].rearrange("p a l -> p (a l)").unsqueeze(1)
                                      .to_broadcast([4 * MP, 8, 4 * DH]), ALU.mult).then_inc(*dve_gat.inc(s, "vbd"))

                def gat_soft(s, o, t):
                    dve.wait_ge(*pe_gat.at(s, it, f"s{t}"))
                    S = o.S.rearrange("p (d h) m -> p d h m", d=2)

                    def heads(x):
                        return x[:, t, :].rearrange("p (d m) -> p d m", d=2).unsqueeze(2).to_broadcast([P, 2, H, M])

                    if t:
                        dve.wait_ge(*act_gat.at(s, it, "e0"))
                    dve.tensor_tensor(S, G[:, s, :, 0:H * M].rearrange("p d (h m) -> p d h m", m=M), heads(o.mask),
                                      ALU.mult).then_inc(*dve_gat.inc(s, f"m{t}"))
                    dve.wait_ge(*dve_gat.at(s, it, f"m{t}"))
                    dve.tensor_tensor(S, S, heads(o.bias), ALU.add).then_inc(*dve_gat.inc(s, f"a{t}"))
                    dve.wait_ge(*dve_gat.at(s, it, f"a{t}"))
                    dve.tensor_reduce(o.mx[:, :], o.S, AX, ALU.max).then_inc(*dve_gat.inc(s, f"x{t}"))
                    dve.wait_ge(*dve_gat.at(s, it, f"x{t}"))
                    dve.tensor_tensor(o.S, o.S, o.mx[:, :].unsqueeze(2).to_broadcast([P, 2 * H, M]), ALU.subtract)\
                        .then_inc(*dve_gat.inc(s, f"d{t}"))

                def gat_sums(s, o, t):
                    dve.wait_ge(*act_gat.at(s, it, f"e{t}"))
                    dve.tensor_reduce(o.sm[:, :], o.P[:, t, :, 0:M], AX, ALU.add).then_inc(*dve_gat.inc(s, f"s{t}"))
                    dve.wait_ge(*dve_gat.at(s, it, f"s{t}"))
                    if t:
                        dve.wait_ge(*pool_g.at(s, it, "p0"))
                    dve.reciprocal(o.ri[:, :], o.sm[:, :]).then_inc(*dve_gat.inc(s, f"r{t}"))

                def gat_out(s, o):
                    dve.wait_ge(*pe_gat.at(s, it, "pv"))
                    for c in range(C):
                        dve.scalar_tensor_tensor(out=o.xc[:, c, :], in0=G[:, s, 0, c * T:(c + 1) * T],
                                                 scalar=vec("gbout")[:, c:c + 1], in1=o.sf[:, c, :],
                                                 op0=ALU.add, op1=ALU.add).then_inc(*dve_gat.inc(s, f"o{c}"))
                    dve.wait_ge(*dve_gat.at(s, it, "o1"))
                    dve.scalar_tensor_tensor(out=o.x2[:, :, :], in0=o.xc[:, :, :], scalar=0.0, in1=o.x1[:, :, :],
                                             op0=ALU.max, op1=ALU.add).then_inc(*dve_gat.inc(s, "x2"))

                def centre(i, s, o, src):
                    dve.wait_ge(*pe_ln[i].at(s, it, "mean"))
                    dve.tensor_tensor(o.xc[:, :, :], src[:, :, :], G[:, s, 1, 0:T].unsqueeze(1).to_broadcast([P, C, T]),
                                      ALU.subtract).then_inc(*dve_ln[i].inc(s, "xc"))

                def scale(i, s, o, gain, shift):
                    dve.wait_ge(*act_ln[i].at(s, it, "rstd"))
                    dve.tensor_tensor(o.xc[:, :, :], o.xc[:, :, :], o.rstd[:, :].unsqueeze(1).to_broadcast([P, C, T]),
                                      ALU.mult).then_inc(*dve_ln[i].inc(s, "xn"))
                    dve.wait_ge(*dve_ln[i].at(s, it, "xn"))
                    for c in range(C):
                        last = dve.tensor_scalar(o.xm[:, c, :], o.xc[:, c, :], gain[:, c:c + 1], shift[:, c:c + 1],
                                                 ALU.mult, ALU.add)
                    last.then_inc(*dve_ln[i].inc(s, "xm"))

                def mod(o, k):
                    return o.par[:, k * C:(k + 1) * C]

                def att_qk(s, o):
                    for k, (name, b) in enumerate((("q", "bq2"), ("k", "bk2"))):
                        dve.wait_ge(*pe_att.at(s, it, name))
                        for c in range(C):
                            last = dve.tensor_scalar(o.qk[:, k, c, :], G[:, s, k, c * T:(c + 1) * T],
                                                     vec(b)[:, c:c + 1], 1.0 / DH if k == 0 else 1.0,
                                                     ALU.add, ALU.mult)
                        last.then_inc(*dve_att.inc(s, name))
                    dve.wait_ge(*act_att.at(s, it, "c1"))
                    dve.tensor_tensor(o.rest, o.qk, o.part[:, 0], ALU.subtract).then_inc(*dve_att.inc(s, "r1"))

                def att_third(s, o):
                    dve.wait_ge(*pe_att.at(s, it, "v"))
                    dve.tensor_tensor(o.vp[:, :, :, 0:DH], G[:, s, 0, :].rearrange("p (t h l) -> p t h l", t=TT, h=H),
                                      row("bv2").rearrange("p (h l) -> p h l", h=H).unsqueeze(1)
                                      .to_broadcast([P, TT, H, DH]), ALU.add).then_inc(*dve_att.inc(s, "vp"))
                    dve.wait_ge(*act_att.at(s, it, "c2"))
                    dve.tensor_tensor(o.part[:, 2], o.rest, o.part[:, 1], ALU.subtract).then_inc(*dve_att.inc(s, "c3"))

                def att_max(s, o):
                    for u in range(8):
                        dve.wait_ge(*pe_att.at(s, it, f"m{u}"))
                        dve.tensor_reduce(o.mx2[:, :, 2 * u:2 * u + 2].rearrange("p t k -> p k t"),
                                          SS[:, u % 2, :].rearrange("p (k t n) -> p k t n", k=2, t=TT), AX, ALU.max)\
                            .then_inc(*dve_att.inc(s, f"m{u}"))

                def att_negmax(s, o):
                    dve.wait_ge(*pe_att.at(s, it, "mx"))
                    dve.tensor_scalar(o.nmx[0:H, :], G[0:H, s, 1, 0:T], -1.0, None, ALU.mult)\
                        .then_inc(*dve_att.inc(s, "hi"))
                    dve.wait_ge(*dve_att.at(s, it, "hi"))
                    dve.scalar_tensor_tensor(out=o.nmx[32:32 + H, :], in0=G[0:H, s, 1, 0:T], scalar=-1.0,
                                             in1=o.nmx[0:H, :], op0=ALU.mult, op1=ALU.subtract)\
                        .then_inc(*dve_att.inc(s, "lo"))

                def att_norm(s, o):
                    dve.wait_ge(*pe_att.at(s, it, "ot"))
                    g = G[:, s, :, :].rearrange("p t (g n) -> p (t g) n", n=2 * DH)
                    dve.reciprocal(o.ri[:, :], g[:, :, DH]).then_inc(*dve_att.inc(s, "ri"))
                    dve.wait_ge(*dve_att.at(s, it, "ri"))
                    dve.tensor_tensor(o.yq, g[:, :, 0:DH], o.ri[:, :].unsqueeze(2).to_broadcast([P, 2 * H, DH]),
                                      ALU.mult).then_inc(*dve_att.inc(s, "yq"))

                def gated(s, o, sems, pe_done, names, bank, bias, k, src, dst):
                    dve.wait_ge(*pe_done)
                    for c in range(C):
                        last = dve.tensor_scalar(o.xc[:, c, :], G[:, s, bank, c * T:(c + 1) * T], vec(bias)[:, c:c + 1],
                                                 mod(o, k)[:, c:c + 1], ALU.add, ALU.mult)
                    last.then_inc(*sems.inc(s, names[0]))
                    dve.wait_ge(*sems.at(s, it, names[0]))
                    dve.tensor_tensor(dst[:, :, :], o.xc[:, :, :], src[:, :, :], ALU.add).then_inc(*sems.inc(s, names[1]))

                def lin_qk(s, o):
                    groups = o.q3.rearrange("p t (h l) -> p (t h) l", l=DH)
                    dve.wait_ge(*pe_lin.at(s, it, "q"))
                    dve.tensor_tensor(o.q3, G[:, s, 0, :].rearrange("p (t n) -> p t n", t=TT),
                                      row("bq3").unsqueeze(1).to_broadcast([P, TT, D]), ALU.add)\
                        .then_inc(*dve_lin.inc(s, "q"))
                    dve.wait_ge(*dve_lin.at(s, it, "q"))
                    dve.tensor_reduce(o.mx[:, :], groups, AX, ALU.max).then_inc(*dve_lin.inc(s, "mx"))
                    dve.wait_ge(*dve_lin.at(s, it, "mx"))
                    dve.tensor_tensor(groups, groups, o.mx[:, :].unsqueeze(2).to_broadcast([P, 2 * H, DH]),
                                      ALU.subtract).then_inc(*dve_lin.inc(s, "d"))
                    dve.wait_ge(*pe_lin.at(s, it, "k"))
                    for c in range(C):
                        last = dve.tensor_scalar(o.kf[:, c, :], G[:, s, 1, c * T:(c + 1) * T], vec("bk3")[:, c:c + 1],
                                                 None, ALU.add)
                    last.then_inc(*dve_lin.inc(s, "k"))
                    dve.wait_ge(*dve_lin.at(s, it, "k"))
                    dve.tensor_reduce(o.nk[:, :], o.kf, AX, ALU.max, negate=True).then_inc(*dve_lin.inc(s, "nk"))

                def lin_vq(s, o):
                    groups = o.q3.rearrange("p t (h l) -> p (t h) l", l=DH)
                    dve.wait_ge(*pe_lin.at(s, it, "v"))
                    dve.tensor_tensor(o.vt, G[:, s, 0, :].rearrange("p (t n) -> p t n", t=TT),
                                      row("bv3").unsqueeze(1).to_broadcast([P, TT, D]), ALU.add)\
                        .then_inc(*dve_lin.inc(s, "v"))
                    dve.wait_ge(*act_lin.at(s, it, "eq"))
                    dve.tensor_reduce(o.sm[:, :], groups, AX, ALU.add).then_inc(*dve_lin.inc(s, "sm"))
                    dve.wait_ge(*dve_lin.at(s, it, "sm"))
                    dve.reciprocal(o.ri[:, :], o.sm[:, :]).then_inc(*dve_lin.inc(s, "ri"))
                    dve.wait_ge(*dve_lin.at(s, it, "ri"))
                    dve.tensor_tensor(groups, groups, o.ri[:, :].unsqueeze(2).to_broadcast([P, 2 * H, DH]),
                                      ALU.mult).then_inc(*dve_lin.inc(s, "p"))
                    dve.wait_ge(*act_lin.at(s, it, "ek"))
                    dve.reciprocal(o.nk[:, :], o.ks[:, :]).then_inc(*dve_lin.inc(s, "rk"))

                def lin_ctx(s, o):
                    dve.wait_ge(*pe_lin.at(s, it, "ctx"))
                    dve.wait_ge(*dve_lin.at(s, it, "rk"))
                    for c in range(C):
                        last = dve.scalar_tensor_tensor(out=o.ctx[:, c, :], in0=G[:, s, 1, c * P:(c + 1) * P],
                                                        scalar=o.nk[:, c:c + 1],
                                                        in1=blk16[:, :, :].rearrange("p h l -> p (h l)"),
                                                        op0=ALU.mult, op1=ALU.mult)
                    last.then_inc(*dve_lin.inc(s, "ctx"))

                def lin_silu(s, o):
                    dve.wait_ge(*act_lin.at(s, it, "tanh"))
                    dve.scalar_tensor_tensor(out=o.sq[:, :, :], in0=o.sq[:, :, :], scalar=1.0, in1=o.xm[:, :, :],
                                             op0=ALU.add, op1=ALU.mult).then_inc(*dve_lin.inc(s, "s"))

                def lin_out(s, o):
                    dve.wait_ge(*pe_lin.at(s, it, "o"))
                    for c in range(C):
                        last = dve.tensor_scalar(o.xc[:, c, :], G[:, s, 1, c * T:(c + 1) * T], vec("ob3")[:, c:c + 1],
                                                 o.par[:, GATE - NLOW + c:GATE - NLOW + c + 1], ALU.add, ALU.mult)
                    last.then_inc(*dve_lin.inc(s, "t"))
                    dve.wait_ge(*dve_lin.at(s, it, "t"))
                    dve.tensor_tensor(o.xc[:, :, :], o.xc[:, :, :], o.x2[:, :, :], ALU.add)\
                        .then_inc(*dve_lin.inc(s, "out"))

                def each(f, *a):
                    for s, o in enumerate(SL):
                        f(s, o, *a)

                def norm(i, src, affine):
                    for s, o in enumerate(SL):
                        centre(i, s, o, src(o))
                    for s, o in enumerate(SL):
                        scale(i, s, o, *affine(o))

                each(low_1)
                each(gat_adj)
                each(low_3)
                each(low_4)
                each(gat_zrow)
                each(gat_self)
                each(gat_keys)
                each(gat_vals)
                each(gat_soft, 0)
                each(gat_sums, 0)
                each(gat_soft, 1)
                each(gat_sums, 1)
                for s, o in enumerate(SL):
                    dve.wait_ge(stored[s], it * 16 + 16)
                each(gat_out)
                for s in range(SLOTS):
                    dve.wait_ge(*pool_p.at(s, it, "par"))
                norm(0, lambda o: o.x2, lambda o: (mod(o, 1), mod(o, 0)))
                each(att_qk)
                each(att_third)
                each(att_max)
                each(att_negmax)
                each(att_norm)
                for s, o in enumerate(SL):
                    gated(s, o, dve_att, pe_att.at(s, it, "o"), ("t", "x3"), 1, "bo2", 2, o.x2, o.x1)
                norm(1, lambda o: o.x1, lambda o: (mod(o, 4), mod(o, 3)))
                for s, o in enumerate(SL):
                    gated(s, o, dve_mlp, pe_mlp.at(s, it, "w2"), ("t", "x4"), 0, "mb2", 5, o.x1, o.x2)
                norm(2, lambda o: o.x2, lambda o: (vec("n3g"), vec("n3b")))
                each(lin_qk)
                each(lin_vq)
                each(lin_ctx)
                norm(3, lambda o: o.yF, lambda o: (o.par[:, AFF - NLOW:AFF - NLOW + C],
                                                   o.par[:, AFF - NLOW + C:AFF - NLOW + 2 * C]))
                each(lin_silu)
                each(lin_out)


def kernel(**inputs):
    import numpy as np
    import concourse.bacc as bacc
    from concourse.bass_utils import run_bass_kernel_spmd

    x = {k: np.asarray(v) for k, v in inputs.items()}

    def rows(a):
        a = np.asarray(a)
        return a.reshape(-1, P, a.shape[1]).transpose(1, 0, 2).reshape(P, -1)

    def cols(v):
        return np.asarray(v).reshape(-1, P).T

    L1, L2, L3 = "L1_cond_", "L2_cond_", "L3_cond_"
    w_self = x[L1 + "W_self"].T
    packs = {
        "self": rows(w_self[:D]),
        "gq": np.concatenate([rows(m.T) for m in x[L1 + "Wq"]], axis=1),
        "gk": np.concatenate([rows(m.T) for m in x[L1 + "Wk"]], axis=1),
        "gv": rows(x[L1 + "Wout"].transpose(3, 0, 1, 2).reshape(D, 2 * D)),
        "q2": rows(x[L2 + "Wq"]), "k2": rows(x[L2 + "Wk"]), "v2": rows(x[L2 + "Wv"]), "o2": rows(x[L2 + "Wo"]),
        "w1": rows(x[L2 + "W1"]), "w2": rows(x[L2 + "W2"]),
        "q3": rows(x[L3 + "Wq"]), "k3": rows(x[L3 + "Wk"]), "v3": rows(x[L3 + "Wv"]), "o3": rows(x[L3 + "out_W"]),
    }
    w_pack = np.concatenate([packs[k] for k in W_COLS], axis=1)
    vecs = {
        "ln_g": cols(x["L0_cond_ln_g"]), "ln_b": cols(x["L0_cond_ln_b"]), "b1": cols(x["L0_cond_b1"]),
        "b2": x["L0_cond_b2"].reshape(4, C, P, RANK).transpose(2, 0, 1, 3).reshape(P, 64),
        "bself": cols(x[L1 + "b_self"]), "gbq": cols(x[L1 + "bq"].reshape(-1)), "gbk": cols(x[L1 + "bk"].reshape(-1)),
        "gbout": cols(x[L1 + "bout"].reshape(-1)), "bc": cols(x[L2 + "bc"]), "bq2": cols(x[L2 + "bq"]),
        "bk2": cols(x[L2 + "bk"]), "bo2": cols(x[L2 + "bo"]), "mb1": cols(x[L2 + "b1"]), "mb2": cols(x[L2 + "b2"]),
        "n3g": cols(x[L3 + "norm_g"]), "n3b": cols(x[L3 + "norm_b"]), "bk3": cols(x[L3 + "bk"]),
        "embb": cols(x[L3 + "emb_b"]), "sng": cols(x[L3 + "sn_g"]), "snb": cols(x[L3 + "sn_b"]),
        "ob3": cols(x[L3 + "out_b"]),
        "cond": x["cond_1024"].T.reshape(C, P, B).transpose(1, 0, 2).reshape(P, C * B),
    }
    v_pack = np.concatenate([vecs[k] for k in V_COLS], axis=1)
    r_pack = np.concatenate([x[L2 + "bv"], x[L3 + "bq"], x[L3 + "bv"], x[L1 + "w_bias"],
                             x[L1 + "b_bias"].reshape(1)])[None, :]
    s_pack = np.concatenate([rows(w_self[D:]), rows(x["L0_cond_W1"]), rows(x[L2 + "Wc"]), rows(x[L3 + "emb_W"])], axis=1)
    low = x["L0_cond_W2"].reshape(C, P, 4, C, P, RANK).transpose(2, 1, 0, 3, 5, 4).reshape(4, P, C, 2048)
    adj = x["mask_BxSxSx11_ik0"]
    adj = np.stack([adj[:, :, :M], adj[:, :M].transpose(0, 2, 1, 3)], axis=2).reshape(B, T, 2 * M * NL)
    x_f = x["x"].transpose(0, 2, 1).reshape(B, C, P, T).transpose(0, 2, 1, 3)

    nc = bacc.Bacc("TRN2", target_bir_lowering=False, num_devices=1)
    arrays, args = {}, []
    for name, a in (("x", x_f), ("cond", x["cond_1024"]), ("adj", adj), ("w", w_pack), ("v", v_pack), ("r", r_pack),
                    ("s", s_pack), ("low", low)):
        arrays[f"in_{name}"] = np.ascontiguousarray(a)
        args.append(nc.dram_tensor(f"in_{name}", list(a.shape), mybir.dt.from_np(a.dtype), kind="ExternalInput").ap())
    args.append(nc.dram_tensor("out_x", [B, P, C, T], F32, kind="ExternalOutput").ap())
    build(nc, *args)
    r = run_bass_kernel_spmd(nc, [arrays], core_ids=[0])
    y = r.results[0]["out_x"]
    return y.transpose(0, 3, 2, 1).reshape(B, T, D)
```

```python
from contextlib import ExitStack

import concourse.bass as bass
from concourse import mybir

F32 = mybir.dt.float32
BF16 = mybir.dt.bfloat16
I32 = mybir.dt.int32
ALU = mybir.AluOpType
ACT = mybir.ActivationFunctionType
AX = mybir.AxisListType.X

B, T, D = 16, 256, 256
P = 128
C = D // P
TT = T // P
H = 16
DH = D // H
HC = P // DH
RANK = 8
M = 20
MP = 24
NL = 11
MLP = 4 * D
EPS = 1e-5
NEG = -9000000000000000.0
SLOTS = 2
PAIRS = B // SLOTS
SPLIT_Q = (0, 0, 0, 1, 1, 2)
SPLIT_K = (0, 1, 2, 0, 1, 0)
SPLIT_RUNS = ((0, 3), (3, 2), (5, 1))
KS = DH * len(SPLIT_Q)
KM = KS + 2
N_STACK = 2 * len(SPLIT_RUNS) + 1

ORDER = '''
A:m0 L:ly F:load A:m1 L:n3a A:m2 A:m3 L:n3b A:gelu A:m4 A:m5 L:tanh A:m6 A:m7 L:lo A:mx F:par F:low1 F:adj F:low2
A:exp A:e0 A:e1 F:low3 A:e2 A:e3 A:p0 A:e4 A:e5 A:p1 A:e6 A:e7 A:p2 A:p3 F:low4 A:ot F:sum A:yt A:wo F:self A:n1a
F:gq0 F:gk A:n1b F:gq1 F:gv F:s0 A:gelu A:h0 A:h1 A:exp F:s1 A:gelu A:h2 A:h3 A:exp F:r0 F:t0 F:r1 F:t1 F:pv A:w2a
F:n0a A:w2b F:n0b A:n2a F:q A:n2b F:k F:v F:r A:lq F:c A:lk A:lv A:ls A:lqt A:lkt A:lc
'''.split()

W_COLS = {}
_at = 0
for _name, _n in (("self", C * D), ("gq", 2 * C * D), ("gk", 2 * C * D), ("gv", C * 2 * D),
                  ("q2", C * D), ("k2", C * D), ("v2", C * D), ("o2", C * D),
                  ("w1", C * MLP), ("w2", MLP // P * D),
                  ("q3", C * D), ("k3", C * D), ("v3", C * D), ("o3", C * D)):
    W_COLS[_name] = (_at, _n)
    _at += _n
W_TOTAL = _at
V_COLS = {}
_at = 0
for _name, _n in (("ln_g", C), ("ln_b", C), ("b1", C), ("b2", 64), ("bself", C), ("gbq", 2 * C), ("gbk", 2 * C),
                  ("gbout", 2 * C), ("bc", 6 * C), ("bq2", C), ("bk2", C), ("bo2", C), ("mb1", MLP // P),
                  ("mb2", C), ("n3g", C), ("n3b", C), ("bk3", C), ("embb", 2 * C), ("sng", C), ("snb", C),
                  ("ob3", C), ("cond", C * B)):
    V_COLS[_name] = (_at, _n)
    _at += _n
V_TOTAL = _at
R_COLS = {"bv2": (0, D), "bq3": (D, D), "bv3": (2 * D, D), "wl": (3 * D, NL), "bb": (3 * D + NL, 1)}
R_TOTAL = 3 * D + NL + 1
S_COLS = {"selfq": (0, C * D), "w1": (C * D, C * D), "wc": (2 * C * D, C * 6 * D), "emb": (8 * C * D, C * 2 * D)}
S_TOTAL = 10 * C * D
NLOW = 4 * C * RANK
MOD = NLOW
AFF = MOD + 6 * C
GATE = AFF + 2 * C
NPAR = GATE + C


class Progress:

    def __init__(self, sems, names):
        self.sems, self.names = sems, names
        self.next = [0] * len(sems)

    def inc(self, s, name):
        assert self.names[self.next[s] % len(self.names)] == name, (name, self.names[self.next[s] % len(self.names)])
        self.next[s] += 1
        return self.sems[s], 1

    def at(self, s, it, name):
        return self.sems[s], it * len(self.names) + self.names.index(name) + 2

    def past(self, s, it):
        return self.sems[s], it * len(self.names) + 1

    def begin(self, engine):
        for sem in self.sems:
            engine.sem_inc(sem, 1)


def build(nc, x_in, cond_in, adj_in, w_in, v_in, r_in, s_in, low_in, out):
    ctx = ExitStack()
    with ctx:
        def sb(name, shape, dt=F32):
            return ctx.enter_context(nc.sbuf_tensor(name, shape, dt))

        def sem(name):
            return ctx.enter_context(nc.semaphore(name))

        def progress(name, names):
            return Progress([sem(f"{name}_{s}") for s in range(SLOTS)], names.split())

        W = sb("W", [P, W_TOTAL])
        V = sb("V", [P, V_TOTAL])
        R = sb("R", [P, R_TOTAL])
        par_all = sb("par_all", [P, B, NPAR])
        ident = sb("ident", [P, P])
        mean_w = sb("mean_w", [P, P])
        ones_c = sb("ones_c", [P, 1])
        eps_c = sb("eps_c", [P, 1])
        ones_b = sb("ones_b", [P, 2 * H * T // P], BF16)
        blk16 = sb("blk16", [P, HC, DH])
        blk24 = sb("blk24", [4 * MP, 4, DH])
        probs = sb("probs", [P, 4, 4, T])

        def w(name, a):
            lo, n = W_COLS[name]
            return W[:, lo:lo + n].rearrange("p (a n) -> p a n", a=a)

        def vec(name):
            lo, n = V_COLS[name]
            return V[:, lo:lo + n]

        def row(name):
            lo, n = R_COLS[name]
            return R[:, lo:lo + n]

        class Slot:
            pass

        SL = []
        for s in range(SLOTS):
            o = Slot()

            def own(name, shape, dt=F32, s=s):
                return sb(f"{name}{s}", shape, dt)

            o.par_low = own("par_low", [P, NLOW])
            o.par = own("par", [P, NPAR - NLOW])
            o.x = own("x", [P, C, T])
            o.x1 = own("x1_", [P, C, T])
            o.x2 = own("x2_", [P, C, T])
            o.xc = own("xc", [P, C, T])
            o.sq = own("sq", [P, C, T])
            o.rstd = own("rstd", [P, T])
            o.xm = own("xm", [P, C, T])
            o.big = own("big", [P, 8, T])
            o.bbT = own("bbT", [P, 2, C, P])
            o.y1 = own("y1_", [P, T])
            o.zrow = own("zrow", [P, T])
            o.qrow = own("qrow", [P, D])
            o.sfrep = own("sfrep", [P, C, 4, MP])
            o.kb = own("kb", [P, 2 * C, M])
            o.cond = own("cond_", [P, TT, 2 * M])
            o.mask = own("mask", [P, TT, 2 * M])
            o.bias = own("bias", [P, TT, 2 * M])
            o.mx = own("mx", [P, 2 * H])
            o.sm = own("sm", [P, 2 * H])
            o.ri = own("ri", [P, 2 * H])
            o.stack = own("stack", [P, 2 * H * T], BF16)
            o.parts = own("parts", [P, 3 * 2 * C * T], BF16)
            o.vp = own("vp", [P, TT, H, 2 * DH])
            o.yF = own("yF", [P, C, T])
            o.mx2 = own("mx2_", [P, TT, H])
            o.nmx = own("nmx", [H, 2, T], BF16)
            o.ks = own("ks", [P, C])
            o.nk = own("nk", [P, C])
            o.ctx = own("ctx_", [P, C, P])
            st = o.stack[:, :].bitcast(F32)
            o.adj = st[:, 0:880].bitcast(I32).rearrange("p (t n) -> p t n", t=TT)
            o.adjw = st[:, 880:1760].rearrange("p (t n) -> p t n", t=TT)
            o.S = st[:, 1760:1760 + 2 * H * M].rearrange("p (g m) -> p g m", m=M)
            o.gq = st[:, 2400:2400 + C * T].rearrange("p (c t) -> p c t", c=C)
            o.kbd = st[:, 2912:2912 + 2 * C * HC * M].rearrange("p (g h m) -> p g h m", h=HC, m=M)
            o.sf = st[:, 3552:3552 + C * T].rearrange("p (c t) -> p c t", c=C)
            o.gq1 = o.xm
            o.st = o.stack[:, :].rearrange("p (k h t) -> p k h t", k=2, h=H)
            o.qk = o.big[:, 0:4, :].rearrange("p (k c) t -> p k c t", k=2)
            o.rest = o.big[:, 4:8, :].rearrange("p (k c) t -> p k c t", k=2)
            o.part = o.parts[:, :].rearrange("p (k j c t) -> p j k c t", j=3, k=2, c=C)
            pf = o.parts[:, :].bitcast(F32)
            o.P = pf[:, :].rearrange("p (t h m) -> p t h m", t=TT, m=MP)
            o.oraw = pf[:, 0:1024].rearrange("p (g t) -> p g t", g=4)
            o.yq = pf[:, 1024:1536].rearrange("p (g l) -> p g l", l=DH)
            o.kT = pf[:, 0:512].rearrange("p (t c) -> p t c", t=TT)
            o.vt = pf[:, 512:1024].rearrange("p (t c) -> p t c", t=TT)
            o.ke = pf[:, 1024:1536].rearrange("p (c t) -> p c t", c=C)
            o.PT = o.big
            o.vbd = o.yF[0:4 * MP, :, :].rearrange("p a n -> p (a n)").rearrange("p (g n) -> p g n", g=8)
            o.h = o.big
            o.q3 = o.big[:, 0:2, :]
            o.q3s = o.big[:, 2:4, :]
            o.kf = o.big[:, 4:6, :]
            SL.append(o)

        G = ctx.enter_context(nc.psum_tensor("G", [P, SLOTS, 2, 512], F32))
        SS = ctx.enter_context(nc.psum_tensor("SS", [P, 2, 1024], F32))
        scr = [nc.dram_tensor(f"scr{s}", [2, 3, C * P, T], BF16, kind="Internal").ap() for s in range(SLOTS)]
        ones_d = nc.dram_tensor("ones_d", [2, H * T], BF16, kind="Internal").ap()
        qscr = nc.dram_tensor("qscr", [B, D], F32, kind="Internal").ap()

        start_w = probs[:, :, :, :].rearrange("p a b t -> p (a b t)")
        sw_f = SL[1].big[:, 0:4, :].rearrange("p a t -> p (a t)")

        def sw(name, a):
            lo, n = S_COLS[name]
            src = start_w[:, lo:lo + n] if lo + n <= 4096 else sw_f[:, lo - 4096:lo + n - 4096]
            return src.rearrange("p (a n) -> p a n", a=a)

        low_w = [SL[s].stack[:, :].bitcast(F32).rearrange("p (c n) -> p c n", c=C) for s in range(SLOTS)]
        ct = sb("ct", [B, D])
        cstat = sb("cstat", [B, 16])
        cT = sb("cT", [P, C, B])
        hT = sb("hT", [P, C, 32])
        wsb = SL[0].big[:, 0:2, :].rearrange("p a t -> p (a t)")
        sil = sb("sil", [P, C * B])
        sil2 = sb("sil2", [P, C * B])
        e1 = sb("e1", [P, 2 * C, B])

        ld_small = sem("ld_small")
        ld_start = sem("ld_start")
        ld_low = [sem(f"ld_low{i}") for i in range(2)]
        ld_w = sem("ld_w")
        ld_x = [sem(f"ld_x{s}") for s in range(SLOTS)]
        ld_adj = [sem(f"ld_adj{s}") for s in range(SLOTS)]
        split_out = [sem(f"split_out{s}") for s in range(SLOTS)]
        stacked = [sem(f"stacked{s}") for s in range(SLOTS)]
        stored = [sem(f"stored{s}") for s in range(SLOTS)]
        q_out = sem("q_out")
        ones_out = sem("ones_out")
        maxima = [sem(f"maxima{s}") for s in range(SLOTS)]
        ld_q = [sem(f"ld_q{s}") for s in range(SLOTS)]
        const_done = sem("const_done")
        pool_mask = sem("pool_mask")
        pre_pe = sem("pre_pe")
        pre_dve = sem("pre_dve")
        pre_act = sem("pre_act")

        pool_p = progress("pool_par", "low par pads")
        pool_g = progress("pool_gat", "p0 p1")
        pe_low = progress("pe_low", "bb y1 y2 z x1")
        act_low = progress("act_low", "g")
        dve_low = progress("dve_low", "bb y1 z x1")
        pe_gat = progress("pe_gat", "sum self q0 k q1 v s0 s1 t0 t1 pv")
        act_gat = progress("act_gat", "sf e0 e1 t0 t1")
        dve_gat = progress("dve_gat", "cond adjw vb mask neg bias zrow sfrep q0 kb kbd q1 vbd "
                           "m0 a0 x0 d0 m1 a1 x1 d1 s0 r0 s1 r1 o0 o1 x2")
        LN = "mean var"
        pe_ln = [progress(f"pe_ln{i}", LN) for i in range(4)]
        act_ln = [progress(f"act_ln{i}", "sq ln rstd") for i in range(4)]
        dve_ln = [progress(f"dve_ln{i}", "xc xn xm") for i in range(4)]
        pe_att = progress("pe_att", "q k v " + " ".join(f"m{u}" for u in range(8)) + " mx "
                          + " ".join(f"e{u}" + (f" p{u // 2 - 1}" if u % 2 and u > 1 else "") for u in range(8))
                          + " p3 ot yt o")
        act_att = progress("act_att", "c1 c2 " + " ".join(f"e{u}" for u in range(8)) + " o y")
        dve_att = progress("dve_att", "q k vp r1 c3 " + " ".join(f"m{u}" for u in range(8))
                           + " hi lo ri yq t x3")
        pe_mlp = progress("pe_mlp", "h0 h1 h2 h3 w2")
        act_mlp = progress("act_mlp", "h0 h1 h2 h3")
        dve_mlp = progress("dve_mlp", "t x4")
        pe_lin = progress("pe_lin", "q k v qT kT ctx y o")
        act_lin = progress("act_lin", "eq ek qT kT y tanh")
        dve_lin = progress("dve_lin", "q mx d k nk v sm ri p rk ctx s t out")

        N_CONST = 8 + SLOTS * 6
        block = ctx.enter_context(nc.Block())

        def each(name, stage, n):
            return {f"{name}{i}": (lambda it, s, o, i=i: stage(it, s, o, i)) for i in range(n)}

        def phase(engine, stages, a, lin, first):
            parts = {"A": a, "L": lin, "F": first}
            for part, name in (step.split(":") for step in ORDER):
                if parts[part] is not None and name in stages:
                    it, s = parts[part]
                    stages[name](it, s, SL[s])

        def run(engine, stages):
            last = PAIRS - 1
            phase(engine, stages, None, None, (0, 0))
            phase(engine, stages, (0, 0), None, (0, 1))
            with engine.Fori(0, last) as it:
                phase(engine, stages, (it, 1), (it, 0), (it + 1, 0))
                phase(engine, stages, (it + 1, 0), (it, 1), (it + 1, 1))
            phase(engine, stages, (last, 1), (last, 0), None)
            phase(engine, stages, None, (last, 1), None)


        @block.sync
        def _(sp):
            sp.dma_start(V[:, :], v_in).then_inc(ld_small, 16)
            sp.dma_start(ct[:, :], cond_in).then_inc(ld_small, 16)
            sp.dma_start(R[:, :], r_in.to_broadcast([P, R_TOTAL])).then_inc(ld_small, 16)
            sp.dma_start(start_w[:, 0:4096], s_in[:, 0:4096]).then_inc(ld_start, 16)
            sp.dma_start(sw_f, s_in[:, 4096:]).then_inc(ld_start, 16)
            sp.wait_ge(const_done, N_CONST)
            sp.dma_start(ones_d.rearrange("a (p n) -> (a p) n", n=2 * H * T // P), ones_b[:, :]).then_inc(ones_out, 16)
            for p in range(4):
                if p >= 2:
                    sp.wait_ge(pre_pe, 5 + 2 * (p - 2))
                sp.dma_start(low_w[p % 2], low_in[p]).then_inc(ld_low[p % 2], 16)
            sp.wait_ge(pre_dve, 6)
            sp.dma_start(qscr, ct[:, :]).then_inc(q_out, 16)
            sp.wait_ge(q_out, 16)
            sp.wait_ge(ones_out, 16)

            def snapped(pair):
                sm, n = pair
                return sm, n if isinstance(n, int) else sp.snap(n)

            def stack_counts(it, s):
                return [snapped(x) for x in (dve_att.at(s, it, "c3"), act_att.at(s, it, "c2"), dve_gat.at(s, it, "x2"),
                                             (split_out[s], it * 16 + 16))]

            def stack(s, counts):
                o = SL[s]
                third, second, graph_read, parts_out = counts
                sp.wait_ge(*third)
                sp.wait_ge(*second)
                sp.dma_start(scr[s].rearrange("k j (c p) t -> p (k j c) t", p=P),
                             o.parts[:, :].rearrange("p (n t) -> p n t", t=T)).then_inc(split_out[s], 16)
                sp.wait_ge(*parts_out)
                sp.wait_ge(*graph_read)
                for k, split in enumerate((SPLIT_Q, SPLIT_K)):
                    for j, n in SPLIT_RUNS:
                        src = scr[s][k, split[j]:split[j] + (n if k else 1)].rearrange("j (c h) t -> j c (h t)", c=DH)
                        sp.dma_start(o.st[j * DH:(j + n) * DH, k, :, :].rearrange("p h t -> p (h t)"),
                                     src.rearrange("j c n -> (j c) n") if k else src.to_broadcast([n, DH, H * T]))\
                            .then_inc(stacked[s], 16)
                sp.dma_start(o.st[KS:KM, 1, :, :].rearrange("p h t -> p (h t)"), ones_d).then_inc(stacked[s], 16)

            def negmax(s, count):
                sp.wait_ge(*count)
                for j in range(2):
                    sp.dma_start(SL[s].st[KS + j:KS + j + 1, 0, :, :], SL[s].nmx[:, j, :]).then_inc(maxima[s], 16)

            last = PAIRS - 1
            stack(0, stack_counts(0, 0))
            negmax(0, dve_att.at(0, 0, "lo"))
            stack(1, stack_counts(0, 1))
            with sp.Fori(0, last) as it:
                counts = [snapped(dve_att.at(1, it, "lo")), stack_counts(it + 1, 0),
                          snapped(dve_att.at(0, it + 1, "lo")), stack_counts(it + 1, 1)]
                negmax(1, counts[0])
                stack(0, counts[1])
                negmax(0, counts[2])
                stack(1, counts[3])
            negmax(1, dve_att.at(1, last, "lo"))
            for s in range(SLOTS):
                sp.wait_ge(stored[s], 16 * (PAIRS + 1))

        @block.gpsimd
        def _(pool):
            for p in (pool_p, pool_g):
                p.begin(pool)
            def mark(ins):
                ins.then_inc(const_done, 1)

            n = 0
            pool.memset(ident[:, :], 0.0).then_inc(pool_mask, 1)
            n += 1
            for t in (blk16[:, :, :], blk24[:, :, :]):
                pool.memset(t, 1.0).then_inc(pool_mask, 1)
                n += 1
            pool.wait_ge(pool_mask, n)
            mark(pool.affine_select(out=ident[:, :], in_=ident[:, :], compare_op=ALU.not_equal, fill=1.0, base=0,
                                    pattern=[[-1, P]], channel_multiplier=1))
            for t, size, g in ((blk16, DH, HC), (blk24, MP, 4)):
                pool.affine_select(out=t[:, :, :], in_=t[:, :, :], compare_op=ALU.is_ge, fill=0.0, base=0,
                                   pattern=[[-size, g], [0, DH]], channel_multiplier=1).then_inc(pool_mask, 1)
                n += 1
                pool.wait_ge(pool_mask, n)
                mark(pool.affine_select(out=t[:, :, :], in_=t[:, :, :], compare_op=ALU.is_ge, fill=0.0, base=size - 1,
                                        pattern=[[size, g], [0, DH]], channel_multiplier=-1))
            mark(pool.memset(mean_w[:, :], 1.0 / D))
            mark(pool.memset(ones_c[:, :], 1.0))
            mark(pool.memset(ones_b[:, :], 1.0))
            mark(pool.memset(eps_c[:, :], EPS))
            mark(pool.memset(hT[:, :, :], 0.0))
            for o in SL:
                for t in (o.bbT[:, :, :, :], o.y1[:, :], o.zrow[:, :], o.qrow[:, :], o.sfrep[:, :, :, :]):
                    mark(pool.memset(t, 0.0))
                mark(pool.memset(o.vp[:, :, :, :], 1.0))
            pool.wait_ge(pre_dve, 17)
            pool.wait_ge(q_out, 16)
            def load(it, s, o):
                b = it * SLOTS + s
                pool.wait_ge(*dve_low.past(s, it))
                pool.dma_start(o.x[:, :, :], x_in[bass.ds(b, 1)].rearrange("o p c t -> p (o c) t")).then_inc(ld_x[s], 16)
                pool.wait_ge(*pe_gat.past(s, it))
                pool.dma_start(o.qrow[0:1, :], qscr[bass.ds(b, 1)]).then_inc(ld_q[s], 16)
                pool.wait_ge(*pe_att.past(s, it))
                pool.dma_start(o.adj, adj_in[bass.ds(b, 1)].rearrange("o (t p) n -> p (o t) n", p=P)).then_inc(ld_adj[s], 16)
                pool.wait_ge(*pe_low.past(s, it))
                pool.tensor_copy(o.par_low[:, :], par_all[:, bass.ds(b, 1), 0:NLOW].rearrange("p o n -> p (o n)"))\
                    .then_inc(*pool_p.inc(s, "low"))

            def params(it, s, o):
                b = it * SLOTS + s
                pool.wait_ge(*dve_lin.past(s, it))
                pool.tensor_copy(o.par[:, :], par_all[:, bass.ds(b, 1), NLOW:NPAR].rearrange("p o n -> p (o n)"))\
                    .then_inc(*pool_p.inc(s, "par"))
                pool.memset(o.P[:, :, :, M:MP], 0.0).then_inc(*pool_p.inc(s, "pads"))

            def gat_norm(it, s, o, t):
                pool.wait_ge(*dve_gat.at(s, it, f"r{t}"))
                pool.tensor_tensor(o.P[:, t, :, 0:M], o.P[:, t, :, 0:M],
                                   o.ri[:, :].unsqueeze(2).to_broadcast([P, 2 * H, M]), ALU.mult)\
                    .then_inc(*pool_g.inc(s, f"p{t}"))

            run(pool, {
                "load": load, "par": params, **each("r", gat_norm, TT)})

        @block.tensor
        def _(pe):
            for p in (pe_low, pe_gat, *pe_ln, pe_att, pe_mlp, pe_lin):
                p.begin(pe)
            def mm(out_, lhsT, rhs, start=True, stop=True):
                return pe.matmul(out_, lhsT, rhs, start=start, stop=stop)

            def dense_f(bank, wt, src, cols=C, n=T):
                for m in range(cols):
                    for c in range(C):
                        last = mm(bank[:, m * n:(m + 1) * n], wt[:, c, m * P:(m + 1) * P], src[:, c, :],
                                  c == 0, c == C - 1)
                return last

            def dense_t(bank, wt, src):
                for t in range(TT):
                    for c in range(C):
                        last = mm(bank[:, t * D:(t + 1) * D], src[:, c, t * P:(t + 1) * P], wt[:, c, :],
                                  c == 0, c == C - 1)
                return last

            A0, A1, A2, A3 = SS[:, 0, 0:512], SS[:, 0, 512:1024], SS[:, 1, 0:512], SS[:, 1, 512:1024]
            pe.wait_ge(const_done, N_CONST)
            pe.wait_ge(ld_start, 32)
            pe.wait_ge(ld_small, 48)
            cF = vec("cond").rearrange("p (c b) -> p c b", c=C)
            for c in range(C):
                last = mm(A3[0:B, 0:D], cF[:, c, :], sw("selfq", C)[:, c, :], c == 0, c == C - 1)
            last.then_inc(pre_pe, 1)
            pe.wait_ge(pre_dve, 2)
            for c in range(C):
                last = pe.transpose(A0[:, c * B:(c + 1) * B], ct[:, c * P:(c + 1) * P], ident[0:B, 0:B])
            last.then_inc(pre_pe, 1)
            pe.wait_ge(pre_dve, 4)
            for m in range(C):
                for c in range(C):
                    last = mm(A1[:, m * B:(m + 1) * B], sw("w1", C)[:, c, m * P:(m + 1) * P], cT[:, c, :],
                              c == 0, c == C - 1)
            last.then_inc(pre_pe, 1)
            pe.wait_ge(pre_act, 3)
            for p in range(4):
                pe.wait_ge(ld_low[p % 2], 16 * (p // 2 + 1))
                if p:
                    pe.wait_ge(pre_act, 3 + p)
                for a in range(4):
                    for c in range(C):
                        last = mm(A2[32 * a:32 * a + 32, :], hT[:, c, :], low_w[p % 2][:, c, a * 512:(a + 1) * 512],
                                  c == 0, c == C - 1)
                last.then_inc(pre_pe, 1)
                pe.wait_ge(pre_act, 4 + p)
                if p:
                    pe.wait_ge(pre_dve, 6 + p)
                else:
                    pe.wait_ge(pre_dve, 4)
                for j in range(4):
                    last = pe.transpose(A0[:, j * P:(j + 1) * P], wsb[:, j * P:(j + 1) * P], ident[:, :])
                last.then_inc(pre_pe, 1)
            pe.wait_ge(pre_act, 8)
            pe.wait_ge(pre_dve, 13)
            silv = sil[:, :].rearrange("p (c b) -> p c b", c=C)
            for m in range(6 * C):
                for c in range(C):
                    mm(A1[:, m * B:(m + 1) * B], sw("wc", C)[:, c, m * P:(m + 1) * P], silv[:, c, :], c == 0, c == C - 1)
            for m in range(2 * C):
                for c in range(C):
                    last = mm(A1[:, (6 * C + m) * B:(6 * C + m + 1) * B], sw("emb", C)[:, c, m * P:(m + 1) * P],
                              silv[:, c, :], c == 0, c == C - 1)
            last.then_inc(pre_pe, 1)
            pe.wait_ge(pre_dve, 17)
            pe.wait_ge(ld_w, 32)

            def low_1(it, s, o):
                pe.wait_ge(*pool_p.at(s, it, "low"))
                pe.wait_ge(*dve_lin.past(s, it))
                for f in range(2):
                    for c in range(C):
                        k = (2 * f + 1) * C * RANK + c * RANK
                        last = pe.transpose(G[0:RANK, s, 1, (f * C + c) * P:(f * C + c + 1) * P],
                                            o.par_low[:, k:k + RANK], ident[:, :])
                last.then_inc(*pe_low.inc(s, "bb"))
                pe.wait_ge(ld_x[s], it * 16 + 16)
                for c in range(C):
                    last = mm(G[0:RANK, s, 0, 0:T], o.par_low[:, c * RANK:(c + 1) * RANK], o.x[:, c, :], c == 0, c == C - 1)
                last.then_inc(*pe_low.inc(s, "y1"))

            def low_2(it, s, o):
                pe.wait_ge(*dve_low.at(s, it, "y1"))
                for c in range(C):
                    last = mm(G[:, s, 0, c * T:(c + 1) * T], o.bbT[:, 0, c, :], o.y1[:, :])
                last.then_inc(*pe_low.inc(s, "y2"))

            def low_3(it, s, o):
                pe.wait_ge(*act_low.at(s, it, "g"))
                for c in range(C):
                    k = 2 * C * RANK + c * RANK
                    last = mm(G[0:RANK, s, 1, 0:T], o.par_low[:, k:k + RANK], o.xm[:, c, :], c == 0, c == C - 1)
                last.then_inc(*pe_low.inc(s, "z"))

            def low_4(it, s, o):
                pe.wait_ge(*dve_low.at(s, it, "z"))
                for c in range(C):
                    last = mm(G[:, s, 0, c * T:(c + 1) * T], o.bbT[:, 1, c, :], o.y1[:, :])
                last.then_inc(*pe_low.inc(s, "x1"))

            def gat_sum(it, s, o):
                pe.wait_ge(*dve_low.at(s, it, "x1"))
                for c in range(C):
                    last = mm(G[0:1, s, 1, 0:T], ones_c[:, :], o.x1[:, c, :], c == 0, c == C - 1)
                last.then_inc(*pe_gat.inc(s, "sum"))

            def gat_self(it, s, o):
                pe.wait_ge(*dve_gat.at(s, it, "zrow"))
                pe.wait_ge(ld_q[s], it * 16 + 16)
                for m in range(C):
                    for c in range(C):
                        mm(G[:, s, 0, m * T:(m + 1) * T], w("self", C)[:, c, m * P:(m + 1) * P], o.x1[:, c, :],
                           c == 0, False)
                    last = mm(G[:, s, 0, m * T:(m + 1) * T], o.qrow[:, m * P:(m + 1) * P], o.zrow[:, :], False, True)
                last.then_inc(*pe_gat.inc(s, "self"))

            def gat_query_0(it, s, o):
                pe.wait_ge(*act_gat.at(s, it, "sf"))
                dense_f(G[:, s, 1, :], w("gq", 2 * C)[:, 0:C, :], o.sf).then_inc(*pe_gat.inc(s, "q0"))

            def gat_keys(it, s, o):
                wk = w("gk", 2 * C)
                for d in range(2):
                    for m in range(C):
                        for c in range(C):
                            last = mm(G[:, s, 0, (d * C + m) * M:(d * C + m + 1) * M],
                                      wk[:, d * C + c, m * P:(m + 1) * P], o.sf[:, c, 0:M], c == 0, c == C - 1)
                last.then_inc(*pe_gat.inc(s, "k"))

            def gat_query_1(it, s, o):
                pe.wait_ge(*dve_gat.at(s, it, "q0"))
                dense_f(G[:, s, 1, :], w("gq", 2 * C)[:, C:2 * C, :], o.sf).then_inc(*pe_gat.inc(s, "q1"))

            def gat_vals(it, s, o):
                pe.wait_ge(*dve_gat.at(s, it, "kb"))
                pe.wait_ge(*dve_gat.at(s, it, "sfrep"))
                for c in range(C):
                    last = mm(G[0:4 * MP, s, 0, :], o.sfrep[:, c, :, :].rearrange("p a m -> p (a m)"),
                              w("gv", C)[:, c, :], c == 0, c == C - 1)
                last.then_inc(*pe_gat.inc(s, "v"))

            def gat_scores(it, s, o, t):
                pe.wait_ge(*dve_gat.at(s, it, "vbd" if t == 0 else "m0"))
                for d, q in enumerate((o.gq, o.gq1)):
                    for c in range(C):
                        last = mm(G[:, s, d, c * HC * M:(c + 1) * HC * M], q[:, c, t * P:(t + 1) * P],
                                  o.kbd[:, d * C + c, :, :].rearrange("p h m -> p (h m)"))
                last.then_inc(*pe_gat.inc(s, f"s{t}"))

            def gat_turn(it, s, o, t):
                pe.wait_ge(*pool_g.at(s, it, f"p{t}"))
                pe.wait_ge(*(dve_gat.at(s, it, "m1") if t == 0 else act_gat.at(s, it, "t0")))
                for g in range(8):
                    last = pe.transpose(G[0:4 * MP, s, g // 4, g % 4 * P:(g % 4 + 1) * P],
                                        o.P[:, t, 4 * g:4 * g + 4, :].rearrange("p h m -> p (h m)"), ident[:, :])
                last.then_inc(*pe_gat.inc(s, f"t{t}"))

            def gat_values(it, s, o):
                pe.wait_ge(*act_gat.at(s, it, "t1"))
                for g in range(4):
                    a = g % 2 * 64
                    for d in range(2):
                        last = mm(G[a:a + 64, s, 0, g // 2 * T:(g // 2 + 1) * T], o.vbd[:, d * 4 + g, :],
                                  o.PT[0:4 * MP, d * 4 + g, :], d == 0, d == 1)
                last.then_inc(*pe_gat.inc(s, "pv"))

            def mean(it, s, o, i, src, *ready):
                for r in ready:
                    pe.wait_ge(*r)
                for c in range(C):
                    last = mm(G[:, s, 1, 0:T], mean_w[:, :], src[:, c, :], c == 0, c == C - 1)
                last.then_inc(*pe_ln[i].inc(s, "mean"))

            def var(it, s, o, i):
                pe.wait_ge(*act_ln[i].at(s, it, "sq"))
                for c in range(C):
                    last = mm(G[:, s, 0, 0:T], mean_w[:, :], o.sq[:, c, :], c == 0, c == C - 1)
                last.then_inc(*pe_ln[i].inc(s, "var"))

            def att_q(it, s, o):
                pe.wait_ge(*dve_ln[0].at(s, it, "xm"))
                dense_f(G[:, s, 0, :], w("q2", C), o.xm).then_inc(*pe_att.inc(s, "q"))

            def att_k(it, s, o):
                dense_f(G[:, s, 1, :], w("k2", C), o.xm).then_inc(*pe_att.inc(s, "k"))

            def att_v(it, s, o):
                pe.wait_ge(*dve_att.at(s, it, "q"))
                dense_t(G[:, s, 0, :], w("v2", C), o.xm).then_inc(*pe_att.inc(s, "v"))

            def att_max(it, s, o, u):
                if u == 0:
                    pe.wait_ge(stacked[s], (it + 1) * 16 * N_STACK)
                if u >= 2:
                    pe.wait_ge(*dve_att.at(s, it, f"m{u - 2}"))
                elif s:
                    pe.wait_ge(*act_att.at(0, it, f"e{u + 6}"))
                else:
                    pe.wait_ge(*act_att.past(1, it))
                for k in range(2):
                    for t in range(TT):
                        h = 2 * u + k
                        last = mm(SS[:, u % 2, (k * TT + t) * T:(k * TT + t + 1) * T],
                                  o.st[0:KS, 0, h, t * P:(t + 1) * P], o.st[0:KS, 1, h, :])
                last.then_inc(*pe_att.inc(s, f"m{u}"))

            def att_turn_max(it, s, o):
                pe.wait_ge(*dve_att.at(s, it, "m7"))
                for t in range(TT):
                    last = pe.transpose(G[0:H, s, 1, t * P:(t + 1) * P], o.mx2[:, t, :], ident[:, :])
                last.then_inc(*pe_att.inc(s, "mx"))

            def att_exp(it, s, o, u):
                if u == 0:
                    pe.wait_ge(maxima[s], (it + 1) * 32)
                if u >= 2:
                    pe.wait_ge(*act_att.at(s, it, f"e{u - 2}"))
                else:
                    pe.wait_ge(*dve_att.at(s, it, f"m{u + 6}"))
                for k in range(2):
                    for t in range(TT):
                        h = 2 * u + k
                        last = mm(SS[:, u % 2, (k * TT + t) * T:(k * TT + t + 1) * T],
                                  o.st[0:KM, 1, h, t * P:(t + 1) * P], o.st[0:KM, 0, h, :])
                last.then_inc(*pe_att.inc(s, f"e{u}"))

            def values(it, s, o, g):
                pe.wait_ge(*act_att.at(s, it, f"e{2 * g + 1}"))
                for t in range(TT):
                    for a in range(4):
                        u, k = (4 * g + a) // 2, a % 2
                        last = mm(G[32 * a:32 * a + 32, s, g // 2, g % 2 * T:(g % 2 + 1) * T],
                                  o.vp[:, t, 4 * g + a, :], probs[:, u % 4, k * TT + t, :], t == 0, t == TT - 1)
                last.then_inc(*pe_att.inc(s, f"p{g}"))

            def att_turn(it, s, o):
                pe.wait_ge(*act_att.at(s, it, "o"))
                for t in range(TT):
                    for g in range(4):
                        last = pe.transpose(G[:, s, t, g * P:(g + 1) * P], o.oraw[:, g, t * P:(t + 1) * P], ident[:, :])
                last.then_inc(*pe_att.inc(s, "ot"))

            def att_back(it, s, o):
                pe.wait_ge(*dve_att.at(s, it, "yq"))
                yq = o.yq.rearrange("p (t g) l -> p t (g l)", t=TT)
                for c in range(C):
                    for t in range(TT):
                        last = pe.transpose(G[:, s, 0, c * T + t * P:c * T + (t + 1) * P],
                                            yq[:, t, c * P:(c + 1) * P], ident[:, :])
                last.then_inc(*pe_att.inc(s, "yt"))

            def att_out(it, s, o):
                pe.wait_ge(*act_att.at(s, it, "y"))
                dense_f(G[:, s, 1, :], w("o2", C), o.yF).then_inc(*pe_att.inc(s, "o"))

            def mlp_up(it, s, o, i):
                if i == 0:
                    pe.wait_ge(*dve_ln[1].at(s, it, "xm"))
                if i >= 2:
                    pe.wait_ge(*act_mlp.at(s, it, f"h{i - 2}"))
                dense_f(G[:, s, i % 2, :], w("w1", C)[:, :, i * 2 * P:(i + 1) * 2 * P], o.xm)\
                    .then_inc(*pe_mlp.inc(s, f"h{i}"))

            def mlp_down(it, s, o, m):
                if m == 0:
                    pe.wait_ge(*act_mlp.at(s, it, "h3"))
                K = MLP // P
                for k in range(K):
                    last = mm(G[:, s, 0, m * T:(m + 1) * T], w("w2", K)[:, k, m * P:(m + 1) * P], o.h[:, k, :],
                              k == 0, k == K - 1)
                if m == C - 1:
                    last.then_inc(*pe_mlp.inc(s, "w2"))

            def lin_q(it, s, o):
                pe.wait_ge(*dve_ln[2].at(s, it, "xm"))
                dense_t(G[:, s, 0, :], w("q3", C), o.xm).then_inc(*pe_lin.inc(s, "q"))

            def lin_k(it, s, o):
                dense_f(G[:, s, 1, :], w("k3", C), o.xm).then_inc(*pe_lin.inc(s, "k"))

            def lin_v(it, s, o):
                pe.wait_ge(*dve_lin.at(s, it, "q"))
                dense_t(G[:, s, 0, :], w("v3", C), o.xm).then_inc(*pe_lin.inc(s, "v"))

            def lin_turn_q(it, s, o):
                pe.wait_ge(*dve_lin.at(s, it, "p"))
                for c in range(C):
                    for t in range(TT):
                        last = pe.transpose(G[:, s, 1, c * T + t * P:c * T + (t + 1) * P],
                                            o.q3[:, t, c * P:(c + 1) * P], ident[:, :])
                last.then_inc(*pe_lin.inc(s, "qT"))

            def lin_turn_k(it, s, o):
                pe.wait_ge(*act_lin.at(s, it, "ek"))
                for t in range(TT):
                    for c in range(C):
                        last = pe.transpose(G[:, s, 0, t * D + c * P:t * D + (c + 1) * P],
                                            o.ke[:, c, t * P:(t + 1) * P], ident[:, :])
                last.then_inc(*pe_lin.inc(s, "kT"))

            def lin_ctx(it, s, o):
                pe.wait_ge(*act_lin.at(s, it, "kT"))
                for c in range(C):
                    for t in range(TT):
                        last = mm(G[:, s, 1, c * P:(c + 1) * P], o.kT[:, t, c * P:(c + 1) * P],
                                  o.vt[:, t, c * P:(c + 1) * P], t == 0, t == TT - 1)
                last.then_inc(*pe_lin.inc(s, "ctx"))

            def lin_y(it, s, o):
                pe.wait_ge(*dve_lin.at(s, it, "ctx"))
                for c in range(C):
                    last = mm(G[:, s, 0, c * T:(c + 1) * T], o.ctx[:, c, :], o.q3s[:, c, :])
                last.then_inc(*pe_lin.inc(s, "y"))

            def lin_out(it, s, o):
                pe.wait_ge(*dve_lin.at(s, it, "s"))
                dense_f(G[:, s, 1, :], w("o3", C), o.sq).then_inc(*pe_lin.inc(s, "o"))

            run(pe, {
                "low1": low_1, "low2": low_2, "low3": low_3, "low4": low_4,
                "sum": gat_sum, "self": gat_self,
                "gq0": gat_query_0, "gk": gat_keys, "gq1": gat_query_1, "gv": gat_vals,
                **each("s", gat_scores, TT), **each("t", gat_turn, TT),
                "pv": gat_values,
                "n0a": lambda it, s, o: mean(it, s, o, 0, o.x2, dve_gat.at(s, it, "x2")),
                "n0b": lambda it, s, o: var(it, s, o, 0),
                "q": att_q, "k": att_k, "v": att_v,
                **each("m", att_max, 8), "mx": att_turn_max, **each("e", att_exp, 8), **each("p", values, 4),
                "ot": att_turn, "yt": att_back, "wo": att_out,
                "n1a": lambda it, s, o: mean(it, s, o, 1, o.x1, dve_att.at(s, it, "x3")),
                "n1b": lambda it, s, o: var(it, s, o, 1),
                **each("h", mlp_up, 4),
                "w2a": lambda it, s, o: mlp_down(it, s, o, 0), "w2b": lambda it, s, o: mlp_down(it, s, o, 1),
                "n2a": lambda it, s, o: mean(it, s, o, 2, o.x2, dve_mlp.at(s, it, "x4")),
                "n2b": lambda it, s, o: var(it, s, o, 2),
                "lq": lin_q, "lk": lin_k, "lv": lin_v, "lqt": lin_turn_q, "lkt": lin_turn_k, "lc": lin_ctx, "ly": lin_y,
                "n3a": lambda it, s, o: mean(it, s, o, 3, o.yF, act_lin.at(s, it, "y")),
                "n3b": lambda it, s, o: var(it, s, o, 3),
                "lo": lin_out})

        @block.scalar
        def _(act):
            for p in (act_low, act_gat, *act_ln, act_att, act_mlp, act_lin):
                p.begin(act)
            for s in range(SLOTS):
                act.sem_inc(stored[s], 16)
            half = W_COLS["q2"][0]
            act.dma_start(W[:, 0:half], w_in[:, 0:half]).then_inc(ld_w, 16)
            act.dma_start(W[:, half:], w_in[:, half:]).then_inc(ld_w, 16)
            act.wait_ge(const_done, N_CONST)
            act.wait_ge(pre_dve, 1)
            act.activation(cstat[:, 8:9], cstat[:, 7:8], ACT.Ln, bias=eps_c[0:B, :]).then_inc(pre_act, 1)
            act.wait_ge(pre_act, 1)
            act.activation(cstat[:, 9:10], cstat[:, 8:9], ACT.Exp, scale=-0.5).then_inc(pre_act, 1)
            A1, A2 = SS[:, 0, 512:1024], SS[:, 1, 0:512]
            act.wait_ge(pre_pe, 3)
            act.activation(hT[:, 0, 0:B], A1[:, 0:B], ACT.Gelu, bias=vec("b1")[:, 0:1])
            act.activation(hT[:, 1, 0:B], A1[:, B:2 * B], ACT.Gelu, bias=vec("b1")[:, 1:2]).then_inc(pre_act, 1)
            for p in range(4):
                act.wait_ge(pre_pe, 4 + 2 * p)
                if p:
                    act.wait_ge(pre_pe, 3 + 2 * p)
                act.activation(wsb[:, :], A2, ACT.Copy).then_inc(pre_act, 1)
            act.activation(sil2[:, :], vec("cond"), ACT.Exp, scale=-1.0).then_inc(pre_act, 1)
            def low_gelu(it, s, o):
                act.wait_ge(*pe_low.at(s, it, "y2"))
                act.activation(o.xm[:, :, :].rearrange("p c t -> p (c t)"), G[:, s, 0, :], ACT.Gelu)\
                    .then_inc(*act_low.inc(s, "g"))

            def gat_self(it, s, o):
                act.wait_ge(*pe_gat.at(s, it, "self"))
                for m in range(C):
                    last = act.activation(o.sf[:, m, :], G[:, s, 0, m * T:(m + 1) * T], ACT.Identity,
                                          bias=vec("bself")[:, m:m + 1])
                last.then_inc(*act_gat.inc(s, "sf"))

            def gat_exp(it, s, o, t):
                act.wait_ge(*dve_gat.at(s, it, f"d{t}"))
                act.activation(o.P[:, t, :, 0:M], o.S, ACT.Exp).then_inc(*act_gat.inc(s, f"e{t}"))

            def gat_turned(it, s, o, t):
                act.wait_ge(*pe_gat.at(s, it, f"t{t}"))
                act.activation(o.PT[0:4 * MP, :, t * P:(t + 1) * P],
                               G[0:4 * MP, s, :, :].rearrange("p a (g n) -> p (a g) n", n=P), ACT.Copy)\
                    .then_inc(*act_gat.inc(s, f"t{t}"))

            def square(it, s, o, i):
                act.wait_ge(*dve_ln[i].at(s, it, "xc"))
                act.activation(o.sq[:, :, :], o.xc[:, :, :], ACT.Square).then_inc(*act_ln[i].inc(s, "sq"))

            def rstd(it, s, o, i):
                act.wait_ge(*pe_ln[i].at(s, it, "var"))
                act.activation(o.rstd[:, :], G[:, s, 0, 0:T], ACT.Ln, bias=eps_c[:, :])\
                    .then_inc(*act_ln[i].inc(s, "ln"))
                act.wait_ge(*act_ln[i].at(s, it, "ln"))
                act.activation(o.rstd[:, :], o.rstd[:, :], ACT.Exp, scale=-0.5).then_inc(*act_ln[i].inc(s, "rstd"))

            def att_part_1(it, s, o):
                act.wait_ge(*dve_att.at(s, it, "k"))
                act.activation(o.part[:, 0], o.qk, ACT.Copy).then_inc(*act_att.inc(s, "c1"))

            def att_part_2(it, s, o):
                act.wait_ge(*dve_att.at(s, it, "r1"))
                act.activation(o.part[:, 1], o.rest, ACT.Copy).then_inc(*act_att.inc(s, "c2"))

            def att_exp(it, s, o, u):
                act.wait_ge(*pe_att.at(s, it, f"e{u}"))
                if u >= 4:
                    act.wait_ge(*pe_att.at(s, it, f"p{(u - 4) // 2}"))
                elif s:
                    act.wait_ge(*pe_att.at(0, it, f"p{u // 2 + 2}"))
                else:
                    act.wait_ge(*pe_att.past(1, it))
                act.activation(probs[:, u % 4, :, :].rearrange("p a t -> p (a t)"), SS[:, u % 2, :], ACT.Exp)\
                    .then_inc(*act_att.inc(s, f"e{u}"))

            def att_o(it, s, o):
                act.wait_ge(*pe_att.at(s, it, "p3"))
                act.activation(o.oraw.rearrange("p g t -> p (g t)"),
                               G[:, s, :, :].rearrange("p a n -> p (a n)"), ACT.Copy)\
                    .then_inc(*act_att.inc(s, "o"))

            def att_y(it, s, o):
                act.wait_ge(*pe_att.at(s, it, "yt"))
                act.activation(o.yF[:, :, :].rearrange("p c t -> p (c t)"), G[:, s, 0, :], ACT.Copy)\
                    .then_inc(*act_att.inc(s, "y"))

            def mlp_gelu(it, s, o, i):
                act.wait_ge(*pe_mlp.at(s, it, f"h{i}"))
                for k in range(2):
                    m = 2 * i + k
                    last = act.activation(o.h[:, m, :], G[:, s, i % 2, k * T:(k + 1) * T], ACT.Gelu,
                                          bias=vec("mb1")[:, m:m + 1])
                last.then_inc(*act_mlp.inc(s, f"h{i}"))

            def lin_exp_q(it, s, o):
                act.wait_ge(*dve_lin.at(s, it, "d"))
                act.activation(o.q3, o.q3, ACT.Exp).then_inc(*act_lin.inc(s, "eq"))

            def lin_exp_k(it, s, o):
                act.wait_ge(*dve_lin.at(s, it, "nk"))
                for c in range(C):
                    last = act.activation(o.ke[:, c, :], o.kf[:, c, :], ACT.Exp, bias=o.nk[:, c:c + 1],
                                          accum_out=o.ks[:, c:c + 1])
                last.then_inc(*act_lin.inc(s, "ek"))

            def lin_turned_q(it, s, o):
                act.wait_ge(*pe_lin.at(s, it, "qT"))
                act.activation(o.q3s.rearrange("p c t -> p (c t)"), G[:, s, 1, :], ACT.Copy)\
                    .then_inc(*act_lin.inc(s, "qT"))

            def lin_turned_k(it, s, o):
                act.wait_ge(*pe_lin.at(s, it, "kT"))
                act.activation(o.kT.rearrange("p t c -> p (t c)"), G[:, s, 0, :], ACT.Copy)\
                    .then_inc(*act_lin.inc(s, "kT"))

            def lin_y(it, s, o):
                act.wait_ge(*pe_lin.at(s, it, "y"))
                act.activation(o.yF[:, :, :].rearrange("p c t -> p (c t)"), G[:, s, 0, :], ACT.Copy)\
                    .then_inc(*act_lin.inc(s, "y"))

            def lin_tanh(it, s, o):
                act.wait_ge(*dve_ln[3].at(s, it, "xm"))
                act.activation(o.sq[:, :, :], o.xm[:, :, :], ACT.Tanh).then_inc(*act_lin.inc(s, "tanh"))

            def store(it, s, o):
                act.wait_ge(*dve_lin.at(s, it, "out"))
                act.dma_start(out[bass.ds(it * SLOTS + s, 1)].rearrange("o p c t -> p (o c) t"), o.xc[:, :, :])\
                    .then_inc(stored[s], 16)

            run(act, {
                "exp": lambda it, s, o: act.preload_act_table_set("natural_log_exp_and_others"),
                "gelu": lambda it, s, o: act.preload_act_table_set("gelu_and_others"),
                "low2": low_gelu, "self": gat_self,
                **each("s", gat_exp, TT), **each("t", gat_turned, TT),
                "n0a": lambda it, s, o: square(it, s, o, 0), "n0b": lambda it, s, o: rstd(it, s, o, 0), "k": att_part_1, "r": att_part_2,
                **each("e", att_exp, 8), "p3": att_o, "yt": att_y,
                "n1a": lambda it, s, o: square(it, s, o, 1), "n1b": lambda it, s, o: rstd(it, s, o, 1), **each("h", mlp_gelu, 4),
                "n2a": lambda it, s, o: square(it, s, o, 2), "n2b": lambda it, s, o: rstd(it, s, o, 2),
                "lq": lin_exp_q, "lk": lin_exp_k, "lqt": lin_turned_q, "lkt": lin_turned_k, "ly": lin_y,
                "n3a": lambda it, s, o: square(it, s, o, 3), "n3b": lambda it, s, o: rstd(it, s, o, 3),
                "tanh": lin_tanh, "lo": store})

        @block.vector
        def _(dve):
            for p in (dve_low, dve_gat, *dve_ln, dve_att, dve_mlp, dve_lin):
                p.begin(dve)
            A0, A1, A3 = SS[:, 0, 0:512], SS[:, 0, 512:1024], SS[:, 1, 512:1024]
            n = 0

            def done(ins):
                nonlocal n
                n += 1
                ins.then_inc(pre_dve, 1)

            dve.wait_ge(ld_small, 48)
            stat = sem("stat")
            dve.bn_stats(cstat[:, 0:6], ct[:, :]).then_inc(stat, 1)
            dve.wait_ge(stat, 1)
            done(dve.bn_aggr(cstat[:, 6:8], cstat[:, 0:6]))
            dve.wait_ge(pre_act, 2)
            dve.wait_ge(pre_dve, 1)
            done(dve.tensor_scalar(ct[:, :], ct[:, :], cstat[:, 6:7], cstat[:, 9:10], ALU.subtract, ALU.mult))
            dve.wait_ge(pre_pe, 2)
            for c in range(C):
                done(dve.tensor_scalar(cT[:, c, :], A0[:, c * B:(c + 1) * B], vec("ln_g")[:, c:c + 1],
                                       vec("ln_b")[:, c:c + 1], ALU.mult, ALU.add))
            dve.wait_ge(pre_pe, 1)
            dve.tensor_tensor(vec("gbout")[:, 0:C], vec("gbout")[:, 0:C], vec("gbout")[:, C:2 * C], ALU.add)\
                .then_inc(stat, 1)
            done(dve.tensor_copy(ct[:, :], A3[0:B, 0:D]))
            done(dve.tensor_copy(par_all[:, :, GATE:GATE + C].rearrange("p b c -> p c b"),
                                 vec("cond").rearrange("p (c b) -> p c b", c=C)))
            for p in range(4):
                dve.wait_ge(pre_pe, 5 + 2 * p)
                lo = p * C * RANK
                done(dve.tensor_tensor(
                    par_all[:, :, lo:lo + 16].rearrange("p b (a j) -> p j a b", j=4),
                    A0.rearrange("p (j a b) -> p j a b", j=4, a=4)[:, :, :, 0:B],
                    vec("b2")[:, lo:lo + 16].rearrange("p (a j) -> p j a", j=4).unsqueeze(3).to_broadcast([P, 4, 4, B]),
                    ALU.add))
            dve.wait_ge(pre_act, 8)
            done(dve.tensor_scalar(sil2[:, :], sil2[:, :], 1.0, None, ALU.add))
            dve.wait_ge(pre_dve, 11)
            done(dve.reciprocal(sil2[:, :], sil2[:, :]))
            dve.wait_ge(pre_dve, 12)
            done(dve.tensor_tensor(sil[:, :], sil2[:, :], vec("cond"), ALU.mult))
            dve.wait_ge(pre_pe, 12)
            mods = A1[:, 0:6 * C * B].rearrange("p (k b) -> p k b", b=B)
            emb = A1[:, 6 * C * B:8 * C * B].rearrange("p (k b) -> p k b", b=B)
            dve.tensor_tensor(par_all[:, :, MOD:AFF].rearrange("p b k -> p k b"), mods,
                              vec("bc").unsqueeze(2).to_broadcast([P, 6 * C, B]), ALU.add).then_inc(stat, 1)
            dve.tensor_tensor(e1[:, :, :], emb, vec("embb").unsqueeze(2).to_broadcast([P, 2 * C, B]), ALU.add)\
                .then_inc(stat, 1)
            dve.wait_ge(stat, 4)
            for k in (1, 4):
                q = par_all[:, :, MOD + k * C:MOD + (k + 1) * C]
                dve.tensor_scalar(q, q, 1.0, None, ALU.add).then_inc(stat, 1)
            dve.tensor_scalar(e1[:, 0:C, :], e1[:, 0:C, :], 1.0, 0.5, ALU.add, ALU.mult).then_inc(stat, 1)
            dve.tensor_scalar(e1[:, C:2 * C, :], e1[:, C:2 * C, :], 0.5, None, ALU.mult).then_inc(stat, 1)
            dve.wait_ge(stat, 8)
            for c in range(C):
                done(dve.tensor_scalar(par_all[:, :, AFF + c], e1[:, c, :], vec("sng")[:, c:c + 1], None, ALU.mult))
                done(dve.scalar_tensor_tensor(out=par_all[:, :, AFF + C + c], in0=e1[:, c, :],
                                              scalar=vec("snb")[:, c:c + 1], in1=e1[:, C + c, :],
                                              op0=ALU.mult, op1=ALU.add))
            dve.wait_ge(const_done, N_CONST)
            assert n == 17
            def low_1(it, s, o):
                dve.wait_ge(*pe_low.at(s, it, "bb"))
                dve.tensor_copy(o.bbT[0:RANK, :, :, :].rearrange("p f c n -> p (f c n)"), G[0:RANK, s, 1, :])\
                    .then_inc(*dve_low.inc(s, "bb"))
                dve.wait_ge(*pe_low.at(s, it, "y1"))
                dve.tensor_copy(o.y1[0:RANK, :], G[0:RANK, s, 0, 0:T]).then_inc(*dve_low.inc(s, "y1"))

            def low_3(it, s, o):
                dve.wait_ge(*pe_low.at(s, it, "z"))
                dve.tensor_copy(o.y1[0:RANK, :], G[0:RANK, s, 1, 0:T]).then_inc(*dve_low.inc(s, "z"))

            def low_4(it, s, o):
                dve.wait_ge(*pe_low.at(s, it, "x1"))
                dve.tensor_tensor(o.x1[:, :, :], G[:, s, 0, :].rearrange("p (c t) -> p c t", c=C), o.x[:, :, :],
                                  ALU.add).then_inc(*dve_low.inc(s, "x1"))

            def gat_adj(it, s, o):
                dve.wait_ge(ld_adj[s], it * 16 + 16)
                adj = o.adj.rearrange("p t (m l) -> p (t m) l", l=NL)
                adjw = o.adjw.rearrange("p t (m l) -> p (t m) l", l=NL)
                flat = [x[:, :, :].rearrange("p t m -> p (t m)") for x in (o.cond, o.mask, o.bias)]
                dve.tensor_reduce(flat[0], adj, AX, ALU.add).then_inc(*dve_gat.inc(s, "cond"))
                dve.tensor_tensor(adjw, adj, row("wl").unsqueeze(1).to_broadcast([P, TT * 2 * M, NL]), ALU.mult)\
                    .then_inc(*dve_gat.inc(s, "adjw"))
                dve.wait_ge(*dve_gat.at(s, it, "adjw"))
                dve.tensor_reduce(flat[2], adjw, AX, ALU.add).then_inc(*dve_gat.inc(s, "vb"))
                dve.tensor_scalar(flat[1], flat[0], 0.0, None, ALU.is_gt).then_inc(*dve_gat.inc(s, "mask"))
                dve.wait_ge(*dve_gat.at(s, it, "mask"))
                dve.tensor_scalar(flat[0], flat[1], -NEG, NEG, ALU.mult, ALU.add).then_inc(*dve_gat.inc(s, "neg"))
                dve.wait_ge(*dve_gat.at(s, it, "neg"))
                dve.scalar_tensor_tensor(out=flat[2], in0=flat[2], scalar=row("bb"), in1=flat[0],
                                         op0=ALU.add, op1=ALU.add).then_inc(*dve_gat.inc(s, "bias"))

            def gat_zrow(it, s, o):
                dve.wait_ge(*pe_gat.at(s, it, "sum"))
                dve.tensor_scalar(o.zrow[0:1, :], G[0:1, s, 1, 0:T], 0.0, None, ALU.not_equal)\
                    .then_inc(*dve_gat.inc(s, "zrow"))

            def gat_query(it, s, o, d, q):
                dve.wait_ge(*pe_gat.at(s, it, f"q{d}"))
                for m in range(C):
                    k = d * C + m
                    last = dve.tensor_scalar(q[:, m, :], G[:, s, 1, m * T:(m + 1) * T], vec("gbq")[:, k:k + 1],
                                             float(DH) ** -0.5, ALU.add, ALU.mult)
                last.then_inc(*dve_gat.inc(s, f"q{d}"))

            def gat_self(it, s, o):
                dve.wait_ge(*act_gat.at(s, it, "sf"))
                dve.tensor_copy(o.sfrep[:, :, :, 0:M], o.sf[:, :, 0:M].unsqueeze(2).to_broadcast([P, C, 4, M]))\
                    .then_inc(*dve_gat.inc(s, "sfrep"))

            def gat_keys(it, s, o):
                dve.wait_ge(*pe_gat.at(s, it, "k"))
                dve.tensor_tensor(o.kb[:, :, :], G[:, s, 0, 0:2 * C * M].rearrange("p (g m) -> p g m", m=M),
                                  vec("gbk").unsqueeze(2).to_broadcast([P, 2 * C, M]), ALU.add)\
                    .then_inc(*dve_gat.inc(s, "kb"))
                dve.wait_ge(*dve_gat.at(s, it, "kb"))
                dve.tensor_tensor(o.kbd, o.kb[:, :, :].unsqueeze(2).to_broadcast([P, 2 * C, HC, M]),
                                  blk16[:, :, 0].unsqueeze(1).unsqueeze(3).to_broadcast([P, 2 * C, HC, M]),
                                  ALU.mult).then_inc(*dve_gat.inc(s, "kbd"))

            def gat_vals(it, s, o):
                dve.wait_ge(*pe_gat.at(s, it, "v"))
                dve.tensor_tensor(o.vbd, G[0:4 * MP, s, 0, :].rearrange("p (g n) -> p g n", g=8),
                                  blk24[:, :, :].rearrange("p a l -> p (a l)").unsqueeze(1)
                                  .to_broadcast([4 * MP, 8, 4 * DH]), ALU.mult).then_inc(*dve_gat.inc(s, "vbd"))

            def gat_soft(it, s, o, t):
                dve.wait_ge(*pe_gat.at(s, it, f"s{t}"))
                S = o.S.rearrange("p (d h) m -> p d h m", d=2)

                def heads(x):
                    return x[:, t, :].rearrange("p (d m) -> p d m", d=2).unsqueeze(2).to_broadcast([P, 2, H, M])

                if t:
                    dve.wait_ge(*act_gat.at(s, it, "e0"))
                dve.tensor_tensor(S, G[:, s, :, 0:H * M].rearrange("p d (h m) -> p d h m", m=M), heads(o.mask),
                                  ALU.mult).then_inc(*dve_gat.inc(s, f"m{t}"))
                dve.wait_ge(*dve_gat.at(s, it, f"m{t}"))
                dve.tensor_tensor(S, S, heads(o.bias), ALU.add).then_inc(*dve_gat.inc(s, f"a{t}"))
                dve.wait_ge(*dve_gat.at(s, it, f"a{t}"))
                dve.tensor_reduce(o.mx[:, :], o.S, AX, ALU.max).then_inc(*dve_gat.inc(s, f"x{t}"))
                dve.wait_ge(*dve_gat.at(s, it, f"x{t}"))
                dve.tensor_tensor(o.S, o.S, o.mx[:, :].unsqueeze(2).to_broadcast([P, 2 * H, M]), ALU.subtract)\
                    .then_inc(*dve_gat.inc(s, f"d{t}"))

            def gat_sums(it, s, o, t):
                dve.wait_ge(*act_gat.at(s, it, f"e{t}"))
                if t:
                    dve.wait_ge(*dve_gat.at(s, it, "r0"))
                dve.tensor_reduce(o.sm[:, :], o.P[:, t, :, 0:M], AX, ALU.add).then_inc(*dve_gat.inc(s, f"s{t}"))
                dve.wait_ge(*dve_gat.at(s, it, f"s{t}"))
                if t:
                    dve.wait_ge(*pool_g.at(s, it, "p0"))
                dve.reciprocal(o.ri[:, :], o.sm[:, :]).then_inc(*dve_gat.inc(s, f"r{t}"))

            def gat_out(it, s, o):
                dve.wait_ge(stored[s], it * 16 + 16)
                dve.wait_ge(*pe_gat.at(s, it, "pv"))
                for c in range(C):
                    dve.scalar_tensor_tensor(out=o.xc[:, c, :], in0=G[:, s, 0, c * T:(c + 1) * T],
                                             scalar=vec("gbout")[:, c:c + 1], in1=o.sf[:, c, :],
                                             op0=ALU.add, op1=ALU.add).then_inc(*dve_gat.inc(s, f"o{c}"))
                dve.wait_ge(*dve_gat.at(s, it, "o1"))
                dve.scalar_tensor_tensor(out=o.x2[:, :, :], in0=o.xc[:, :, :], scalar=0.0, in1=o.x1[:, :, :],
                                         op0=ALU.max, op1=ALU.add).then_inc(*dve_gat.inc(s, "x2"))

            def centre(it, s, o, i, src):
                dve.wait_ge(*pe_ln[i].at(s, it, "mean"))
                dve.tensor_tensor(o.xc[:, :, :], src[:, :, :], G[:, s, 1, 0:T].unsqueeze(1).to_broadcast([P, C, T]),
                                  ALU.subtract).then_inc(*dve_ln[i].inc(s, "xc"))

            def scale(it, s, o, i, gain, shift):
                dve.wait_ge(*act_ln[i].at(s, it, "rstd"))
                dve.tensor_tensor(o.xc[:, :, :], o.xc[:, :, :], o.rstd[:, :].unsqueeze(1).to_broadcast([P, C, T]),
                                  ALU.mult).then_inc(*dve_ln[i].inc(s, "xn"))
                dve.wait_ge(*dve_ln[i].at(s, it, "xn"))
                for c in range(C):
                    last = dve.tensor_scalar(o.xm[:, c, :], o.xc[:, c, :], gain[:, c:c + 1], shift[:, c:c + 1],
                                             ALU.mult, ALU.add)
                last.then_inc(*dve_ln[i].inc(s, "xm"))

            def mod(o, k):
                return o.par[:, k * C:(k + 1) * C]

            def att_qk(it, s, o, k):
                name, b = (("q", "bq2"), ("k", "bk2"))[k]
                dve.wait_ge(*pe_att.at(s, it, name))
                for c in range(C):
                    last = dve.tensor_scalar(o.qk[:, k, c, :], G[:, s, k, c * T:(c + 1) * T],
                                             vec(b)[:, c:c + 1], 1.0 / DH if k == 0 else 1.0,
                                             ALU.add, ALU.mult)
                last.then_inc(*dve_att.inc(s, name))

            def att_v(it, s, o):
                dve.wait_ge(*pe_att.at(s, it, "v"))
                dve.tensor_tensor(o.vp[:, :, :, 0:DH], G[:, s, 0, :].rearrange("p (t h l) -> p t h l", t=TT, h=H),
                                  row("bv2").rearrange("p (h l) -> p h l", h=H).unsqueeze(1)
                                  .to_broadcast([P, TT, H, DH]), ALU.add).then_inc(*dve_att.inc(s, "vp"))

            def att_rest(it, s, o):
                dve.wait_ge(*act_att.at(s, it, "c1"))
                dve.tensor_tensor(o.rest, o.qk, o.part[:, 0], ALU.subtract).then_inc(*dve_att.inc(s, "r1"))

            def att_part_3(it, s, o):
                dve.wait_ge(*act_att.at(s, it, "c2"))
                dve.tensor_tensor(o.part[:, 2], o.rest, o.part[:, 1], ALU.subtract).then_inc(*dve_att.inc(s, "c3"))

            def att_max(it, s, o, u):
                dve.wait_ge(*pe_att.at(s, it, f"m{u}"))
                dve.tensor_reduce(o.mx2[:, :, 2 * u:2 * u + 2].rearrange("p t k -> p k t"),
                                  SS[:, u % 2, :].rearrange("p (k t n) -> p k t n", k=2, t=TT), AX, ALU.max)\
                    .then_inc(*dve_att.inc(s, f"m{u}"))

            def att_negmax(it, s, o):
                dve.wait_ge(*pe_att.at(s, it, "mx"))
                dve.tensor_scalar(o.nmx[:, 0, :], G[0:H, s, 1, 0:T], -1.0, None, ALU.mult)\
                    .then_inc(*dve_att.inc(s, "hi"))
                dve.wait_ge(*dve_att.at(s, it, "hi"))
                dve.scalar_tensor_tensor(out=o.nmx[:, 1, :], in0=G[0:H, s, 1, 0:T], scalar=-1.0,
                                         in1=o.nmx[:, 0, :], op0=ALU.mult, op1=ALU.subtract)\
                    .then_inc(*dve_att.inc(s, "lo"))

            def att_norm(it, s, o):
                dve.wait_ge(*pe_att.at(s, it, "ot"))
                g = G[:, s, :, :].rearrange("p t (g n) -> p (t g) n", n=2 * DH)
                dve.reciprocal(o.ri[:, :], g[:, :, DH]).then_inc(*dve_att.inc(s, "ri"))
                dve.wait_ge(*dve_att.at(s, it, "ri"))
                dve.tensor_tensor(o.yq, g[:, :, 0:DH], o.ri[:, :].unsqueeze(2).to_broadcast([P, 2 * H, DH]),
                                  ALU.mult).then_inc(*dve_att.inc(s, "yq"))

            def gated(it, s, o, sems, pe_done, names, bank, bias, k, src, dst):
                dve.wait_ge(*pe_done)
                for c in range(C):
                    last = dve.tensor_scalar(o.xc[:, c, :], G[:, s, bank, c * T:(c + 1) * T], vec(bias)[:, c:c + 1],
                                             mod(o, k)[:, c:c + 1], ALU.add, ALU.mult)
                last.then_inc(*sems.inc(s, names[0]))
                dve.wait_ge(*sems.at(s, it, names[0]))
                dve.tensor_tensor(dst[:, :, :], o.xc[:, :, :], src[:, :, :], ALU.add).then_inc(*sems.inc(s, names[1]))

            def lin_q(it, s, o):
                groups = o.q3.rearrange("p t (h l) -> p (t h) l", l=DH)
                dve.wait_ge(*pe_lin.at(s, it, "q"))
                dve.tensor_tensor(o.q3, G[:, s, 0, :].rearrange("p (t n) -> p t n", t=TT),
                                  row("bq3").unsqueeze(1).to_broadcast([P, TT, D]), ALU.add)\
                    .then_inc(*dve_lin.inc(s, "q"))
                dve.wait_ge(*dve_lin.at(s, it, "q"))
                dve.tensor_reduce(o.mx[:, :], groups, AX, ALU.max).then_inc(*dve_lin.inc(s, "mx"))
                dve.wait_ge(*dve_lin.at(s, it, "mx"))
                dve.tensor_tensor(groups, groups, o.mx[:, :].unsqueeze(2).to_broadcast([P, 2 * H, DH]),
                                  ALU.subtract).then_inc(*dve_lin.inc(s, "d"))

            def lin_k(it, s, o):
                dve.wait_ge(*pe_lin.at(s, it, "k"))
                for c in range(C):
                    last = dve.tensor_scalar(o.kf[:, c, :], G[:, s, 1, c * T:(c + 1) * T], vec("bk3")[:, c:c + 1],
                                             None, ALU.add)
                last.then_inc(*dve_lin.inc(s, "k"))
                dve.wait_ge(*dve_lin.at(s, it, "k"))
                dve.tensor_reduce(o.nk[:, :], o.kf, AX, ALU.max, negate=True).then_inc(*dve_lin.inc(s, "nk"))

            def lin_v(it, s, o):
                dve.wait_ge(*pe_lin.at(s, it, "v"))
                dve.tensor_tensor(o.vt, G[:, s, 0, :].rearrange("p (t n) -> p t n", t=TT),
                                  row("bv3").unsqueeze(1).to_broadcast([P, TT, D]), ALU.add)\
                    .then_inc(*dve_lin.inc(s, "v"))

            def lin_soft(it, s, o):
                groups = o.q3.rearrange("p t (h l) -> p (t h) l", l=DH)
                dve.wait_ge(*act_lin.at(s, it, "eq"))
                dve.tensor_reduce(o.sm[:, :], groups, AX, ALU.add).then_inc(*dve_lin.inc(s, "sm"))
                dve.wait_ge(*dve_lin.at(s, it, "sm"))
                dve.reciprocal(o.ri[:, :], o.sm[:, :]).then_inc(*dve_lin.inc(s, "ri"))
                dve.wait_ge(*dve_lin.at(s, it, "ri"))
                dve.tensor_tensor(groups, groups, o.ri[:, :].unsqueeze(2).to_broadcast([P, 2 * H, DH]),
                                  ALU.mult).then_inc(*dve_lin.inc(s, "p"))
                dve.wait_ge(*act_lin.at(s, it, "ek"))
                dve.reciprocal(o.nk[:, :], o.ks[:, :]).then_inc(*dve_lin.inc(s, "rk"))

            def lin_ctx(it, s, o):
                dve.wait_ge(*pe_lin.at(s, it, "ctx"))
                dve.wait_ge(*dve_lin.at(s, it, "rk"))
                for c in range(C):
                    last = dve.scalar_tensor_tensor(out=o.ctx[:, c, :], in0=G[:, s, 1, c * P:(c + 1) * P],
                                                    scalar=o.nk[:, c:c + 1],
                                                    in1=blk16[:, :, :].rearrange("p h l -> p (h l)"),
                                                    op0=ALU.mult, op1=ALU.mult)
                last.then_inc(*dve_lin.inc(s, "ctx"))

            def lin_silu(it, s, o):
                dve.wait_ge(*act_lin.at(s, it, "tanh"))
                dve.scalar_tensor_tensor(out=o.sq[:, :, :], in0=o.sq[:, :, :], scalar=1.0, in1=o.xm[:, :, :],
                                         op0=ALU.add, op1=ALU.mult).then_inc(*dve_lin.inc(s, "s"))

            def lin_out(it, s, o):
                dve.wait_ge(*pe_lin.at(s, it, "o"))
                for c in range(C):
                    last = dve.tensor_scalar(o.xc[:, c, :], G[:, s, 1, c * T:(c + 1) * T], vec("ob3")[:, c:c + 1],
                                             o.par[:, GATE - NLOW + c:GATE - NLOW + c + 1], ALU.add, ALU.mult)
                last.then_inc(*dve_lin.inc(s, "t"))
                dve.wait_ge(*dve_lin.at(s, it, "t"))
                dve.tensor_tensor(o.xc[:, :, :], o.xc[:, :, :], o.x2[:, :, :], ALU.add)\
                    .then_inc(*dve_lin.inc(s, "out"))

            def att_gate(it, s, o):
                gated(it, s, o, dve_att, pe_att.at(s, it, "o"), ("t", "x3"), 1, "bo2", 2, o.x2, o.x1)

            def mlp_gate(it, s, o):
                gated(it, s, o, dve_mlp, pe_mlp.at(s, it, "w2"), ("t", "x4"), 0, "mb2", 5, o.x1, o.x2)

            def norm_0(it, s, o):
                dve.wait_ge(*pool_p.at(s, it, "par"))
                scale(it, s, o, 0, mod(o, 1), mod(o, 0))

            run(dve, {
                "low1": low_1, "adj": gat_adj, "low3": low_3, "low4": low_4, "sum": gat_zrow, "self": gat_self,
                "gq0": lambda it, s, o: gat_query(it, s, o, 0, o.gq), "gk": gat_keys,
                "gq1": lambda it, s, o: gat_query(it, s, o, 1, o.gq1), "gv": gat_vals,
                **each("s", gat_soft, TT), **each("r", gat_sums, TT), "pv": gat_out,
                "n0a": lambda it, s, o: centre(it, s, o, 0, o.x2), "n0b": norm_0,
                "q": lambda it, s, o: att_qk(it, s, o, 0), "k": lambda it, s, o: att_qk(it, s, o, 1),
                "v": att_v, "r": att_rest, "c": att_part_3, **each("m", att_max, 8),
                "mx": att_negmax, "ot": att_norm, "wo": att_gate,
                "n1a": lambda it, s, o: centre(it, s, o, 1, o.x1),
                "n1b": lambda it, s, o: scale(it, s, o, 1, mod(o, 4), mod(o, 3)),
                "w2b": mlp_gate,
                "n2a": lambda it, s, o: centre(it, s, o, 2, o.x2),
                "n2b": lambda it, s, o: scale(it, s, o, 2, vec("n3g"), vec("n3b")),
                "lq": lin_q, "lk": lin_k, "lv": lin_v, "ls": lin_soft, "lc": lin_ctx,
                "n3a": lambda it, s, o: centre(it, s, o, 3, o.yF),
                "n3b": lambda it, s, o: scale(it, s, o, 3, o.par[:, AFF - NLOW:AFF - NLOW + C],
                                              o.par[:, AFF - NLOW + C:AFF - NLOW + 2 * C]),
                "tanh": lin_silu, "lo": lin_out})


def kernel(**inputs):
    import numpy as np
    import concourse.bacc as bacc
    from concourse.bass_utils import run_bass_kernel_spmd

    x = {k: np.asarray(v) for k, v in inputs.items()}

    def rows(a):
        a = np.asarray(a)
        return a.reshape(-1, P, a.shape[1]).transpose(1, 0, 2).reshape(P, -1)

    def cols(v):
        return np.asarray(v).reshape(-1, P).T

    def by_channel(a):
        a = np.asarray(a)
        return a.reshape(*a.shape[:-1], H, DH).swapaxes(-1, -2).reshape(a.shape)

    L1, L2, L3 = "L1_cond_", "L2_cond_", "L3_cond_"
    w_self = x[L1 + "W_self"].T
    packs = {
        "self": rows(w_self[:D]),
        "gq": np.concatenate([rows(m.T) for m in x[L1 + "Wq"]], axis=1),
        "gk": np.concatenate([rows(m.T) for m in x[L1 + "Wk"]], axis=1),
        "gv": rows(x[L1 + "Wout"].transpose(3, 0, 1, 2).reshape(D, 2 * D)),
        "q2": rows(by_channel(x[L2 + "Wq"])), "k2": rows(by_channel(x[L2 + "Wk"])), "v2": rows(x[L2 + "Wv"]), "o2": rows(x[L2 + "Wo"]),
        "w1": rows(x[L2 + "W1"]), "w2": rows(x[L2 + "W2"]),
        "q3": rows(x[L3 + "Wq"]), "k3": rows(x[L3 + "Wk"]), "v3": rows(x[L3 + "Wv"]), "o3": rows(x[L3 + "out_W"]),
    }
    w_pack = np.concatenate([packs[k] for k in W_COLS], axis=1)
    vecs = {
        "ln_g": cols(x["L0_cond_ln_g"]), "ln_b": cols(x["L0_cond_ln_b"]), "b1": cols(x["L0_cond_b1"]),
        "b2": x["L0_cond_b2"].reshape(4, C, P, RANK).transpose(2, 0, 1, 3).reshape(P, 64),
        "bself": cols(x[L1 + "b_self"]), "gbq": cols(x[L1 + "bq"].reshape(-1)), "gbk": cols(x[L1 + "bk"].reshape(-1)),
        "gbout": cols(x[L1 + "bout"].reshape(-1)), "bc": cols(x[L2 + "bc"]), "bq2": cols(by_channel(x[L2 + "bq"])),
        "bk2": cols(by_channel(x[L2 + "bk"])), "bo2": cols(x[L2 + "bo"]), "mb1": cols(x[L2 + "b1"]), "mb2": cols(x[L2 + "b2"]),
        "n3g": cols(x[L3 + "norm_g"]), "n3b": cols(x[L3 + "norm_b"]), "bk3": cols(x[L3 + "bk"]),
        "embb": cols(x[L3 + "emb_b"]), "sng": cols(x[L3 + "sn_g"]), "snb": cols(x[L3 + "sn_b"]),
        "ob3": cols(x[L3 + "out_b"]),
        "cond": x["cond_1024"].T.reshape(C, P, B).transpose(1, 0, 2).reshape(P, C * B),
    }
    v_pack = np.concatenate([vecs[k] for k in V_COLS], axis=1)
    r_pack = np.concatenate([x[L2 + "bv"], x[L3 + "bq"], x[L3 + "bv"], x[L1 + "w_bias"],
                             x[L1 + "b_bias"].reshape(1)])[None, :]
    s_pack = np.concatenate([rows(w_self[D:]), rows(x["L0_cond_W1"]), rows(x[L2 + "Wc"]), rows(x[L3 + "emb_W"])], axis=1)
    low = x["L0_cond_W2"].reshape(C, P, 4, C, P, RANK).transpose(2, 1, 0, 3, 5, 4).reshape(4, P, C, 2048)
    adj = x["mask_BxSxSx11_ik0"]
    adj = np.stack([adj[:, :, :M], adj[:, :M].transpose(0, 2, 1, 3)], axis=2).reshape(B, T, 2 * M * NL)
    x_f = x["x"].transpose(0, 2, 1).reshape(B, C, P, T).transpose(0, 2, 1, 3)

    nc = bacc.Bacc("TRN2", target_bir_lowering=False, num_devices=1)
    arrays, args = {}, []
    for name, a in (("x", x_f), ("cond", x["cond_1024"]), ("adj", adj), ("w", w_pack), ("v", v_pack), ("r", r_pack),
                    ("s", s_pack), ("low", low)):
        arrays[f"in_{name}"] = np.ascontiguousarray(a)
        args.append(nc.dram_tensor(f"in_{name}", list(a.shape), mybir.dt.from_np(a.dtype), kind="ExternalInput").ap())
    args.append(nc.dram_tensor("out_x", [B, P, C, T], F32, kind="ExternalOutput").ap())
    nc.disable_value_cache = True
    build(nc, *args)
    r = run_bass_kernel_spmd(nc, [arrays], core_ids=[0])
    y = r.results[0]["out_x"]
    return y.transpose(0, 3, 2, 1).reshape(B, T, D)
```

```python
from contextlib import ExitStack

import concourse.bass as bass
from concourse import mybir

F32 = mybir.dt.float32
BF16 = mybir.dt.bfloat16
I32 = mybir.dt.int32
ALU = mybir.AluOpType
ACT = mybir.ActivationFunctionType
AX = mybir.AxisListType.X

B, T, D = 16, 256, 256
P = 128
C = D // P
TT = T // P
H = 16
DH = D // H
HC = P // DH
RANK = 8
M = 20
MP = 24
NL = 11
MLP = 4 * D
EPS = 1e-5
NEG = -9000000000000000.0
SLOTS = 2
PAIRS = B // SLOTS
SPLIT_Q = (0, 0, 1, 1, 0, 2)
SPLIT_K = (0, 1, 0, 1, 2, 0)
KS = DH * len(SPLIT_Q)
KM = KS + 2
N_STACK = 4 + 3 + 1

ORDER = {
    "PE": '''
        L:n2a A:v L:n2b L:lq L:lk L:lv A:m0 A:m1 L:lqt L:lkt A:m2 A:m3 L:lc A:m4 A:x0 L:ly A:m5 L:n3a A:m6 A:m7
        L:n3b A:x1 A:e0 A:e1 L:lo A:e2 A:e3 A:p0 A:e4 A:e5 F:low1 A:p1 F:low2 A:e6 A:e7 F:low3 A:p2 F:low4 A:p3
        F:sum F:self A:ot F:gq0 A:yt F:gk A:wo F:gq1 F:gv A:n1a F:s0 A:n1b F:s1 A:h0 A:h1 F:t0 A:h2 F:t1 A:h3 F:pv
        A:w2a F:n0a F:n0b A:w2b F:q F:k
    '''.split(),
    "DVE": '''
        L:n2a A:cq A:rk A:v A:ck L:n2b L:lq L:lk L:lv L:ls A:m0 A:m1 A:m2 A:m3 L:lc A:m4 A:x0 A:m5 L:n3a A:m6 A:m7
        L:n3b A:x1 L:tanh L:lo F:low1 F:adj F:low3 F:low4 F:sum F:self A:ot F:gq0 F:gk A:wo F:gq1 F:gv A:n1a F:s0
        A:n1b F:s1 F:r0 F:r1 F:pv F:n0a F:n0b A:w2b F:q F:rq F:k
    '''.split(),
    "ACT": '''
        L:n2a A:rk L:n2b L:lq L:lk L:lqt L:lkt L:ly L:n3a L:n3b A:gelu L:tanh A:exp A:e0 A:e1 A:e2 A:e3 A:e4 L:lo
        A:e5 A:gelu F:low2 A:exp A:e6 A:e7 A:p3 A:yt A:n1a A:n1b F:s0 F:s1 A:gelu A:h0 A:h1 F:t0 A:h2 F:t1 A:h3
        F:n0a A:exp F:n0b F:q F:rq F:k
    '''.split(),
    "POOL": '''
        F:load F:par F:r0 F:r1
    '''.split(),
}


W_COLS = {}
_at = 0
for _name, _n in (("self", C * D), ("gq", 2 * C * D), ("gk", 2 * C * D), ("gv", C * 2 * D),
                  ("q2", C * D), ("k2", C * D), ("v2", C * D), ("o2", C * D),
                  ("w1", C * MLP), ("w2", MLP // P * D),
                  ("q3", C * D), ("k3", C * D), ("v3", C * D), ("o3", C * D)):
    W_COLS[_name] = (_at, _n)
    _at += _n
W_TOTAL = _at
V_COLS = {}
_at = 0
for _name, _n in (("ln_g", C), ("ln_b", C), ("b1", C), ("b2", 64), ("bself", C), ("gbq", 2 * C), ("gbk", 2 * C),
                  ("gbout", 2 * C), ("bc", 6 * C), ("bq2", C), ("bk2", C), ("bo2", C), ("mb1", MLP // P),
                  ("mb2", C), ("n3g", C), ("n3b", C), ("bk3", C), ("embb", 2 * C), ("sng", C), ("snb", C),
                  ("ob3", C), ("cond", C * B)):
    V_COLS[_name] = (_at, _n)
    _at += _n
V_TOTAL = _at
R_COLS = {"bv2": (0, D), "bq3": (D, D), "bv3": (2 * D, D), "wl": (3 * D, NL), "bb": (3 * D + NL, 1)}
R_TOTAL = 3 * D + NL + 1
S_COLS = {"selfq": (0, C * D), "w1": (C * D, C * D), "wc": (2 * C * D, C * 6 * D), "emb": (8 * C * D, C * 2 * D)}
S_TOTAL = 10 * C * D
NLOW = 4 * C * RANK
MOD = NLOW
AFF = MOD + 6 * C
GATE = AFF + 2 * C
QRY = GATE + C
NPAR = QRY + C


class Progress:

    def __init__(self, sems, names):
        self.sems, self.names = sems, names
        self.next = [0] * len(sems)

    def inc(self, s, name):
        assert self.names[self.next[s] % len(self.names)] == name, (name, self.names[self.next[s] % len(self.names)])
        self.next[s] += 1
        return self.sems[s], 1

    def at(self, s, it, name):
        return self.sems[s], it * len(self.names) + self.names.index(name) + 2

    def before(self, s, it, name):
        return self.sems[s], (it - 1) * len(self.names) + self.names.index(name) + 2

    def past(self, s, it):
        return self.sems[s], it * len(self.names) + 1

    def begin(self, engine):
        for sem in self.sems:
            engine.sem_inc(sem, 1)


def build(nc, x_in, cond_in, adj_in, w_in, v_in, r_in, s_in, low_in, out):
    ctx = ExitStack()
    with ctx:
        def sb(name, shape, dt=F32):
            return ctx.enter_context(nc.sbuf_tensor(name, shape, dt))

        def sem(name):
            return ctx.enter_context(nc.semaphore(name))

        def progress(name, names):
            return Progress([sem(f"{name}_{s}") for s in range(SLOTS)], names.split())

        W = sb("W", [P, W_TOTAL])
        V = sb("V", [P, V_TOTAL])
        R = sb("R", [P, R_TOTAL])
        par_all = sb("par_all", [P, B, NPAR])
        ident = sb("ident", [P, P])
        mean_w = sb("mean_w", [P, P])
        eps_c = sb("eps_c", [P, 1])
        ones_b = sb("ones_b", [P, 2 * H * T // P], BF16)
        blk16 = sb("blk16", [P, HC, DH])
        blk24 = sb("blk24", [4 * MP, 4, DH])
        probs = sb("probs", [P, 4, 4, T])

        def w(name, a):
            lo, n = W_COLS[name]
            return W[:, lo:lo + n].rearrange("p (a n) -> p a n", a=a)

        def vec(name):
            lo, n = V_COLS[name]
            return V[:, lo:lo + n]

        def row(name):
            lo, n = R_COLS[name]
            return R[:, lo:lo + n]

        class Slot:
            pass

        SL = []
        for s in range(SLOTS):
            o = Slot()

            def own(name, shape, dt=F32, s=s):
                return sb(f"{name}{s}", shape, dt)

            o.par_low = own("par_low", [P, NLOW])
            o.par = own("par", [P, NPAR - NLOW])
            o.x = own("x", [P, C, T])
            o.x1 = own("x1_", [P, C, T])
            o.x2 = own("x2_", [P, C, T])
            o.xc = own("xc", [P, C, T])
            o.sq = own("sq", [P, C, T])
            o.rstd = own("rstd", [P, T])
            o.xm = own("xm", [P, C, T])
            o.big = own("big", [P, 8, T])
            o.bbT = own("bbT", [P, 2, C, P])
            o.y1 = own("y1_", [P, T])
            o.zq = own("zq", [P, C, T])
            o.sfrep = own("sfrep", [P, C, 4, MP])
            o.kb = own("kb", [P, 2 * C, M])
            o.cond = own("cond_", [P, TT, 2 * M])
            o.mask = own("mask", [P, TT, 2 * M])
            o.bias = own("bias", [P, TT, 2 * M])
            o.mx = own("mx", [P, 2 * H])
            o.sm = own("sm", [P, 2 * H])
            o.ri = own("ri", [P, 2 * H])
            o.stack = own("stack", [P, 2 * H * T], BF16)
            o.parts = own("parts", [P, 3 * 2 * C * T], BF16)
            o.vp = own("vp", [P, TT, H, 2 * DH])
            o.yF = own("yF", [P, C, T])
            o.mx2 = own("mx2_", [P, TT, H])
            o.nmx = own("nmx", [H // 2, 2, 2, T], BF16)
            o.ks = own("ks", [P, C])
            o.nk = own("nk", [P, C])
            o.ctx = own("ctx_", [P, C, P])
            st = o.stack[:, :].bitcast(F32)
            o.adj = st[:, 0:880].bitcast(I32).rearrange("p (t n) -> p t n", t=TT)
            o.adjw = st[:, 880:1760].rearrange("p (t n) -> p t n", t=TT)
            o.S = st[:, 1760:1760 + 2 * H * M].rearrange("p (g m) -> p g m", m=M)
            o.gq = st[:, 2400:2400 + C * T].rearrange("p (c t) -> p c t", c=C)
            o.kbd = st[:, 2912:2912 + 2 * C * HC * M].rearrange("p (g h m) -> p g h m", h=HC, m=M)
            o.sf = st[:, 3552:3552 + C * T].rearrange("p (c t) -> p c t", c=C)
            o.gq1 = o.xm
            o.st = o.stack[:, :].rearrange("p (k h t) -> p k h t", k=2, h=H)
            o.qk = o.big[:, 0:4, :].rearrange("p (k c) t -> p k c t", k=2)
            o.rest = o.big[:, 4:8, :].rearrange("p (k c) t -> p k c t", k=2)
            o.part = o.parts[:, :].rearrange("p (j k c t) -> p j k c t", j=3, k=2, c=C)
            pf = o.parts[:, :].bitcast(F32)
            o.P = pf[:, :].rearrange("p (t h m) -> p t h m", t=TT, m=MP)
            o.oraw = pf[:, 0:1024].rearrange("p (g t) -> p g t", g=4)
            o.yq = pf[:, 1024:1536].rearrange("p (g l) -> p g l", l=DH)
            o.kT = pf[:, 0:512].rearrange("p (t c) -> p t c", t=TT)
            o.vt = pf[:, 512:1024].rearrange("p (t c) -> p t c", t=TT)
            o.ke = pf[:, 1024:1536].rearrange("p (c t) -> p c t", c=C)
            o.PT = o.big
            o.vbd = o.yF[0:4 * MP, :, :].rearrange("p a n -> p (a n)").rearrange("p (g n) -> p g n", g=8)
            o.h = o.big
            o.q3 = o.big[:, 0:2, :]
            o.q3s = o.big[:, 2:4, :]
            o.kf = o.big[:, 4:6, :]
            SL.append(o)

        G = ctx.enter_context(nc.psum_tensor("G", [P, SLOTS, 2, 512], F32))
        SS = ctx.enter_context(nc.psum_tensor("SS", [P, 2, 1024], F32))
        scr = [nc.dram_tensor(f"scr{s}", [3, 2, C * P, T], BF16, kind="Internal").ap() for s in range(SLOTS)]
        ones_d = nc.dram_tensor("ones_d", [2, H * T], BF16, kind="Internal").ap()

        start_w = probs[:, :, :, :].rearrange("p a b t -> p (a b t)")
        sw_f = SL[1].big[:, 0:4, :].rearrange("p a t -> p (a t)")

        def sw(name, a):
            lo, n = S_COLS[name]
            src = start_w[:, lo:lo + n] if lo + n <= 4096 else sw_f[:, lo - 4096:lo + n - 4096]
            return src.rearrange("p (a n) -> p a n", a=a)

        low_w = [SL[s].stack[:, :].bitcast(F32).rearrange("p (c n) -> p c n", c=C) for s in range(SLOTS)]
        ct = sb("ct", [B, D])
        cstat = sb("cstat", [B, 16])
        cT = sb("cT", [P, C, B])
        hT = sb("hT", [P, C, 32])
        wsb = SL[0].big[:, 0:2, :].rearrange("p a t -> p (a t)")
        sil = sb("sil", [P, C * B])
        sil2 = sb("sil2", [P, C * B])
        e1 = sb("e1", [P, 2 * C, B])

        ld_small = sem("ld_small")
        ld_start = sem("ld_start")
        ld_low = [sem(f"ld_low{i}") for i in range(2)]
        ld_w = sem("ld_w")
        ld_x = [sem(f"ld_x{s}") for s in range(SLOTS)]
        ld_adj = [sem(f"ld_adj{s}") for s in range(SLOTS)]
        first_out = [sem(f"first_out{s}") for s in range(SLOTS)]
        third_out = [sem(f"third_out{s}") for s in range(SLOTS)]
        stacked = [sem(f"stacked{s}") for s in range(SLOTS)]
        stored = [sem(f"stored{s}") for s in range(SLOTS)]
        ones_out = sem("ones_out")
        maxima = [[sem(f"maxima{i}_{s}") for s in range(SLOTS)] for i in range(2)]
        const_done = sem("const_done")
        pool_mask = sem("pool_mask")
        pre_pe = sem("pre_pe")
        pre_dve = sem("pre_dve")
        pre_act = sem("pre_act")

        pool_p = progress("pool_par", "low par pads")
        pool_g = progress("pool_gat", "p0 p1")
        pe_low = progress("pe_low", "bb y1 y2 z x1")
        act_low = progress("act_low", "g")
        dve_low = progress("dve_low", "bb y1 z x1")
        pe_gat = progress("pe_gat", "sum self q0 k q1 v s0 s1 t0 t1 pv")
        act_gat = progress("act_gat", "e0 e1 t0 t1")
        dve_gat = progress("dve_gat", "cond adjw vb mask neg bias zq sf sfrep q0 kb kbd q1 vbd "
                           "m0 a0 x0 d0 m1 a1 x1 d1 s0 r0 s1 r1 o0 o1 x2")
        LN = "mean var"
        pe_ln = [progress(f"pe_ln{i}", LN) for i in range(4)]
        act_ln = [progress(f"act_ln{i}", "sq ln rstd") for i in range(4)]
        dve_ln = [progress(f"dve_ln{i}", "xc xn xm") for i in range(4)]
        pe_att = progress("pe_att", "q k v m0 m1 m2 m3 m4 x0 m5 m6 m7 x1 "
                          + " ".join(f"e{u}" + (f" p{u // 2 - 1}" if u % 2 and u > 1 else "") for u in range(8))
                          + " p3 ot yt o")
        act_att = progress("act_att", "c1q c2q c1k c2k " + " ".join(f"e{u}" for u in range(8)) + " o y")
        dve_att = progress("dve_att", "q rq k cq rk vp ck m0 m1 m2 m3 m4 hi0 lo0 m5 m6 m7 hi1 lo1 ri yq t x3")
        pe_mlp = progress("pe_mlp", "h0 h1 h2 h3 w2")
        act_mlp = progress("act_mlp", "h0 h1 h2 h3")
        dve_mlp = progress("dve_mlp", "t x4")
        pe_lin = progress("pe_lin", "q k v qT kT ctx y o")
        act_lin = progress("act_lin", "eq ek qT kT y tanh")
        dve_lin = progress("dve_lin", "q mx d k nk v sm ri p rk ctx s t out")

        N_CONST = 7 + SLOTS * 4
        PART_DONE, PART_STORED = (4, 6, 9, 11), (10, 11, 16, 17)
        block = ctx.enter_context(nc.Block())

        def each(name, stage, n):
            return {f"{name}{i}": (lambda it, s, o, i=i: stage(it, s, o, i)) for i in range(n)}

        def phase(engine, order, stages, a, lin, first):
            parts = {"A": a, "L": lin, "F": first}
            for part, name in (step.split(":") for step in order):
                if parts[part] is not None:
                    it, s = parts[part]
                    stages[name](it, s, SL[s])

        def run(engine, order, stages):
            last = PAIRS - 1
            phase(engine, order, stages, None, None, (0, 0))
            phase(engine, order, stages, (0, 0), None, (0, 1))
            with engine.Fori(0, last) as it:
                phase(engine, order, stages, (it, 1), (it, 0), (it + 1, 0))
                phase(engine, order, stages, (it + 1, 0), (it, 1), (it + 1, 1))
            phase(engine, order, stages, (last, 1), (last, 0), None)
            phase(engine, order, stages, None, (last, 1), None)


        @block.sync
        def _(sp):
            sp.dma_start(V[:, :], v_in).then_inc(ld_small, 16)
            sp.dma_start(ct[:, :], cond_in).then_inc(ld_small, 16)
            sp.dma_start(R[:, :], r_in.to_broadcast([P, R_TOTAL])).then_inc(ld_small, 16)
            sp.dma_start(start_w[:, 0:4096], s_in[:, 0:4096]).then_inc(ld_start, 16)
            sp.dma_start(sw_f, s_in[:, 4096:]).then_inc(ld_start, 16)
            sp.wait_ge(const_done, N_CONST)
            sp.dma_start(ones_d.rearrange("a (p n) -> (a p) n", n=2 * H * T // P), ones_b[:, :]).then_inc(ones_out, 16)
            for p in range(4):
                if p >= 2:
                    sp.wait_ge(pre_pe, PART_DONE[p - 2])
                sp.dma_start(low_w[p % 2], low_in[p]).then_inc(ld_low[p % 2], 16)
            sp.wait_ge(ones_out, 16)

            def snapped(pair):
                sm, n = pair
                return sm, n if isinstance(n, int) else sp.snap(n)

            def stack_counts(it, s):
                return [snapped(x) for x in (act_att.at(s, it, "c1k"), act_att.at(s, it, "c2k"), dve_att.at(s, it, "ck"),
                                             dve_gat.at(s, it, "x2"), (first_out[s], it * 32 + 32),
                                             (third_out[s], it * 16 + 16))]

            def stack(s, counts):
                o = SL[s]
                first, second, third, graph_read, first_two_out, last_out = counts
                sp.wait_ge(*graph_read)
                sp.dma_start(o.st[KS:KM, 1, :, :].rearrange("p h t -> p (h t)"), ones_d).then_inc(stacked[s], 16)
                for j, (ready, out_sem) in enumerate(((first, first_out), (second, first_out), (third, third_out))):
                    sp.wait_ge(*ready)
                    sp.dma_start(scr[s][j].rearrange("k (c p) t -> p (k c) t", p=P),
                                 o.part[:, j].rearrange("p k c t -> p (k c) t"))\
                        .then_inc(out_sem[s], 16)

                def gather(k, j, n, src):
                    sp.dma_start(o.st[j * DH:(j + n) * DH, k, :, :].rearrange("p h t -> p (h t)"), src)\
                        .then_inc(stacked[s], 16)

                def rows_of(k, parts):
                    return scr[s][parts, k].rearrange("j (c h) t -> j c (h t)", c=DH)

                sp.wait_ge(*first_two_out)
                for j in range(2):
                    gather(0, 2 * j, 2, rows_of(0, slice(j, j + 1)).to_broadcast([2, DH, H * T]))
                    gather(1, 2 * j, 2, rows_of(1, slice(0, 2)))
                sp.wait_ge(*last_out)
                gather(0, 4, 2, rows_of(0, slice(0, 3, 2)))
                for j in (4, 5):
                    gather(1, j, 1, rows_of(1, slice(SPLIT_K[j], SPLIT_K[j] + 1)))

            def negmax_counts(it, s):
                return [snapped(dve_att.at(s, it, f"lo{i}")) for i in range(2)]

            def negmax(s, counts):
                for i, count in enumerate(counts):
                    sp.wait_ge(*count)
                    for j in range(2):
                        sp.dma_start(SL[s].st[KS + j:KS + j + 1, 0, i * H // 2:(i + 1) * H // 2, :],
                                     SL[s].nmx[:, i, j, :]).then_inc(maxima[i][s], 16)

            last = PAIRS - 1
            stack(0, stack_counts(0, 0))
            negmax(0, negmax_counts(0, 0))
            stack(1, stack_counts(0, 1))
            with sp.Fori(0, last) as it:
                counts = [negmax_counts(it, 1), stack_counts(it + 1, 0), negmax_counts(it + 1, 0), stack_counts(it + 1, 1)]
                negmax(1, counts[0])
                stack(0, counts[1])
                negmax(0, counts[2])
                stack(1, counts[3])
            negmax(1, negmax_counts(last, 1))
            for s in range(SLOTS):
                sp.wait_ge(stored[s], 16 * (PAIRS + 1))

        @block.gpsimd
        def _(pool):
            for p in (pool_p, pool_g):
                p.begin(pool)
            def mark(ins):
                ins.then_inc(const_done, 1)

            n = 0
            pool.memset(ident[:, :], 0.0).then_inc(pool_mask, 1)
            n += 1
            for t in (blk16[:, :, :], blk24[:, :, :]):
                pool.memset(t, 1.0).then_inc(pool_mask, 1)
                n += 1
            pool.wait_ge(pool_mask, n)
            mark(pool.affine_select(out=ident[:, :], in_=ident[:, :], compare_op=ALU.not_equal, fill=1.0, base=0,
                                    pattern=[[-1, P]], channel_multiplier=1))
            for t, size, g in ((blk16, DH, HC), (blk24, MP, 4)):
                pool.affine_select(out=t[:, :, :], in_=t[:, :, :], compare_op=ALU.is_ge, fill=0.0, base=0,
                                   pattern=[[-size, g], [0, DH]], channel_multiplier=1).then_inc(pool_mask, 1)
                n += 1
                pool.wait_ge(pool_mask, n)
                mark(pool.affine_select(out=t[:, :, :], in_=t[:, :, :], compare_op=ALU.is_ge, fill=0.0, base=size - 1,
                                        pattern=[[size, g], [0, DH]], channel_multiplier=-1))
            mark(pool.memset(mean_w[:, :], 1.0 / D))
            mark(pool.memset(ones_b[:, :], 1.0))
            mark(pool.memset(eps_c[:, :], EPS))
            mark(pool.memset(hT[:, :, :], 0.0))
            for o in SL:
                for t in (o.bbT[:, :, :, :], o.y1[:, :], o.sfrep[:, :, :, :]):
                    mark(pool.memset(t, 0.0))
                mark(pool.memset(o.vp[:, :, :, :], 1.0))
            def load(it, s, o):
                b = it * SLOTS + s
                pool.wait_ge(*dve_low.past(s, it))
                pool.dma_start(o.x[:, :, :], x_in[bass.ds(b, 1)].rearrange("o p c t -> p (o c) t")).then_inc(ld_x[s], 16)
                if isinstance(it, int) and it == 0:
                    pool.wait_ge(pre_dve, 17)
                pool.wait_ge(*pe_att.past(s, it))
                pool.dma_start(o.adj, adj_in[bass.ds(b, 1)].rearrange("o (t p) n -> p (o t) n", p=P)).then_inc(ld_adj[s], 16)
                pool.wait_ge(*pe_low.past(s, it))
                pool.tensor_copy(o.par_low[:, :], par_all[:, bass.ds(b, 1), 0:NLOW].rearrange("p o n -> p (o n)"))\
                    .then_inc(*pool_p.inc(s, "low"))

            def params(it, s, o):
                b = it * SLOTS + s
                pool.wait_ge(*dve_lin.past(s, it))
                pool.tensor_copy(o.par[:, :], par_all[:, bass.ds(b, 1), NLOW:NPAR].rearrange("p o n -> p (o n)"))\
                    .then_inc(*pool_p.inc(s, "par"))
                pool.memset(o.P[:, :, :, M:MP], 0.0).then_inc(*pool_p.inc(s, "pads"))

            def gat_norm(it, s, o, t):
                pool.wait_ge(*dve_gat.at(s, it, f"r{t}"))
                pool.tensor_tensor(o.P[:, t, :, 0:M], o.P[:, t, :, 0:M],
                                   o.ri[:, :].unsqueeze(2).to_broadcast([P, 2 * H, M]), ALU.mult)\
                    .then_inc(*pool_g.inc(s, f"p{t}"))

            run(pool, ORDER["POOL"], {
                "load": load, "par": params, **each("r", gat_norm, TT)})

        @block.tensor
        def _(pe):
            for p in (pe_low, pe_gat, *pe_ln, pe_att, pe_mlp, pe_lin):
                p.begin(pe)
            def mm(out_, lhsT, rhs, start=True, stop=True):
                return pe.matmul(out_, lhsT, rhs, start=start, stop=stop)

            def dense_f(bank, wt, src, cols=C, n=T):
                for m in range(cols):
                    for c in range(C):
                        last = mm(bank[:, m * n:(m + 1) * n], wt[:, c, m * P:(m + 1) * P], src[:, c, :],
                                  c == 0, c == C - 1)
                return last

            def dense_t(bank, wt, src):
                for t in range(TT):
                    for c in range(C):
                        last = mm(bank[:, t * D:(t + 1) * D], src[:, c, t * P:(t + 1) * P], wt[:, c, :],
                                  c == 0, c == C - 1)
                return last

            A0, A1, A2, A3 = SS[:, 0, 0:512], SS[:, 0, 512:1024], SS[:, 1, 0:512], SS[:, 1, 512:1024]
            pe.wait_ge(const_done, N_CONST)
            pe.wait_ge(ld_start, 32)
            pe.wait_ge(ld_small, 48)
            cF = vec("cond").rearrange("p (c b) -> p c b", c=C)
            for m in range(C):
                for c in range(C):
                    last = mm(A3[:, m * B:(m + 1) * B], sw("selfq", C)[:, c, m * P:(m + 1) * P], cF[:, c, :],
                              c == 0, c == C - 1)
            last.then_inc(pre_pe, 1)
            pe.wait_ge(pre_dve, 2)
            for c in range(C):
                last = pe.transpose(A0[:, c * B:(c + 1) * B], ct[:, c * P:(c + 1) * P], ident[0:B, 0:B])
            last.then_inc(pre_pe, 1)
            pe.wait_ge(pre_dve, 7)
            for m in range(C):
                for c in range(C):
                    last = mm(A1[:, m * B:(m + 1) * B], sw("w1", C)[:, c, m * P:(m + 1) * P], cT[:, c, :],
                              c == 0, c == C - 1)
            last.then_inc(pre_pe, 1)
            def modulations():
                pe.wait_ge(pre_dve, 5)
                pe.wait_ge(pre_act, 4)
                silv = sil[:, :].rearrange("p (c b) -> p c b", c=C)
                for m in range(6 * C):
                    for c in range(C):
                        mm(A1[:, m * B:(m + 1) * B], sw("wc", C)[:, c, m * P:(m + 1) * P], silv[:, c, :],
                           c == 0, c == C - 1)
                for m in range(2 * C):
                    for c in range(C):
                        k = (6 * C + m) * B
                        last = mm(A1[:, k:k + B], sw("emb", C)[:, c, m * P:(m + 1) * P], silv[:, c, :],
                                  c == 0, c == C - 1)
                last.then_inc(pre_pe, 1)

            for p in range(4):
                if p == 2:
                    modulations()
                pe.wait_ge(ld_low[p % 2], 16 * (p // 2 + 1))
                pe.wait_ge(pre_act, 4 + p)
                for a in range(4):
                    for c in range(C):
                        last = mm(A2[32 * a:32 * a + 32, :], hT[:, c, :], low_w[p % 2][:, c, a * 512:(a + 1) * 512],
                                  c == 0, c == C - 1)
                last.then_inc(pre_pe, 1)
                pe.wait_ge(pre_act, 5 + p)
                pe.wait_ge(pre_dve, PART_STORED[p - 1] if p else 7)
                for j in range(4):
                    last = pe.transpose(A0[:, j * P:(j + 1) * P], wsb[:, j * P:(j + 1) * P], ident[:, :])
                last.then_inc(pre_pe, 1)
            pe.wait_ge(pre_dve, 17)

            def low_1(it, s, o):
                pe.wait_ge(*pool_p.at(s, it, "low"))
                if not isinstance(it, int):
                    pe.wait_ge(*dve_lin.before(s, it, "t"))
                for f in range(2):
                    for c in range(C):
                        k = (2 * f + 1) * C * RANK + c * RANK
                        last = pe.transpose(G[0:RANK, s, 1, (f * C + c) * P:(f * C + c + 1) * P],
                                            o.par_low[:, k:k + RANK], ident[:, :])
                last.then_inc(*pe_low.inc(s, "bb"))
                pe.wait_ge(ld_x[s], it * 16 + 16)
                for c in range(C):
                    last = mm(G[0:RANK, s, 0, 0:T], o.par_low[:, c * RANK:(c + 1) * RANK], o.x[:, c, :], c == 0, c == C - 1)
                last.then_inc(*pe_low.inc(s, "y1"))

            def low_2(it, s, o):
                pe.wait_ge(*dve_low.at(s, it, "y1"))
                for c in range(C):
                    last = mm(G[:, s, 0, c * T:(c + 1) * T], o.bbT[:, 0, c, :], o.y1[:, :])
                last.then_inc(*pe_low.inc(s, "y2"))

            def low_3(it, s, o):
                pe.wait_ge(*act_low.at(s, it, "g"))
                for c in range(C):
                    k = 2 * C * RANK + c * RANK
                    last = mm(G[0:RANK, s, 1, 0:T], o.par_low[:, k:k + RANK], o.xm[:, c, :], c == 0, c == C - 1)
                last.then_inc(*pe_low.inc(s, "z"))

            def low_4(it, s, o):
                pe.wait_ge(*dve_low.at(s, it, "z"))
                for c in range(C):
                    last = mm(G[:, s, 0, c * T:(c + 1) * T], o.bbT[:, 1, c, :], o.y1[:, :])
                last.then_inc(*pe_low.inc(s, "x1"))

            def gat_sum(it, s, o):
                pe.wait_ge(*dve_low.at(s, it, "x1"))
                for c in range(C):
                    last = mm(G[:, s, 1, 0:T], mean_w[:, :], o.x1[:, c, :], c == 0, c == C - 1)
                last.then_inc(*pe_gat.inc(s, "sum"))

            def gat_self(it, s, o):
                pe.wait_ge(ld_w, 32)
                for m in range(C):
                    for c in range(C):
                        last = mm(G[:, s, 0, m * T:(m + 1) * T], w("self", C)[:, c, m * P:(m + 1) * P],
                                  o.x1[:, c, :], c == 0, c == C - 1)
                last.then_inc(*pe_gat.inc(s, "self"))

            def gat_query_0(it, s, o):
                pe.wait_ge(*dve_gat.at(s, it, "sf"))
                dense_f(G[:, s, 1, :], w("gq", 2 * C)[:, 0:C, :], o.sf).then_inc(*pe_gat.inc(s, "q0"))

            def gat_keys(it, s, o):
                wk = w("gk", 2 * C)
                for d in range(2):
                    for m in range(C):
                        for c in range(C):
                            last = mm(G[:, s, 0, (d * C + m) * M:(d * C + m + 1) * M],
                                      wk[:, d * C + c, m * P:(m + 1) * P], o.sf[:, c, 0:M], c == 0, c == C - 1)
                last.then_inc(*pe_gat.inc(s, "k"))

            def gat_query_1(it, s, o):
                pe.wait_ge(*dve_gat.at(s, it, "q0"))
                dense_f(G[:, s, 1, :], w("gq", 2 * C)[:, C:2 * C, :], o.sf).then_inc(*pe_gat.inc(s, "q1"))

            def gat_vals(it, s, o):
                pe.wait_ge(*dve_gat.at(s, it, "kb"))
                pe.wait_ge(*dve_gat.at(s, it, "sfrep"))
                for c in range(C):
                    last = mm(G[0:4 * MP, s, 0, :], o.sfrep[:, c, :, :].rearrange("p a m -> p (a m)"),
                              w("gv", C)[:, c, :], c == 0, c == C - 1)
                last.then_inc(*pe_gat.inc(s, "v"))

            def gat_scores(it, s, o, t):
                pe.wait_ge(*dve_gat.at(s, it, "vbd" if t == 0 else "m0"))
                for d, q in enumerate((o.gq, o.gq1)):
                    for c in range(C):
                        last = mm(G[:, s, d, c * HC * M:(c + 1) * HC * M], q[:, c, t * P:(t + 1) * P],
                                  o.kbd[:, d * C + c, :, :].rearrange("p h m -> p (h m)"))
                last.then_inc(*pe_gat.inc(s, f"s{t}"))

            def gat_turn(it, s, o, t):
                pe.wait_ge(*pool_g.at(s, it, f"p{t}"))
                pe.wait_ge(*(dve_gat.at(s, it, "m1") if t == 0 else act_gat.at(s, it, "t0")))
                for g in range(8):
                    last = pe.transpose(G[0:4 * MP, s, g // 4, g % 4 * P:(g % 4 + 1) * P],
                                        o.P[:, t, 4 * g:4 * g + 4, :].rearrange("p h m -> p (h m)"), ident[:, :])
                last.then_inc(*pe_gat.inc(s, f"t{t}"))

            def gat_values(it, s, o):
                pe.wait_ge(*act_gat.at(s, it, "t1"))
                for g in range(4):
                    a = g % 2 * 64
                    for d in range(2):
                        last = mm(G[a:a + 64, s, 0, g // 2 * T:(g // 2 + 1) * T], o.vbd[:, d * 4 + g, :],
                                  o.PT[0:4 * MP, d * 4 + g, :], d == 0, d == 1)
                last.then_inc(*pe_gat.inc(s, "pv"))

            def mean(it, s, o, i, src, *ready):
                for r in ready:
                    pe.wait_ge(*r)
                for c in range(C):
                    last = mm(G[:, s, 1, 0:T], mean_w[:, :], src[:, c, :], c == 0, c == C - 1)
                last.then_inc(*pe_ln[i].inc(s, "mean"))

            def var(it, s, o, i):
                pe.wait_ge(*act_ln[i].at(s, it, "sq"))
                for c in range(C):
                    last = mm(G[:, s, 0, 0:T], mean_w[:, :], o.sq[:, c, :], c == 0, c == C - 1)
                last.then_inc(*pe_ln[i].inc(s, "var"))

            def att_q(it, s, o):
                pe.wait_ge(*dve_ln[0].at(s, it, "xm"))
                dense_f(G[:, s, 0, :], w("q2", C), o.xm).then_inc(*pe_att.inc(s, "q"))

            def att_k(it, s, o):
                dense_f(G[:, s, 1, :], w("k2", C), o.xm).then_inc(*pe_att.inc(s, "k"))

            def att_v(it, s, o):
                pe.wait_ge(*dve_att.at(s, it, "q"))
                dense_t(G[:, s, 0, :], w("v2", C), o.xm).then_inc(*pe_att.inc(s, "v"))

            def att_max(it, s, o, u):
                if u == 0:
                    pe.wait_ge(stacked[s], (it + 1) * 16 * N_STACK)
                if u >= 2:
                    pe.wait_ge(*dve_att.at(s, it, f"m{u - 2}"))
                elif s:
                    pe.wait_ge(*act_att.at(0, it, f"e{u + 6}"))
                else:
                    pe.wait_ge(*act_att.past(1, it))
                for k in range(2):
                    for t in range(TT):
                        h = 2 * u + k
                        last = mm(SS[:, u % 2, (k * TT + t) * T:(k * TT + t + 1) * T],
                                  o.st[0:KS, 0, h, t * P:(t + 1) * P], o.st[0:KS, 1, h, :])
                last.then_inc(*pe_att.inc(s, f"m{u}"))

            def att_turn_max(it, s, o, i):
                pe.wait_ge(*dve_att.at(s, it, f"m{4 * i + 3}"))
                for t in range(TT):
                    last = pe.transpose(G[0:H // 2, s, 1, i * T + t * P:i * T + (t + 1) * P],
                                        o.mx2[:, t, i * H // 2:(i + 1) * H // 2], ident[:, :])
                last.then_inc(*pe_att.inc(s, f"x{i}"))

            def att_exp(it, s, o, u):
                if u % 4 == 0:
                    pe.wait_ge(maxima[u // 4][s], (it + 1) * 32)
                if u >= 2:
                    pe.wait_ge(*act_att.at(s, it, f"e{u - 2}"))
                else:
                    pe.wait_ge(*dve_att.at(s, it, f"m{u + 6}"))
                for k in range(2):
                    for t in range(TT):
                        h = 2 * u + k
                        last = mm(SS[:, u % 2, (k * TT + t) * T:(k * TT + t + 1) * T],
                                  o.st[0:KM, 1, h, t * P:(t + 1) * P], o.st[0:KM, 0, h, :])
                last.then_inc(*pe_att.inc(s, f"e{u}"))

            def values(it, s, o, g):
                pe.wait_ge(*act_att.at(s, it, f"e{2 * g + 1}"))
                for t in range(TT):
                    for a in range(4):
                        u, k = (4 * g + a) // 2, a % 2
                        last = mm(G[32 * a:32 * a + 32, s, g // 2, g % 2 * T:(g % 2 + 1) * T],
                                  o.vp[:, t, 4 * g + a, :], probs[:, u % 4, k * TT + t, :], t == 0, t == TT - 1)
                last.then_inc(*pe_att.inc(s, f"p{g}"))

            def att_turn(it, s, o):
                pe.wait_ge(*act_att.at(s, it, "o"))
                for t in range(TT):
                    for g in range(4):
                        last = pe.transpose(G[:, s, t, g * P:(g + 1) * P], o.oraw[:, g, t * P:(t + 1) * P], ident[:, :])
                last.then_inc(*pe_att.inc(s, "ot"))

            def att_back(it, s, o):
                pe.wait_ge(*dve_att.at(s, it, "yq"))
                yq = o.yq.rearrange("p (t g) l -> p t (g l)", t=TT)
                for c in range(C):
                    for t in range(TT):
                        last = pe.transpose(G[:, s, 0, c * T + t * P:c * T + (t + 1) * P],
                                            yq[:, t, c * P:(c + 1) * P], ident[:, :])
                last.then_inc(*pe_att.inc(s, "yt"))

            def att_out(it, s, o):
                pe.wait_ge(*act_att.at(s, it, "y"))
                dense_f(G[:, s, 1, :], w("o2", C), o.yF).then_inc(*pe_att.inc(s, "o"))

            def mlp_up(it, s, o, i):
                if i == 0:
                    pe.wait_ge(*dve_ln[1].at(s, it, "xm"))
                if i >= 2:
                    pe.wait_ge(*act_mlp.at(s, it, f"h{i - 2}"))
                dense_f(G[:, s, i % 2, :], w("w1", C)[:, :, i * 2 * P:(i + 1) * 2 * P], o.xm)\
                    .then_inc(*pe_mlp.inc(s, f"h{i}"))

            def mlp_down(it, s, o, m):
                if m == 0:
                    pe.wait_ge(*act_mlp.at(s, it, "h3"))
                K = MLP // P
                for k in range(K):
                    last = mm(G[:, s, 0, m * T:(m + 1) * T], w("w2", K)[:, k, m * P:(m + 1) * P], o.h[:, k, :],
                              k == 0, k == K - 1)
                if m == C - 1:
                    last.then_inc(*pe_mlp.inc(s, "w2"))

            def lin_q(it, s, o):
                pe.wait_ge(*dve_ln[2].at(s, it, "xm"))
                dense_t(G[:, s, 0, :], w("q3", C), o.xm).then_inc(*pe_lin.inc(s, "q"))

            def lin_k(it, s, o):
                dense_f(G[:, s, 1, :], w("k3", C), o.xm).then_inc(*pe_lin.inc(s, "k"))

            def lin_v(it, s, o):
                pe.wait_ge(*dve_lin.at(s, it, "q"))
                dense_t(G[:, s, 0, :], w("v3", C), o.xm).then_inc(*pe_lin.inc(s, "v"))

            def lin_turn_q(it, s, o):
                pe.wait_ge(*dve_lin.at(s, it, "p"))
                for c in range(C):
                    for t in range(TT):
                        last = pe.transpose(G[:, s, 1, c * T + t * P:c * T + (t + 1) * P],
                                            o.q3[:, t, c * P:(c + 1) * P], ident[:, :])
                last.then_inc(*pe_lin.inc(s, "qT"))

            def lin_turn_k(it, s, o):
                pe.wait_ge(*act_lin.at(s, it, "ek"))
                for t in range(TT):
                    for c in range(C):
                        last = pe.transpose(G[:, s, 0, t * D + c * P:t * D + (c + 1) * P],
                                            o.ke[:, c, t * P:(t + 1) * P], ident[:, :])
                last.then_inc(*pe_lin.inc(s, "kT"))

            def lin_ctx(it, s, o):
                pe.wait_ge(*act_lin.at(s, it, "kT"))
                for c in range(C):
                    for t in range(TT):
                        last = mm(G[:, s, 1, c * P:(c + 1) * P], o.kT[:, t, c * P:(c + 1) * P],
                                  o.vt[:, t, c * P:(c + 1) * P], t == 0, t == TT - 1)
                last.then_inc(*pe_lin.inc(s, "ctx"))

            def lin_y(it, s, o):
                pe.wait_ge(*dve_lin.at(s, it, "ctx"))
                for c in range(C):
                    last = mm(G[:, s, 0, c * T:(c + 1) * T], o.ctx[:, c, :], o.q3s[:, c, :])
                last.then_inc(*pe_lin.inc(s, "y"))

            def lin_out(it, s, o):
                pe.wait_ge(*dve_lin.at(s, it, "s"))
                dense_f(G[:, s, 1, :], w("o3", C), o.sq).then_inc(*pe_lin.inc(s, "o"))

            run(pe, ORDER["PE"], {
                "low1": low_1, "low2": low_2, "low3": low_3, "low4": low_4,
                "sum": gat_sum, "self": gat_self,
                "gq0": gat_query_0, "gk": gat_keys, "gq1": gat_query_1, "gv": gat_vals,
                **each("s", gat_scores, TT), **each("t", gat_turn, TT),
                "pv": gat_values,
                "n0a": lambda it, s, o: mean(it, s, o, 0, o.x2, dve_gat.at(s, it, "x2")),
                "n0b": lambda it, s, o: var(it, s, o, 0),
                "q": att_q, "k": att_k, "v": att_v,
                **each("m", att_max, 8), **each("x", att_turn_max, 2), **each("e", att_exp, 8), **each("p", values, 4),
                "ot": att_turn, "yt": att_back, "wo": att_out,
                "n1a": lambda it, s, o: mean(it, s, o, 1, o.x1, dve_att.at(s, it, "x3")),
                "n1b": lambda it, s, o: var(it, s, o, 1),
                **each("h", mlp_up, 4),
                "w2a": lambda it, s, o: mlp_down(it, s, o, 0), "w2b": lambda it, s, o: mlp_down(it, s, o, 1),
                "n2a": lambda it, s, o: mean(it, s, o, 2, o.x2, dve_mlp.at(s, it, "x4")),
                "n2b": lambda it, s, o: var(it, s, o, 2),
                "lq": lin_q, "lk": lin_k, "lv": lin_v, "lqt": lin_turn_q, "lkt": lin_turn_k, "lc": lin_ctx, "ly": lin_y,
                "n3a": lambda it, s, o: mean(it, s, o, 3, o.yF, act_lin.at(s, it, "y")),
                "n3b": lambda it, s, o: var(it, s, o, 3),
                "lo": lin_out})

        @block.scalar
        def _(act):
            for p in (act_low, act_gat, *act_ln, act_att, act_mlp, act_lin):
                p.begin(act)
            for s in range(SLOTS):
                act.sem_inc(stored[s], 16)
            act.wait_ge(const_done, N_CONST)
            act.wait_ge(pre_dve, 1)
            act.activation(cstat[:, 8:9], cstat[:, 7:8], ACT.Ln, bias=eps_c[0:B, :]).then_inc(pre_act, 1)
            act.wait_ge(pre_act, 1)
            act.activation(cstat[:, 9:10], cstat[:, 8:9], ACT.Exp, scale=-0.5).then_inc(pre_act, 1)
            act.activation(sil2[:, :], vec("cond"), ACT.Exp, scale=-1.0).then_inc(pre_act, 1)
            A1, A2 = SS[:, 0, 512:1024], SS[:, 1, 0:512]
            act.wait_ge(pre_pe, 3)
            act.activation(hT[:, 0, 0:B], A1[:, 0:B], ACT.Gelu, bias=vec("b1")[:, 0:1])
            act.activation(hT[:, 1, 0:B], A1[:, B:2 * B], ACT.Gelu, bias=vec("b1")[:, 1:2]).then_inc(pre_act, 1)
            half = W_COLS["q2"][0]
            for p in range(4):
                act.wait_ge(pre_pe, PART_DONE[p])
                act.activation(wsb[:, :], A2, ACT.Copy).then_inc(pre_act, 1)
                if p == 1:
                    act.dma_start(W[:, 0:half], w_in[:, 0:half]).then_inc(ld_w, 16)
                    act.dma_start(W[:, half:], w_in[:, half:]).then_inc(ld_w, 16)

            def low_gelu(it, s, o):
                act.wait_ge(*pe_low.at(s, it, "y2"))
                act.activation(o.xm[:, :, :].rearrange("p c t -> p (c t)"), G[:, s, 0, :], ACT.Gelu)\
                    .then_inc(*act_low.inc(s, "g"))

            def gat_exp(it, s, o, t):
                act.wait_ge(*dve_gat.at(s, it, f"d{t}"))
                act.activation(o.P[:, t, :, 0:M], o.S, ACT.Exp).then_inc(*act_gat.inc(s, f"e{t}"))

            def gat_turned(it, s, o, t):
                act.wait_ge(*pe_gat.at(s, it, f"t{t}"))
                act.activation(o.PT[0:4 * MP, :, t * P:(t + 1) * P],
                               G[0:4 * MP, s, :, :].rearrange("p a (g n) -> p (a g) n", n=P), ACT.Copy)\
                    .then_inc(*act_gat.inc(s, f"t{t}"))

            def square(it, s, o, i):
                act.wait_ge(*dve_ln[i].at(s, it, "xc"))
                act.activation(o.sq[:, :, :], o.xc[:, :, :], ACT.Square).then_inc(*act_ln[i].inc(s, "sq"))

            def rstd(it, s, o, i):
                act.wait_ge(*pe_ln[i].at(s, it, "var"))
                act.activation(o.rstd[:, :], G[:, s, 0, 0:T], ACT.Ln, bias=eps_c[:, :])\
                    .then_inc(*act_ln[i].inc(s, "ln"))
                act.wait_ge(*act_ln[i].at(s, it, "ln"))
                act.activation(o.rstd[:, :], o.rstd[:, :], ACT.Exp, scale=-0.5).then_inc(*act_ln[i].inc(s, "rstd"))

            def att_part_1(it, s, o, k):
                name = "qk"[k]
                act.wait_ge(*dve_att.at(s, it, name))
                act.activation(o.part[:, 0, k], o.qk[:, k], ACT.Copy).then_inc(*act_att.inc(s, f"c1{name}"))

            def att_part_2(it, s, o, k):
                name = "qk"[k]
                act.wait_ge(*dve_att.at(s, it, f"r{name}"))
                act.activation(o.part[:, 1, k], o.rest[:, k], ACT.Copy).then_inc(*act_att.inc(s, f"c2{name}"))

            def att_exp(it, s, o, u):
                act.wait_ge(*pe_att.at(s, it, f"e{u}"))
                if u >= 4:
                    act.wait_ge(*pe_att.at(s, it, f"p{(u - 4) // 2}"))
                elif s:
                    act.wait_ge(*pe_att.at(0, it, f"p{u // 2 + 2}"))
                else:
                    act.wait_ge(*pe_att.past(1, it))
                act.activation(probs[:, u % 4, :, :].rearrange("p a t -> p (a t)"), SS[:, u % 2, :], ACT.Exp)\
                    .then_inc(*act_att.inc(s, f"e{u}"))

            def att_o(it, s, o):
                act.wait_ge(*pe_att.at(s, it, "p3"))
                act.activation(o.oraw.rearrange("p g t -> p (g t)"),
                               G[:, s, :, :].rearrange("p a n -> p (a n)"), ACT.Copy)\
                    .then_inc(*act_att.inc(s, "o"))

            def att_y(it, s, o):
                act.wait_ge(*pe_att.at(s, it, "yt"))
                act.activation(o.yF[:, :, :].rearrange("p c t -> p (c t)"), G[:, s, 0, :], ACT.Copy)\
                    .then_inc(*act_att.inc(s, "y"))

            def mlp_gelu(it, s, o, i):
                act.wait_ge(*pe_mlp.at(s, it, f"h{i}"))
                for k in range(2):
                    m = 2 * i + k
                    last = act.activation(o.h[:, m, :], G[:, s, i % 2, k * T:(k + 1) * T], ACT.Gelu,
                                          bias=vec("mb1")[:, m:m + 1])
                last.then_inc(*act_mlp.inc(s, f"h{i}"))

            def lin_exp_q(it, s, o):
                act.wait_ge(*dve_lin.at(s, it, "d"))
                act.activation(o.q3, o.q3, ACT.Exp).then_inc(*act_lin.inc(s, "eq"))

            def lin_exp_k(it, s, o):
                act.wait_ge(*dve_lin.at(s, it, "nk"))
                for c in range(C):
                    last = act.activation(o.ke[:, c, :], o.kf[:, c, :], ACT.Exp, bias=o.nk[:, c:c + 1],
                                          accum_out=o.ks[:, c:c + 1])
                last.then_inc(*act_lin.inc(s, "ek"))

            def lin_turned_q(it, s, o):
                act.wait_ge(*pe_lin.at(s, it, "qT"))
                act.activation(o.q3s.rearrange("p c t -> p (c t)"), G[:, s, 1, :], ACT.Copy)\
                    .then_inc(*act_lin.inc(s, "qT"))

            def lin_turned_k(it, s, o):
                act.wait_ge(*pe_lin.at(s, it, "kT"))
                act.activation(o.kT.rearrange("p t c -> p (t c)"), G[:, s, 0, :], ACT.Copy)\
                    .then_inc(*act_lin.inc(s, "kT"))

            def lin_y(it, s, o):
                act.wait_ge(*pe_lin.at(s, it, "y"))
                act.activation(o.yF[:, :, :].rearrange("p c t -> p (c t)"), G[:, s, 0, :], ACT.Copy)\
                    .then_inc(*act_lin.inc(s, "y"))

            def lin_tanh(it, s, o):
                act.wait_ge(*dve_ln[3].at(s, it, "xm"))
                act.activation(o.sq[:, :, :], o.xm[:, :, :], ACT.Tanh).then_inc(*act_lin.inc(s, "tanh"))

            def store(it, s, o):
                act.wait_ge(*dve_lin.at(s, it, "out"))
                act.dma_start(out[bass.ds(it * SLOTS + s, 1)].rearrange("o p c t -> p (o c) t"), o.xc[:, :, :])\
                    .then_inc(stored[s], 16)

            run(act, ORDER["ACT"], {
                "exp": lambda it, s, o: act.preload_act_table_set("natural_log_exp_and_others"),
                "gelu": lambda it, s, o: act.preload_act_table_set("gelu_and_others"),
                "low2": low_gelu,
                **each("s", gat_exp, TT), **each("t", gat_turned, TT),
                "n0a": lambda it, s, o: square(it, s, o, 0), "n0b": lambda it, s, o: rstd(it, s, o, 0), 
                "q": lambda it, s, o: att_part_1(it, s, o, 0), "k": lambda it, s, o: att_part_1(it, s, o, 1),
                "rq": lambda it, s, o: att_part_2(it, s, o, 0), "rk": lambda it, s, o: att_part_2(it, s, o, 1),
               
                **each("e", att_exp, 8), "p3": att_o, "yt": att_y,
                "n1a": lambda it, s, o: square(it, s, o, 1), "n1b": lambda it, s, o: rstd(it, s, o, 1), **each("h", mlp_gelu, 4),
                "n2a": lambda it, s, o: square(it, s, o, 2), "n2b": lambda it, s, o: rstd(it, s, o, 2),
                "lq": lin_exp_q, "lk": lin_exp_k, "lqt": lin_turned_q, "lkt": lin_turned_k, "ly": lin_y,
                "n3a": lambda it, s, o: square(it, s, o, 3), "n3b": lambda it, s, o: rstd(it, s, o, 3),
                "tanh": lin_tanh, "lo": store})

        @block.vector
        def _(dve):
            for p in (dve_low, dve_gat, *dve_ln, dve_att, dve_mlp, dve_lin):
                p.begin(dve)
            A0, A1, A3 = SS[:, 0, 0:512], SS[:, 0, 512:1024], SS[:, 1, 512:1024]
            n = 0

            def done(ins):
                nonlocal n
                n += 1
                ins.then_inc(pre_dve, 1)

            dve.wait_ge(ld_small, 48)
            stat = sem("stat")
            dve.bn_stats(cstat[:, 0:6], ct[:, :]).then_inc(stat, 1)
            dve.wait_ge(stat, 1)
            done(dve.bn_aggr(cstat[:, 6:8], cstat[:, 0:6]))
            dve.wait_ge(pre_act, 2)
            dve.wait_ge(pre_dve, 1)
            done(dve.tensor_scalar(ct[:, :], ct[:, :], cstat[:, 6:7], cstat[:, 9:10], ALU.subtract, ALU.mult))
            dve.wait_ge(pre_act, 3)
            done(dve.tensor_scalar(sil2[:, :], sil2[:, :], 1.0, None, ALU.add))
            dve.wait_ge(pre_dve, 3)
            done(dve.reciprocal(sil2[:, :], sil2[:, :]))
            dve.wait_ge(pre_dve, 4)
            done(dve.tensor_tensor(sil[:, :], sil2[:, :], vec("cond"), ALU.mult))
            dve.wait_ge(pre_pe, 2)
            for c in range(C):
                done(dve.tensor_scalar(cT[:, c, :], A0[:, c * B:(c + 1) * B], vec("ln_g")[:, c:c + 1],
                                       vec("ln_b")[:, c:c + 1], ALU.mult, ALU.add))
            dve.wait_ge(pre_pe, 1)
            dve.tensor_tensor(vec("gbout")[:, 0:C], vec("gbout")[:, 0:C], vec("gbout")[:, C:2 * C], ALU.add)\
                .then_inc(stat, 1)
            done(dve.tensor_copy(par_all[:, :, QRY:QRY + C].rearrange("p b c -> p c b"),
                                 A3[:, 0:C * B].rearrange("p (c b) -> p c b", c=C)))
            done(dve.tensor_copy(par_all[:, :, GATE:GATE + C].rearrange("p b c -> p c b"),
                                 vec("cond").rearrange("p (c b) -> p c b", c=C)))
            def modulations():
                dve.wait_ge(pre_pe, 8)
                mods = A1[:, 0:6 * C * B].rearrange("p (k b) -> p k b", b=B)
                emb = A1[:, 6 * C * B:8 * C * B].rearrange("p (k b) -> p k b", b=B)
                dve.tensor_tensor(par_all[:, :, MOD:AFF].rearrange("p b k -> p k b"), mods,
                                  vec("bc").unsqueeze(2).to_broadcast([P, 6 * C, B]), ALU.add).then_inc(stat, 1)
                dve.tensor_tensor(e1[:, :, :], emb, vec("embb").unsqueeze(2).to_broadcast([P, 2 * C, B]), ALU.add)\
                    .then_inc(stat, 1)
                dve.wait_ge(stat, 4)
                for k in (1, 4):
                    q = par_all[:, :, MOD + k * C:MOD + (k + 1) * C]
                    dve.tensor_scalar(q, q, 1.0, None, ALU.add).then_inc(stat, 1)
                dve.tensor_scalar(e1[:, 0:C, :], e1[:, 0:C, :], 1.0, 0.5, ALU.add, ALU.mult).then_inc(stat, 1)
                dve.tensor_scalar(e1[:, C:2 * C, :], e1[:, C:2 * C, :], 0.5, None, ALU.mult).then_inc(stat, 1)
                dve.wait_ge(stat, 8)
                for c in range(C):
                    done(dve.tensor_scalar(par_all[:, :, AFF + c], e1[:, c, :], vec("sng")[:, c:c + 1], None, ALU.mult))
                    done(dve.scalar_tensor_tensor(out=par_all[:, :, AFF + C + c], in0=e1[:, c, :],
                                                  scalar=vec("snb")[:, c:c + 1], in1=e1[:, C + c, :],
                                                  op0=ALU.mult, op1=ALU.add))

            for p in range(4):
                if p == 2:
                    modulations()
                dve.wait_ge(pre_pe, PART_DONE[p] + 1)
                lo = p * C * RANK
                done(dve.tensor_tensor(
                    par_all[:, :, lo:lo + 16].rearrange("p b (a j) -> p j a b", j=4),
                    A0.rearrange("p (j a b) -> p j a b", j=4, a=4)[:, :, :, 0:B],
                    vec("b2")[:, lo:lo + 16].rearrange("p (a j) -> p j a", j=4).unsqueeze(3).to_broadcast([P, 4, 4, B]),
                    ALU.add))
            dve.wait_ge(const_done, N_CONST)
            assert n == 17
            def low_1(it, s, o):
                dve.wait_ge(*pe_low.at(s, it, "bb"))
                dve.tensor_copy(o.bbT[0:RANK, :, :, :].rearrange("p f c n -> p (f c n)"), G[0:RANK, s, 1, :])\
                    .then_inc(*dve_low.inc(s, "bb"))
                dve.wait_ge(*pe_low.at(s, it, "y1"))
                dve.tensor_copy(o.y1[0:RANK, :], G[0:RANK, s, 0, 0:T]).then_inc(*dve_low.inc(s, "y1"))

            def low_3(it, s, o):
                dve.wait_ge(*pe_low.at(s, it, "z"))
                dve.tensor_copy(o.y1[0:RANK, :], G[0:RANK, s, 1, 0:T]).then_inc(*dve_low.inc(s, "z"))

            def low_4(it, s, o):
                dve.wait_ge(*pe_low.at(s, it, "x1"))
                dve.tensor_tensor(o.x1[:, :, :], G[:, s, 0, :].rearrange("p (c t) -> p c t", c=C), o.x[:, :, :],
                                  ALU.add).then_inc(*dve_low.inc(s, "x1"))

            def gat_adj(it, s, o):
                dve.wait_ge(ld_adj[s], it * 16 + 16)
                adj = o.adj.rearrange("p t (m l) -> p (t m) l", l=NL)
                adjw = o.adjw.rearrange("p t (m l) -> p (t m) l", l=NL)
                flat = [x[:, :, :].rearrange("p t m -> p (t m)") for x in (o.cond, o.mask, o.bias)]
                dve.tensor_reduce(flat[0], adj, AX, ALU.add).then_inc(*dve_gat.inc(s, "cond"))
                dve.tensor_tensor(adjw, adj, row("wl").unsqueeze(1).to_broadcast([P, TT * 2 * M, NL]), ALU.mult)\
                    .then_inc(*dve_gat.inc(s, "adjw"))
                dve.wait_ge(*dve_gat.at(s, it, "adjw"))
                dve.tensor_reduce(flat[2], adjw, AX, ALU.add).then_inc(*dve_gat.inc(s, "vb"))
                dve.tensor_scalar(flat[1], flat[0], 0.0, None, ALU.is_gt).then_inc(*dve_gat.inc(s, "mask"))
                dve.wait_ge(*dve_gat.at(s, it, "mask"))
                dve.tensor_scalar(flat[0], flat[1], -NEG, NEG, ALU.mult, ALU.add).then_inc(*dve_gat.inc(s, "neg"))
                dve.wait_ge(*dve_gat.at(s, it, "neg"))
                dve.scalar_tensor_tensor(out=flat[2], in0=flat[2], scalar=row("bb"), in1=flat[0],
                                         op0=ALU.add, op1=ALU.add).then_inc(*dve_gat.inc(s, "bias"))

            def gat_zero(it, s, o):
                dve.wait_ge(*pool_p.at(s, it, "par"))
                dve.wait_ge(*pe_gat.at(s, it, "sum"))
                for c in range(C):
                    last = dve.tensor_scalar(o.zq[:, c, :], G[:, s, 1, 0:T], 0.0,
                                             o.par[:, QRY - NLOW + c:QRY - NLOW + c + 1], ALU.not_equal, ALU.mult)
                last.then_inc(*dve_gat.inc(s, "zq"))

            def gat_query(it, s, o, d, q):
                dve.wait_ge(*pe_gat.at(s, it, f"q{d}"))
                for m in range(C):
                    k = d * C + m
                    last = dve.tensor_scalar(q[:, m, :], G[:, s, 1, m * T:(m + 1) * T], vec("gbq")[:, k:k + 1],
                                             float(DH) ** -0.5, ALU.add, ALU.mult)
                last.then_inc(*dve_gat.inc(s, f"q{d}"))

            def gat_self(it, s, o):
                dve.wait_ge(*pe_gat.at(s, it, "self"))
                dve.wait_ge(*dve_gat.at(s, it, "zq"))
                for c in range(C):
                    last = dve.scalar_tensor_tensor(out=o.sf[:, c, :], in0=G[:, s, 0, c * T:(c + 1) * T],
                                                    scalar=vec("bself")[:, c:c + 1], in1=o.zq[:, c, :],
                                                    op0=ALU.add, op1=ALU.add)
                last.then_inc(*dve_gat.inc(s, "sf"))
                dve.wait_ge(*dve_gat.at(s, it, "sf"))
                dve.tensor_copy(o.sfrep[:, :, :, 0:M], o.sf[:, :, 0:M].unsqueeze(2).to_broadcast([P, C, 4, M]))\
                    .then_inc(*dve_gat.inc(s, "sfrep"))

            def gat_keys(it, s, o):
                dve.wait_ge(*pe_gat.at(s, it, "k"))
                dve.tensor_tensor(o.kb[:, :, :], G[:, s, 0, 0:2 * C * M].rearrange("p (g m) -> p g m", m=M),
                                  vec("gbk").unsqueeze(2).to_broadcast([P, 2 * C, M]), ALU.add)\
                    .then_inc(*dve_gat.inc(s, "kb"))
                dve.wait_ge(*dve_gat.at(s, it, "kb"))
                dve.tensor_tensor(o.kbd, o.kb[:, :, :].unsqueeze(2).to_broadcast([P, 2 * C, HC, M]),
                                  blk16[:, :, 0].unsqueeze(1).unsqueeze(3).to_broadcast([P, 2 * C, HC, M]),
                                  ALU.mult).then_inc(*dve_gat.inc(s, "kbd"))

            def gat_vals(it, s, o):
                dve.wait_ge(*pe_gat.at(s, it, "v"))
                dve.tensor_tensor(o.vbd, G[0:4 * MP, s, 0, :].rearrange("p (g n) -> p g n", g=8),
                                  blk24[:, :, :].rearrange("p a l -> p (a l)").unsqueeze(1)
                                  .to_broadcast([4 * MP, 8, 4 * DH]), ALU.mult).then_inc(*dve_gat.inc(s, "vbd"))

            def gat_soft(it, s, o, t):
                dve.wait_ge(*pe_gat.at(s, it, f"s{t}"))
                S = o.S.rearrange("p (d h) m -> p d h m", d=2)

                def heads(x):
                    return x[:, t, :].rearrange("p (d m) -> p d m", d=2).unsqueeze(2).to_broadcast([P, 2, H, M])

                if t:
                    dve.wait_ge(*act_gat.at(s, it, "e0"))
                dve.tensor_tensor(S, G[:, s, :, 0:H * M].rearrange("p d (h m) -> p d h m", m=M), heads(o.mask),
                                  ALU.mult).then_inc(*dve_gat.inc(s, f"m{t}"))
                dve.wait_ge(*dve_gat.at(s, it, f"m{t}"))
                dve.tensor_tensor(S, S, heads(o.bias), ALU.add).then_inc(*dve_gat.inc(s, f"a{t}"))
                dve.wait_ge(*dve_gat.at(s, it, f"a{t}"))
                dve.tensor_reduce(o.mx[:, :], o.S, AX, ALU.max).then_inc(*dve_gat.inc(s, f"x{t}"))
                dve.wait_ge(*dve_gat.at(s, it, f"x{t}"))
                dve.tensor_tensor(o.S, o.S, o.mx[:, :].unsqueeze(2).to_broadcast([P, 2 * H, M]), ALU.subtract)\
                    .then_inc(*dve_gat.inc(s, f"d{t}"))

            def gat_sums(it, s, o, t):
                dve.wait_ge(*act_gat.at(s, it, f"e{t}"))
                if t:
                    dve.wait_ge(*dve_gat.at(s, it, "r0"))
                dve.tensor_reduce(o.sm[:, :], o.P[:, t, :, 0:M], AX, ALU.add).then_inc(*dve_gat.inc(s, f"s{t}"))
                dve.wait_ge(*dve_gat.at(s, it, f"s{t}"))
                if t:
                    dve.wait_ge(*pool_g.at(s, it, "p0"))
                dve.reciprocal(o.ri[:, :], o.sm[:, :]).then_inc(*dve_gat.inc(s, f"r{t}"))

            def gat_out(it, s, o):
                dve.wait_ge(stored[s], it * 16 + 16)
                dve.wait_ge(*pe_gat.at(s, it, "pv"))
                for c in range(C):
                    dve.scalar_tensor_tensor(out=o.xc[:, c, :], in0=G[:, s, 0, c * T:(c + 1) * T],
                                             scalar=vec("gbout")[:, c:c + 1], in1=o.sf[:, c, :],
                                             op0=ALU.add, op1=ALU.add).then_inc(*dve_gat.inc(s, f"o{c}"))
                dve.wait_ge(*dve_gat.at(s, it, "o1"))
                dve.scalar_tensor_tensor(out=o.x2[:, :, :], in0=o.xc[:, :, :], scalar=0.0, in1=o.x1[:, :, :],
                                         op0=ALU.max, op1=ALU.add).then_inc(*dve_gat.inc(s, "x2"))

            def centre(it, s, o, i, src):
                dve.wait_ge(*pe_ln[i].at(s, it, "mean"))
                dve.tensor_tensor(o.xc[:, :, :], src[:, :, :], G[:, s, 1, 0:T].unsqueeze(1).to_broadcast([P, C, T]),
                                  ALU.subtract).then_inc(*dve_ln[i].inc(s, "xc"))

            def scale(it, s, o, i, gain, shift):
                dve.wait_ge(*act_ln[i].at(s, it, "rstd"))
                dve.tensor_tensor(o.xc[:, :, :], o.xc[:, :, :], o.rstd[:, :].unsqueeze(1).to_broadcast([P, C, T]),
                                  ALU.mult).then_inc(*dve_ln[i].inc(s, "xn"))
                dve.wait_ge(*dve_ln[i].at(s, it, "xn"))
                for c in range(C):
                    last = dve.tensor_scalar(o.xm[:, c, :], o.xc[:, c, :], gain[:, c:c + 1], shift[:, c:c + 1],
                                             ALU.mult, ALU.add)
                last.then_inc(*dve_ln[i].inc(s, "xm"))

            def mod(o, k):
                return o.par[:, k * C:(k + 1) * C]

            def att_qk(it, s, o, k):
                name, b = (("q", "bq2"), ("k", "bk2"))[k]
                dve.wait_ge(*pe_att.at(s, it, name))
                for c in range(C):
                    last = dve.tensor_scalar(o.qk[:, k, c, :], G[:, s, k, c * T:(c + 1) * T],
                                             vec(b)[:, c:c + 1], 1.0 / DH if k == 0 else 1.0,
                                             ALU.add, ALU.mult)
                last.then_inc(*dve_att.inc(s, name))

            def att_v(it, s, o):
                dve.wait_ge(*pe_att.at(s, it, "v"))
                dve.tensor_tensor(o.vp[:, :, :, 0:DH], G[:, s, 0, :].rearrange("p (t h l) -> p t h l", t=TT, h=H),
                                  row("bv2").rearrange("p (h l) -> p h l", h=H).unsqueeze(1)
                                  .to_broadcast([P, TT, H, DH]), ALU.add).then_inc(*dve_att.inc(s, "vp"))

            def att_rest(it, s, o, k):
                name = "qk"[k]
                dve.wait_ge(*act_att.at(s, it, f"c1{name}"))
                dve.tensor_tensor(o.rest[:, k], o.qk[:, k], o.part[:, 0, k], ALU.subtract)\
                    .then_inc(*dve_att.inc(s, f"r{name}"))

            def att_part_3(it, s, o, k):
                name = "qk"[k]
                dve.wait_ge(*act_att.at(s, it, f"c2{name}"))
                dve.tensor_tensor(o.part[:, 2, k], o.rest[:, k], o.part[:, 1, k], ALU.subtract)\
                    .then_inc(*dve_att.inc(s, f"c{name}"))

            def att_max(it, s, o, u):
                dve.wait_ge(*pe_att.at(s, it, f"m{u}"))
                dve.tensor_reduce(o.mx2[:, :, 2 * u:2 * u + 2].rearrange("p t k -> p k t"),
                                  SS[:, u % 2, :].rearrange("p (k t n) -> p k t n", k=2, t=TT), AX, ALU.max)\
                    .then_inc(*dve_att.inc(s, f"m{u}"))

            def att_negmax(it, s, o, i):
                dve.wait_ge(*pe_att.at(s, it, f"x{i}"))
                mx = G[0:H // 2, s, 1, i * T:(i + 1) * T]
                dve.tensor_scalar(o.nmx[:, i, 0, :], mx, -1.0, None, ALU.mult).then_inc(*dve_att.inc(s, f"hi{i}"))
                dve.wait_ge(*dve_att.at(s, it, f"hi{i}"))
                dve.scalar_tensor_tensor(out=o.nmx[:, i, 1, :], in0=mx, scalar=-1.0, in1=o.nmx[:, i, 0, :],
                                         op0=ALU.mult, op1=ALU.subtract).then_inc(*dve_att.inc(s, f"lo{i}"))

            def att_norm(it, s, o):
                dve.wait_ge(*pe_att.at(s, it, "ot"))
                g = G[:, s, :, :].rearrange("p t (g n) -> p (t g) n", n=2 * DH)
                dve.reciprocal(o.ri[:, :], g[:, :, DH]).then_inc(*dve_att.inc(s, "ri"))
                dve.wait_ge(*dve_att.at(s, it, "ri"))
                dve.tensor_tensor(o.yq, g[:, :, 0:DH], o.ri[:, :].unsqueeze(2).to_broadcast([P, 2 * H, DH]),
                                  ALU.mult).then_inc(*dve_att.inc(s, "yq"))

            def gated(it, s, o, sems, pe_done, names, bank, bias, k, src, dst):
                dve.wait_ge(*pe_done)
                for c in range(C):
                    last = dve.tensor_scalar(o.xc[:, c, :], G[:, s, bank, c * T:(c + 1) * T], vec(bias)[:, c:c + 1],
                                             mod(o, k)[:, c:c + 1], ALU.add, ALU.mult)
                last.then_inc(*sems.inc(s, names[0]))
                dve.wait_ge(*sems.at(s, it, names[0]))
                dve.tensor_tensor(dst[:, :, :], o.xc[:, :, :], src[:, :, :], ALU.add).then_inc(*sems.inc(s, names[1]))

            def lin_q(it, s, o):
                groups = o.q3.rearrange("p t (h l) -> p (t h) l", l=DH)
                dve.wait_ge(*pe_lin.at(s, it, "q"))
                dve.tensor_tensor(o.q3, G[:, s, 0, :].rearrange("p (t n) -> p t n", t=TT),
                                  row("bq3").unsqueeze(1).to_broadcast([P, TT, D]), ALU.add)\
                    .then_inc(*dve_lin.inc(s, "q"))
                dve.wait_ge(*dve_lin.at(s, it, "q"))
                dve.tensor_reduce(o.mx[:, :], groups, AX, ALU.max).then_inc(*dve_lin.inc(s, "mx"))
                dve.wait_ge(*dve_lin.at(s, it, "mx"))
                dve.tensor_tensor(groups, groups, o.mx[:, :].unsqueeze(2).to_broadcast([P, 2 * H, DH]),
                                  ALU.subtract).then_inc(*dve_lin.inc(s, "d"))

            def lin_k(it, s, o):
                dve.wait_ge(*pe_lin.at(s, it, "k"))
                for c in range(C):
                    last = dve.tensor_scalar(o.kf[:, c, :], G[:, s, 1, c * T:(c + 1) * T], vec("bk3")[:, c:c + 1],
                                             None, ALU.add)
                last.then_inc(*dve_lin.inc(s, "k"))
                dve.wait_ge(*dve_lin.at(s, it, "k"))
                dve.tensor_reduce(o.nk[:, :], o.kf, AX, ALU.max, negate=True).then_inc(*dve_lin.inc(s, "nk"))

            def lin_v(it, s, o):
                dve.wait_ge(*pe_lin.at(s, it, "v"))
                dve.tensor_tensor(o.vt, G[:, s, 0, :].rearrange("p (t n) -> p t n", t=TT),
                                  row("bv3").unsqueeze(1).to_broadcast([P, TT, D]), ALU.add)\
                    .then_inc(*dve_lin.inc(s, "v"))

            def lin_soft(it, s, o):
                groups = o.q3.rearrange("p t (h l) -> p (t h) l", l=DH)
                dve.wait_ge(*act_lin.at(s, it, "eq"))
                dve.tensor_reduce(o.sm[:, :], groups, AX, ALU.add).then_inc(*dve_lin.inc(s, "sm"))
                dve.wait_ge(*dve_lin.at(s, it, "sm"))
                dve.reciprocal(o.ri[:, :], o.sm[:, :]).then_inc(*dve_lin.inc(s, "ri"))
                dve.wait_ge(*dve_lin.at(s, it, "ri"))
                dve.tensor_tensor(groups, groups, o.ri[:, :].unsqueeze(2).to_broadcast([P, 2 * H, DH]),
                                  ALU.mult).then_inc(*dve_lin.inc(s, "p"))
                dve.wait_ge(*act_lin.at(s, it, "ek"))
                dve.reciprocal(o.nk[:, :], o.ks[:, :]).then_inc(*dve_lin.inc(s, "rk"))

            def lin_ctx(it, s, o):
                dve.wait_ge(*pe_lin.at(s, it, "ctx"))
                dve.wait_ge(*dve_lin.at(s, it, "rk"))
                for c in range(C):
                    last = dve.scalar_tensor_tensor(out=o.ctx[:, c, :], in0=G[:, s, 1, c * P:(c + 1) * P],
                                                    scalar=o.nk[:, c:c + 1],
                                                    in1=blk16[:, :, :].rearrange("p h l -> p (h l)"),
                                                    op0=ALU.mult, op1=ALU.mult)
                last.then_inc(*dve_lin.inc(s, "ctx"))

            def lin_silu(it, s, o):
                dve.wait_ge(*act_lin.at(s, it, "tanh"))
                dve.scalar_tensor_tensor(out=o.sq[:, :, :], in0=o.sq[:, :, :], scalar=1.0, in1=o.xm[:, :, :],
                                         op0=ALU.add, op1=ALU.mult).then_inc(*dve_lin.inc(s, "s"))

            def lin_out(it, s, o):
                dve.wait_ge(*pe_lin.at(s, it, "o"))
                for c in range(C):
                    last = dve.tensor_scalar(o.xc[:, c, :], G[:, s, 1, c * T:(c + 1) * T], vec("ob3")[:, c:c + 1],
                                             o.par[:, GATE - NLOW + c:GATE - NLOW + c + 1], ALU.add, ALU.mult)
                last.then_inc(*dve_lin.inc(s, "t"))
                dve.wait_ge(*dve_lin.at(s, it, "t"))
                dve.tensor_tensor(o.xc[:, :, :], o.xc[:, :, :], o.x2[:, :, :], ALU.add)\
                    .then_inc(*dve_lin.inc(s, "out"))

            def att_gate(it, s, o):
                gated(it, s, o, dve_att, pe_att.at(s, it, "o"), ("t", "x3"), 1, "bo2", 2, o.x2, o.x1)

            def mlp_gate(it, s, o):
                gated(it, s, o, dve_mlp, pe_mlp.at(s, it, "w2"), ("t", "x4"), 0, "mb2", 5, o.x1, o.x2)

            def norm_0(it, s, o):
                dve.wait_ge(*pool_p.at(s, it, "par"))
                scale(it, s, o, 0, mod(o, 1), mod(o, 0))

            run(dve, ORDER["DVE"], {
                "low1": low_1, "adj": gat_adj, "low3": low_3, "low4": low_4, "sum": gat_zero, "self": gat_self,
                "gq0": lambda it, s, o: gat_query(it, s, o, 0, o.gq), "gk": gat_keys,
                "gq1": lambda it, s, o: gat_query(it, s, o, 1, o.gq1), "gv": gat_vals,
                **each("s", gat_soft, TT), **each("r", gat_sums, TT), "pv": gat_out,
                "n0a": lambda it, s, o: centre(it, s, o, 0, o.x2), "n0b": norm_0,
                "q": lambda it, s, o: att_qk(it, s, o, 0), "k": lambda it, s, o: att_qk(it, s, o, 1),
                "v": att_v, "rq": lambda it, s, o: att_rest(it, s, o, 0), "rk": lambda it, s, o: att_rest(it, s, o, 1),
                "cq": lambda it, s, o: att_part_3(it, s, o, 0), "ck": lambda it, s, o: att_part_3(it, s, o, 1),
                **each("m", att_max, 8), **each("x", att_negmax, 2),
                "ot": att_norm, "wo": att_gate,
                "n1a": lambda it, s, o: centre(it, s, o, 1, o.x1),
                "n1b": lambda it, s, o: scale(it, s, o, 1, mod(o, 4), mod(o, 3)),
                "w2b": mlp_gate,
                "n2a": lambda it, s, o: centre(it, s, o, 2, o.x2),
                "n2b": lambda it, s, o: scale(it, s, o, 2, vec("n3g"), vec("n3b")),
                "lq": lin_q, "lk": lin_k, "lv": lin_v, "ls": lin_soft, "lc": lin_ctx,
                "n3a": lambda it, s, o: centre(it, s, o, 3, o.yF),
                "n3b": lambda it, s, o: scale(it, s, o, 3, o.par[:, AFF - NLOW:AFF - NLOW + C],
                                              o.par[:, AFF - NLOW + C:AFF - NLOW + 2 * C]),
                "tanh": lin_silu, "lo": lin_out})


def kernel(**inputs):
    import numpy as np
    import concourse.bacc as bacc
    from concourse.bass_utils import run_bass_kernel_spmd

    x = {k: np.asarray(v) for k, v in inputs.items()}

    def rows(a):
        a = np.asarray(a)
        return a.reshape(-1, P, a.shape[1]).transpose(1, 0, 2).reshape(P, -1)

    def cols(v):
        return np.asarray(v).reshape(-1, P).T

    def by_channel(a):
        a = np.asarray(a)
        return a.reshape(*a.shape[:-1], H, DH).swapaxes(-1, -2).reshape(a.shape)

    L1, L2, L3 = "L1_cond_", "L2_cond_", "L3_cond_"
    w_self = x[L1 + "W_self"].T
    packs = {
        "self": rows(w_self[:D]),
        "gq": np.concatenate([rows(m.T) for m in x[L1 + "Wq"]], axis=1),
        "gk": np.concatenate([rows(m.T) for m in x[L1 + "Wk"]], axis=1),
        "gv": rows(x[L1 + "Wout"].transpose(3, 0, 1, 2).reshape(D, 2 * D)),
        "q2": rows(by_channel(x[L2 + "Wq"])), "k2": rows(by_channel(x[L2 + "Wk"])), "v2": rows(x[L2 + "Wv"]), "o2": rows(x[L2 + "Wo"]),
        "w1": rows(x[L2 + "W1"]), "w2": rows(x[L2 + "W2"]),
        "q3": rows(x[L3 + "Wq"]), "k3": rows(x[L3 + "Wk"]), "v3": rows(x[L3 + "Wv"]), "o3": rows(x[L3 + "out_W"]),
    }
    w_pack = np.concatenate([packs[k] for k in W_COLS], axis=1)
    vecs = {
        "ln_g": cols(x["L0_cond_ln_g"]), "ln_b": cols(x["L0_cond_ln_b"]), "b1": cols(x["L0_cond_b1"]),
        "b2": x["L0_cond_b2"].reshape(4, C, P, RANK).transpose(2, 0, 1, 3).reshape(P, 64),
        "bself": cols(x[L1 + "b_self"]), "gbq": cols(x[L1 + "bq"].reshape(-1)), "gbk": cols(x[L1 + "bk"].reshape(-1)),
        "gbout": cols(x[L1 + "bout"].reshape(-1)), "bc": cols(x[L2 + "bc"]), "bq2": cols(by_channel(x[L2 + "bq"])),
        "bk2": cols(by_channel(x[L2 + "bk"])), "bo2": cols(x[L2 + "bo"]), "mb1": cols(x[L2 + "b1"]), "mb2": cols(x[L2 + "b2"]),
        "n3g": cols(x[L3 + "norm_g"]), "n3b": cols(x[L3 + "norm_b"]), "bk3": cols(x[L3 + "bk"]),
        "embb": cols(x[L3 + "emb_b"]), "sng": cols(x[L3 + "sn_g"]), "snb": cols(x[L3 + "sn_b"]),
        "ob3": cols(x[L3 + "out_b"]),
        "cond": x["cond_1024"].T.reshape(C, P, B).transpose(1, 0, 2).reshape(P, C * B),
    }
    v_pack = np.concatenate([vecs[k] for k in V_COLS], axis=1)
    r_pack = np.concatenate([x[L2 + "bv"], x[L3 + "bq"], x[L3 + "bv"], x[L1 + "w_bias"],
                             x[L1 + "b_bias"].reshape(1)])[None, :]
    s_pack = np.concatenate([rows(w_self[D:]), rows(x["L0_cond_W1"]), rows(x[L2 + "Wc"]), rows(x[L3 + "emb_W"])], axis=1)
    low = x["L0_cond_W2"].reshape(C, P, 4, C, P, RANK).transpose(2, 1, 0, 3, 5, 4).reshape(4, P, C, 2048)
    adj = x["mask_BxSxSx11_ik0"]
    adj = np.stack([adj[:, :, :M], adj[:, :M].transpose(0, 2, 1, 3)], axis=2).reshape(B, T, 2 * M * NL)
    x_f = x["x"].transpose(0, 2, 1).reshape(B, C, P, T).transpose(0, 2, 1, 3)

    nc = bacc.Bacc("TRN2", target_bir_lowering=False, num_devices=1)
    arrays, args = {}, []
    for name, a in (("x", x_f), ("cond", x["cond_1024"]), ("adj", adj), ("w", w_pack), ("v", v_pack), ("r", r_pack),
                    ("s", s_pack), ("low", low)):
        arrays[f"in_{name}"] = np.ascontiguousarray(a)
        args.append(nc.dram_tensor(f"in_{name}", list(a.shape), mybir.dt.from_np(a.dtype), kind="ExternalInput").ap())
    args.append(nc.dram_tensor("out_x", [B, P, C, T], F32, kind="ExternalOutput").ap())
    nc.disable_value_cache = True
    build(nc, *args)
    r = run_bass_kernel_spmd(nc, [arrays], core_ids=[0])
    y = r.results[0]["out_x"]
    return y.transpose(0, 3, 2, 1).reshape(B, T, D)
```
